# Optimizing a Trainium2 kernel written in Bass

```python
import numpy as np
import jax
import jax.numpy as jnp

def _softmax(x, axis=-1):
    return jax.nn.softmax(x, axis=axis)

def _gelu(x):
    return jax.nn.gelu(x, approximate=True)

def _silu(x):
    return jax.nn.silu(x)

def _sigmoid(x):
    return jax.nn.sigmoid(x)

def _layernorm(x, axis=-1, eps=1e-05):
    m = jnp.mean(x, axis=axis, keepdims=True)
    v = jnp.var(x, axis=axis, keepdims=True)
    return (x - m) / jnp.sqrt(v + eps)

def _scatter_add(tgt, idx, src, axis=0):
    return tgt.at[idx].add(src)

def _segment_sum(src, seg, n):
    return jax.ops.segment_sum(src, seg, n)
kernel_name = 'mk_gnn_ffn_d4_gnn_r32_5932e2'

def setup_inputs(seed: int=0):
    np.random.seed(seed)
    _w = jnp.asarray

    def _rec_inputs():
        import jax
        import jax.numpy as jnp
        _gk = jax.random.key(seed)
        x = -8.776e-05 + 1 * jax.random.normal(jax.random.fold_in(_gk, 1), (625, 256), jnp.float32)
        _s = jax.random.randint(jax.random.fold_in(_gk, 2), (5000,), 0, 625, jnp.int32)
        _d = jax.random.randint(jax.random.fold_in(_gk, 3), (5000,), 0, 625, jnp.int32)
        _loop = jnp.arange(625, dtype=jnp.int32)
        src = jnp.concatenate([_s, _d, _loop])
        dst = jnp.concatenate([_d, _s, _loop])
        _o = jnp.argsort(dst, stable=True)
        src = src[_o]
        dst = dst[_o]
        return (x, src, dst)
    x, src, dst = _rec_inputs()

    def _L0_gnn_setup():
        import jax, jax.numpy as jnp
        import numpy as np
        N_NODES = 625

        def gcn_conv(x, W, b, src, dst, num_nodes):
            loops = jnp.arange(num_nodes, dtype=src.dtype)
            s = jnp.concatenate([src, loops])
            d = jnp.concatenate([dst, loops])
            deg = jax.ops.segment_sum(jnp.ones_like(d, dtype=x.dtype), d, num_segments=num_nodes)
            inv_sqrt = jax.lax.rsqrt(jnp.maximum(deg, 1.0))
            norm = inv_sqrt[s] * inv_sqrt[d]
            h = x @ W
            msg = h[s] * norm[:, None]
            out = jax.ops.segment_sum(msg, d, num_segments=num_nodes)
            return out + b
        key = jax.random.key(seed)
        k1, k2, k3, k4 = jax.random.split(key, 4)
        in_dim, hid, out_dim = (256, 512, 256)
        x = jax.random.normal(k1, (N_NODES, in_dim), dtype=jnp.float32)
        edge_index = jax.random.randint(k2, (2, 10000), 0, N_NODES, dtype=jnp.int64)
        W1 = jax.random.normal(k3, (in_dim, hid), dtype=jnp.float32) * (1.0 / np.sqrt(in_dim))
        b1 = jnp.zeros((hid,), dtype=jnp.float32)
        W2 = jax.random.normal(k4, (hid, out_dim), dtype=jnp.float32) * (1.0 / np.sqrt(hid))
        b2 = jnp.zeros((out_dim,), dtype=jnp.float32)
        return {'x': x, 'edge_index': edge_index, 'W1': W1, 'b1': b1, 'W2': W2, 'b2': b2}
    _L0_gnn_all = _L0_gnn_setup()
    _L0_gnn_in = {k: v for k, v in _L0_gnn_all.items() if k in ('W1', 'b1', 'W2', 'b2')}
    del _L0_gnn_all

    def _L0_ffn_setup():
        import jax, jax.numpy as jnp
        import numpy as np
        B, N, D = (16, 128, 256)
        NUM_EXPERTS, TOP_K, HEADS = (4, 2, 4)
        N_EDGES = 32768
        LN_EPS = 1e-05

        def _layernorm(x, g, b):
            mu = x.mean(-1, keepdims=True)
            var = ((x - mu) ** 2).mean(-1, keepdims=True)
            return (x - mu) * jax.lax.rsqrt(var + LN_EPS) * g + b

        def _forward(x, edge_index, W_gat, att_src, att_dst, b_gat, ln_gamma, ln_beta, W1, b1, W2, b2):
            Bc, Nc, Dc = x.shape
            M = Bc * Nc
            x_flat = x.reshape(M, Dc)
            h = (x_flat @ W_gat).reshape(M, HEADS, NUM_EXPERTS)
            loops = jnp.arange(M, dtype=edge_index.dtype)
            src = jnp.concatenate([edge_index[0], loops])
            dst = jnp.concatenate([edge_index[1], loops])
            a_src = (h * att_src).sum(-1)
            a_dst = (h * att_dst).sum(-1)
            e = jax.nn.leaky_relu(a_src[src] + a_dst[dst], negative_slope=0.2)
            e_max = jax.ops.segment_max(e, dst, num_segments=M)
            ee = jnp.exp(e - e_max[dst])
            denom = jax.ops.segment_sum(ee, dst, num_segments=M)
            alpha = ee / (denom[dst] + 1e-16)
            msg = h[src] * alpha[:, :, None]
            agg = jax.ops.segment_sum(msg, dst, num_segments=M).reshape(M, HEADS * NUM_EXPERTS) + b_gat
            scores = _layernorm(agg, ln_gamma, ln_beta).reshape(M, HEADS, NUM_EXPERTS).mean(1)
            scores = scores.reshape(Bc, Nc, NUM_EXPERTS)
            topk_s, topk_i = jax.lax.top_k(scores, TOP_K)
            w = jax.nn.softmax(topk_s, axis=-1)
            out = jnp.zeros_like(x)
            for ei in range(NUM_EXPERTS):
                g = jnp.where(topk_i == ei, w, 0.0).sum(-1)
                hh = jax.nn.gelu(x @ W1[ei] + b1[ei], approximate=False)
                out = out + g[..., None] * (hh @ W2[ei] + b2[ei])
            return out
        key = jax.random.key(seed)
        ks = jax.random.split(key, 8)
        s = 0.05
        return {'x': jax.random.normal(ks[0], (B, N, D), jnp.float32), 'W_gat': jax.random.normal(ks[1], (D, HEADS * NUM_EXPERTS), jnp.float32) * s, 'att_src': jax.random.normal(ks[2], (HEADS, NUM_EXPERTS), jnp.float32) * s, 'att_dst': jax.random.normal(ks[3], (HEADS, NUM_EXPERTS), jnp.float32) * s, 'b_gat': jnp.zeros((HEADS * NUM_EXPERTS,), jnp.float32), 'ln_gamma': jnp.ones((HEADS * NUM_EXPERTS,), jnp.float32), 'ln_beta': jnp.zeros((HEADS * NUM_EXPERTS,), jnp.float32), 'W1': jax.random.normal(ks[4], (NUM_EXPERTS, D, 2 * D), jnp.float32) * s, 'b1': jnp.zeros((NUM_EXPERTS, 2 * D), jnp.float32), 'W2': jax.random.normal(ks[5], (NUM_EXPERTS, 2 * D, D), jnp.float32) * s, 'b2': jnp.zeros((NUM_EXPERTS, D), jnp.float32), 'edge_index': jax.random.randint(ks[6], (2, N_EDGES), 0, B * N, jnp.int32)}
    _L0_ffn_all = _L0_ffn_setup()
    _L0_ffn_in = {k: v for k, v in _L0_ffn_all.items() if k in ('W_gat', 'att_src', 'att_dst', 'b_gat', 'ln_gamma', 'ln_beta', 'W1', 'b1', 'W2', 'b2', 'edge_index')}
    del _L0_ffn_all

    def _L1_gnn_setup():
        import jax, jax.numpy as jnp
        import numpy as np
        N, E = (50000, 25000)
        IN_C, HID_C, OUT_C = (256, 256, 256)

        def _gcn_prep(edge_index, n_nodes):
            src = jnp.concatenate([edge_index[0], jnp.arange(n_nodes, dtype=edge_index.dtype)])
            dst = jnp.concatenate([edge_index[1], jnp.arange(n_nodes, dtype=edge_index.dtype)])
            deg = jax.ops.segment_sum(jnp.ones_like(dst, dtype=jnp.float32), dst, num_segments=n_nodes)
            deg_inv_sqrt = jnp.where(deg > 0, jax.lax.rsqrt(jnp.maximum(deg, 1.0)), 0.0)
            norm = deg_inv_sqrt[src] * deg_inv_sqrt[dst]
            return (src, dst, norm)

        def _gcn_layer(x, src, dst, norm, W, b, n_nodes):
            h = x @ W
            msg = h[src] * norm[:, None]
            out = jax.ops.segment_sum(msg, dst, num_segments=n_nodes)
            return out + b
        key = jax.random.key(seed)
        ks = jax.random.split(key, 8)
        x_piece = jax.random.normal(ks[0], (N, IN_C), dtype=jnp.float32)
        edge_index_piece = jax.random.randint(ks[1], (2, E), 0, N, dtype=jnp.int64)
        batch = jnp.zeros((N,), dtype=jnp.int64)

        def glorot(k, fan_in, fan_out):
            s = jnp.sqrt(6.0 / (fan_in + fan_out)).astype(jnp.float32)
            return jax.random.uniform(k, (fan_in, fan_out), jnp.float32, -s, s)
        return {'x_piece': x_piece, 'edge_index_piece': edge_index_piece, 'batch': batch, 'W1': glorot(ks[2], IN_C, HID_C), 'b1': jnp.zeros((HID_C,), jnp.float32), 'W2': glorot(ks[3], HID_C, HID_C), 'b2': jnp.zeros((HID_C,), jnp.float32), 'W3': glorot(ks[4], HID_C, OUT_C), 'b3': jnp.zeros((OUT_C,), jnp.float32)}
    _L1_gnn_all = _L1_gnn_setup()
    _L1_gnn_in = {k: v for k, v in _L1_gnn_all.items() if k in ('W1', 'b1', 'W2', 'b2', 'W3', 'b3')}
    del _L1_gnn_all

    def _L1_ffn_setup():
        import jax, jax.numpy as jnp
        import numpy as np
        B, S, D = (8, 128, 256)
        H = 4 * D
        CAPACITY = 0.5
        key = jax.random.key(seed)
        ks = jax.random.split(key, 6)
        x = jax.random.normal(ks[0], (B, S, D), dtype=jnp.float32)
        attention_mask = jnp.zeros((B, 1, 1, S), dtype=jnp.float32)
        wr = jax.random.normal(ks[1], (D, 1), dtype=jnp.float32) * 0.02
        br = jnp.zeros((1,), dtype=jnp.float32)
        w1 = jax.random.normal(ks[2], (D, H), dtype=jnp.float32) * 0.02
        b1 = jnp.zeros((H,), dtype=jnp.float32)
        w2 = jax.random.normal(ks[3], (H, D), dtype=jnp.float32) * 0.02
        b2 = jnp.zeros((D,), dtype=jnp.float32)
        return {'x': x, 'attention_mask': attention_mask, 'wr': wr, 'br': br, 'w1': w1, 'b1': b1, 'w2': w2, 'b2': b2}
    _L1_ffn_all = _L1_ffn_setup()
    _L1_ffn_in = {k: v for k, v in _L1_ffn_all.items() if k in ('attention_mask', 'wr', 'br', 'w1', 'b1', 'w2', 'b2')}
    del _L1_ffn_all

    def _L2_gnn_setup():
        import jax, jax.numpy as jnp
        import numpy as np
        N = 3125
        E = 50000
        IN_FEATS = 256
        OUT_FEATS = 256
        MAXK = 32

        def _maxk(x, k):
            _, idx = jax.lax.top_k(x, k)
            rows = jnp.arange(x.shape[0])[:, None]
            mask = jnp.zeros_like(x).at[rows, idx].set(1.0)
            return x * mask
        key = jax.random.key(seed)
        k1, k2, k3, k4, k5 = jax.random.split(key, 5)
        feat = jax.random.normal(k1, (N, IN_FEATS), dtype=jnp.float32)
        W_self = jax.random.normal(k2, (IN_FEATS, OUT_FEATS), dtype=jnp.float32) * (1.0 / np.sqrt(IN_FEATS))
        W_neigh = jax.random.normal(k3, (IN_FEATS, OUT_FEATS), dtype=jnp.float32) * (1.0 / np.sqrt(IN_FEATS))
        src = jax.random.randint(k4, (E,), 0, N, dtype=jnp.int64)
        dst = jax.random.randint(k5, (E,), 0, N, dtype=jnp.int64)
        return {'feat': feat, 'W_self': W_self, 'W_neigh': W_neigh, 'src': src, 'dst': dst}
    _L2_gnn_all = _L2_gnn_setup()
    _L2_gnn_in = {k: v for k, v in _L2_gnn_all.items() if k in ('W_self', 'W_neigh')}
    del _L2_gnn_all

    def _L2_ffn_setup():
        import math
        import jax, jax.numpy as jnp
        import numpy as np
        CAPACITY_FACTOR = 1.25
        key = jax.random.key(seed)
        ks = jax.random.split(key, 5)
        B, L, D, F, E = (8, 256, 256, 1024, 8)
        h = jax.random.normal(ks[0], (B, L, D), dtype=jnp.float32)
        gate_w = jax.random.normal(ks[1], (D, E), dtype=jnp.float32) * 0.02
        gate_b = jnp.zeros((E,), dtype=jnp.float32)
        w1 = jax.random.normal(ks[2], (E, D, F), dtype=jnp.float32) * (1.0 / math.sqrt(D))
        b1 = jnp.zeros((E, F), dtype=jnp.float32)
        w2 = jax.random.normal(ks[3], (E, F, D), dtype=jnp.float32) * (1.0 / math.sqrt(F))
        b2 = jnp.zeros((E, D), dtype=jnp.float32)
        return {'h': h, 'gate_w': gate_w, 'gate_b': gate_b, 'w1': w1, 'b1': b1, 'w2': w2, 'b2': b2}
    _L2_ffn_all = _L2_ffn_setup()
    _L2_ffn_in = {k: v for k, v in _L2_ffn_all.items() if k in ('gate_w', 'gate_b', 'w1', 'b1', 'w2', 'b2')}
    del _L2_ffn_all

    def _L3_gnn_setup():
        import jax, jax.numpy as jnp
        import numpy as np
        N, IN_CH, HEADS, OUT_CH, E = (50000, 256, 4, 64, 25000)
        key = jax.random.key(seed)
        k1, k2, k3, k4, k5 = jax.random.split(key, 5)
        x = jax.random.normal(k1, (N, IN_CH), dtype=jnp.float32)
        edge_index = jax.random.randint(k2, (2, E), 0, N, dtype=jnp.int64)
        bw = float(np.sqrt(6.0 / (IN_CH + HEADS * OUT_CH)))
        ba = float(np.sqrt(6.0 / (HEADS + OUT_CH)))
        weight = jax.random.uniform(k3, (IN_CH, HEADS * OUT_CH), jnp.float32, -bw, bw)
        attn_l = jax.random.uniform(k4, (HEADS, OUT_CH), jnp.float32, -ba, ba)
        attn_r = jax.random.uniform(k5, (HEADS, OUT_CH), jnp.float32, -ba, ba)
        return {'x': x, 'edge_index': edge_index, 'weight': weight, 'attn_l': attn_l, 'attn_r': attn_r}
    _L3_gnn_all = _L3_gnn_setup()
    _L3_gnn_in = {k: v for k, v in _L3_gnn_all.items() if k in ('weight', 'attn_l', 'attn_r')}
    del _L3_gnn_all

    def _L3_ffn_setup():
        import jax, jax.numpy as jnp
        import numpy as np
        B, S, H, F, E, K = (8, 128, 256, 512, 16, 2)
        EPS = 1e-05
        key = jax.random.key(seed)
        ks = jax.random.split(key, 9)
        sc = 0.02
        return {'x': jax.random.normal(ks[0], (B, S, H), dtype=jnp.float32), 'gate_w': jax.random.normal(ks[1], (H, E), dtype=jnp.float32) * sc, 'gate_b': jnp.zeros((E,), dtype=jnp.float32), 'w1': jax.random.normal(ks[2], (E, H, F), dtype=jnp.float32) * sc, 'b1': jnp.zeros((E, F), dtype=jnp.float32), 'w2': jax.random.normal(ks[3], (E, F, H), dtype=jnp.float32) * sc, 'b2': jnp.zeros((E, H), dtype=jnp.float32), 'gamma': jnp.ones((H,), dtype=jnp.float32), 'beta': jnp.zeros((H,), dtype=jnp.float32)}
    _L3_ffn_all = _L3_ffn_setup()
    _L3_ffn_in = {k: v for k, v in _L3_ffn_all.items() if k in ('gate_w', 'gate_b', 'w1', 'b1', 'w2', 'b2', 'gamma', 'beta')}
    del _L3_ffn_all
    return {'x': x, 'src': src, 'dst': dst, 'L0_gnn_W1': _L0_gnn_in['W1'], 'L0_gnn_b1': _L0_gnn_in['b1'], 'L0_gnn_W2': _L0_gnn_in['W2'], 'L0_gnn_b2': _L0_gnn_in['b2'], 'L0_ffn_W_gat': _L0_ffn_in['W_gat'], 'L0_ffn_att_src': _L0_ffn_in['att_src'], 'L0_ffn_att_dst': _L0_ffn_in['att_dst'], 'L0_ffn_b_gat': _L0_ffn_in['b_gat'], 'L0_ffn_ln_gamma': _L0_ffn_in['ln_gamma'], 'L0_ffn_ln_beta': _L0_ffn_in['ln_beta'], 'L0_ffn_W1': _L0_ffn_in['W1'], 'L0_ffn_b1': _L0_ffn_in['b1'], 'L0_ffn_W2': _L0_ffn_in['W2'], 'L0_ffn_b2': _L0_ffn_in['b2'], 'L0_ffn_edge_index': _L0_ffn_in['edge_index'], 'L1_gnn_W1': _L1_gnn_in['W1'], 'L1_gnn_b1': _L1_gnn_in['b1'], 'L1_gnn_W2': _L1_gnn_in['W2'], 'L1_gnn_b2': _L1_gnn_in['b2'], 'L1_gnn_W3': _L1_gnn_in['W3'], 'L1_gnn_b3': _L1_gnn_in['b3'], 'L1_ffn_attention_mask': _L1_ffn_in['attention_mask'], 'L1_ffn_wr': _L1_ffn_in['wr'], 'L1_ffn_br': _L1_ffn_in['br'], 'L1_ffn_w1': _L1_ffn_in['w1'], 'L1_ffn_b1': _L1_ffn_in['b1'], 'L1_ffn_w2': _L1_ffn_in['w2'], 'L1_ffn_b2': _L1_ffn_in['b2'], 'L2_gnn_W_self': _L2_gnn_in['W_self'], 'L2_gnn_W_neigh': _L2_gnn_in['W_neigh'], 'L2_ffn_gate_w': _L2_ffn_in['gate_w'], 'L2_ffn_gate_b': _L2_ffn_in['gate_b'], 'L2_ffn_w1': _L2_ffn_in['w1'], 'L2_ffn_b1': _L2_ffn_in['b1'], 'L2_ffn_w2': _L2_ffn_in['w2'], 'L2_ffn_b2': _L2_ffn_in['b2'], 'L3_gnn_weight': _L3_gnn_in['weight'], 'L3_gnn_attn_l': _L3_gnn_in['attn_l'], 'L3_gnn_attn_r': _L3_gnn_in['attn_r'], 'L3_ffn_gate_w': _L3_ffn_in['gate_w'], 'L3_ffn_gate_b': _L3_ffn_in['gate_b'], 'L3_ffn_w1': _L3_ffn_in['w1'], 'L3_ffn_b1': _L3_ffn_in['b1'], 'L3_ffn_w2': _L3_ffn_in['w2'], 'L3_ffn_b2': _L3_ffn_in['b2'], 'L3_ffn_gamma': _L3_ffn_in['gamma'], 'L3_ffn_beta': _L3_ffn_in['beta']}

def reference(x, src, dst, L0_gnn_W1, L0_gnn_b1, L0_gnn_W2, L0_gnn_b2, L0_ffn_W_gat, L0_ffn_att_src, L0_ffn_att_dst, L0_ffn_b_gat, L0_ffn_ln_gamma, L0_ffn_ln_beta, L0_ffn_W1, L0_ffn_b1, L0_ffn_W2, L0_ffn_b2, L0_ffn_edge_index, L1_gnn_W1, L1_gnn_b1, L1_gnn_W2, L1_gnn_b2, L1_gnn_W3, L1_gnn_b3, L1_ffn_attention_mask, L1_ffn_wr, L1_ffn_br, L1_ffn_w1, L1_ffn_b1, L1_ffn_w2, L1_ffn_b2, L2_gnn_W_self, L2_gnn_W_neigh, L2_ffn_gate_w, L2_ffn_gate_b, L2_ffn_w1, L2_ffn_b1, L2_ffn_w2, L2_ffn_b2, L3_gnn_weight, L3_gnn_attn_l, L3_gnn_attn_r, L3_ffn_gate_w, L3_ffn_gate_b, L3_ffn_w1, L3_ffn_b1, L3_ffn_w2, L3_ffn_b2, L3_ffn_gamma, L3_ffn_beta):
    import jax
    import jax.numpy as jnp

    def _L0_gnn_ref(x, edge_index, W1, b1, W2, b2):
        import jax, jax.numpy as jnp
        import numpy as np
        N_NODES = 625

        def gcn_conv(x, W, b, src, dst, num_nodes):
            loops = jnp.arange(num_nodes, dtype=src.dtype)
            s = jnp.concatenate([src, loops])
            d = jnp.concatenate([dst, loops])
            deg = jax.ops.segment_sum(jnp.ones_like(d, dtype=x.dtype), d, num_segments=num_nodes)
            inv_sqrt = jax.lax.rsqrt(jnp.maximum(deg, 1.0))
            norm = inv_sqrt[s] * inv_sqrt[d]
            h = x @ W
            msg = h[s] * norm[:, None]
            out = jax.ops.segment_sum(msg, d, num_segments=num_nodes)
            return out + b
        src, dst = (edge_index[0], edge_index[1])
        h = gcn_conv(x, W1, b1, src, dst, N_NODES)
        h = jax.nn.relu(h)
        out = gcn_conv(h, W2, b2, src, dst, N_NODES)
        return out

    def _L0_ffn_ref(x, W_gat, att_src, att_dst, b_gat, ln_gamma, ln_beta, W1, b1, W2, b2, edge_index):
        import jax, jax.numpy as jnp
        import numpy as np
        B, N, D = (16, 128, 256)
        NUM_EXPERTS, TOP_K, HEADS = (4, 2, 4)
        N_EDGES = 32768
        LN_EPS = 1e-05

        def _layernorm(x, g, b):
            mu = x.mean(-1, keepdims=True)
            var = ((x - mu) ** 2).mean(-1, keepdims=True)
            return (x - mu) * jax.lax.rsqrt(var + LN_EPS) * g + b

        def _forward(x, edge_index, W_gat, att_src, att_dst, b_gat, ln_gamma, ln_beta, W1, b1, W2, b2):
            Bc, Nc, Dc = x.shape
            M = Bc * Nc
            x_flat = x.reshape(M, Dc)
            h = (x_flat @ W_gat).reshape(M, HEADS, NUM_EXPERTS)
            loops = jnp.arange(M, dtype=edge_index.dtype)
            src = jnp.concatenate([edge_index[0], loops])
            dst = jnp.concatenate([edge_index[1], loops])
            a_src = (h * att_src).sum(-1)
            a_dst = (h * att_dst).sum(-1)
            e = jax.nn.leaky_relu(a_src[src] + a_dst[dst], negative_slope=0.2)
            e_max = jax.ops.segment_max(e, dst, num_segments=M)
            ee = jnp.exp(e - e_max[dst])
            denom = jax.ops.segment_sum(ee, dst, num_segments=M)
            alpha = ee / (denom[dst] + 1e-16)
            msg = h[src] * alpha[:, :, None]
            agg = jax.ops.segment_sum(msg, dst, num_segments=M).reshape(M, HEADS * NUM_EXPERTS) + b_gat
            scores = _layernorm(agg, ln_gamma, ln_beta).reshape(M, HEADS, NUM_EXPERTS).mean(1)
            scores = scores.reshape(Bc, Nc, NUM_EXPERTS)
            topk_s, topk_i = jax.lax.top_k(scores, TOP_K)
            w = jax.nn.softmax(topk_s, axis=-1)
            out = jnp.zeros_like(x)
            for ei in range(NUM_EXPERTS):
                g = jnp.where(topk_i == ei, w, 0.0).sum(-1)
                hh = jax.nn.gelu(x @ W1[ei] + b1[ei], approximate=False)
                out = out + g[..., None] * (hh @ W2[ei] + b2[ei])
            return out
        return _forward(x, edge_index, W_gat, att_src, att_dst, b_gat, ln_gamma, ln_beta, W1, b1, W2, b2)

    def _L1_gnn_ref(x_piece, edge_index_piece, batch, W1, b1, W2, b2, W3, b3):
        import jax, jax.numpy as jnp
        import numpy as np
        N, E = (50000, 25000)
        IN_C, HID_C, OUT_C = (256, 256, 256)

        def _gcn_prep(edge_index, n_nodes):
            src = jnp.concatenate([edge_index[0], jnp.arange(n_nodes, dtype=edge_index.dtype)])
            dst = jnp.concatenate([edge_index[1], jnp.arange(n_nodes, dtype=edge_index.dtype)])
            deg = jax.ops.segment_sum(jnp.ones_like(dst, dtype=jnp.float32), dst, num_segments=n_nodes)
            deg_inv_sqrt = jnp.where(deg > 0, jax.lax.rsqrt(jnp.maximum(deg, 1.0)), 0.0)
            norm = deg_inv_sqrt[src] * deg_inv_sqrt[dst]
            return (src, dst, norm)

        def _gcn_layer(x, src, dst, norm, W, b, n_nodes):
            h = x @ W
            msg = h[src] * norm[:, None]
            out = jax.ops.segment_sum(msg, dst, num_segments=n_nodes)
            return out + b
        n_nodes = x_piece.shape[0]
        src, dst, norm = _gcn_prep(edge_index_piece, n_nodes)
        x = _gcn_layer(x_piece, src, dst, norm, W1, b1, n_nodes)
        x = jax.nn.gelu(x)
        x = _gcn_layer(x, src, dst, norm, W2, b2, n_nodes)
        x = jax.nn.gelu(x)
        x = _gcn_layer(x, src, dst, norm, W3, b3, n_nodes)
        return x

    def _L1_ffn_ref(x, attention_mask, wr, br, w1, b1, w2, b2):
        import jax, jax.numpy as jnp
        import numpy as np
        B, S, D = (8, 128, 256)
        H = 4 * D
        CAPACITY = 0.5
        b, s, d = x.shape
        weights = (jnp.einsum('bsd,do->bso', x, wr) + br)[..., 0]
        k = max(1, int(CAPACITY * s))
        kk = k - 1 if k > 1 else 1
        _, idx = jax.lax.top_k(weights, k)
        sel_idx = idx[:, :kk]
        sel = jnp.take_along_axis(x, sel_idx[:, :, None], axis=1)
        h = jax.nn.gelu(jnp.einsum('bkd,dh->bkh', sel, w1) + b1)
        y = jnp.einsum('bkh,hd->bkd', h, w2) + b2
        w_sel = jnp.take_along_axis(weights, sel_idx, axis=1)
        y = y * w_sel[..., None]
        batch_idx = jnp.arange(b)[:, None]
        processed = jnp.zeros_like(x).at[batch_idx, sel_idx].set(y)
        return processed + x

    def _L2_gnn_ref(feat, W_self, W_neigh, src, dst):
        import jax, jax.numpy as jnp
        import numpy as np
        N = 3125
        E = 50000
        IN_FEATS = 256
        OUT_FEATS = 256
        MAXK = 32

        def _maxk(x, k):
            _, idx = jax.lax.top_k(x, k)
            rows = jnp.arange(x.shape[0])[:, None]
            mask = jnp.zeros_like(x).at[rows, idx].set(1.0)
            return x * mask
        n = feat.shape[0]
        h_self = feat @ W_self
        h_neigh = feat @ W_neigh
        h_sparse = _maxk(h_neigh, MAXK)
        msg = h_sparse[src]
        summed = jax.ops.segment_sum(msg, dst, num_segments=n)
        deg = jax.ops.segment_sum(jnp.ones((src.shape[0],), dtype=feat.dtype), dst, num_segments=n)
        neigh = summed / jnp.maximum(deg, 1.0)[:, None]
        return h_self + neigh

    def _L2_ffn_ref(h, gate_w, gate_b, w1, b1, w2, b2):
        import math
        import jax, jax.numpy as jnp
        import numpy as np
        CAPACITY_FACTOR = 1.25
        B, L, D = h.shape
        E = gate_w.shape[1]
        T = B * L
        C = max(1, math.ceil(CAPACITY_FACTOR * T / E))
        x = h.reshape(T, D)
        logits = x @ gate_w + gate_b
        probs = jax.nn.softmax(logits, axis=-1)
        idx = jnp.argmax(probs, axis=-1)
        prb = jnp.take_along_axis(probs, idx[:, None], axis=1)[:, 0]
        one_hot = jax.nn.one_hot(idx, E, dtype=jnp.float32)
        pos = (jnp.cumsum(one_hot, axis=0) * one_hot).sum(-1).astype(jnp.int32) - 1
        kept = pos < C
        pos_safe = jnp.where(kept, pos, C)
        buf = jnp.zeros((E, C, D), dtype=h.dtype).at[idx, pos_safe].set(x, mode='drop')
        hmid = jax.nn.relu(jnp.einsum('ecd,edf->ecf', buf, w1) + b1[:, None, :])
        ybuf = jnp.einsum('ecf,efd->ecd', hmid, w2) + b2[:, None, :]
        pos_g = jnp.minimum(pos, C - 1)
        y_tok = ybuf[idx, pos_g] * (prb * kept)[:, None]
        y = y_tok.reshape(B, L, D)
        y = jnp.nan_to_num(y, nan=0.0, posinf=10000.0, neginf=-10000.0)
        return y

    def _L3_gnn_ref(x, edge_index, weight, attn_l, attn_r):
        import jax, jax.numpy as jnp
        import numpy as np
        N, IN_CH, HEADS, OUT_CH, E = (50000, 256, 4, 64, 25000)
        heads, out_ch = attn_l.shape
        n = x.shape[0]
        xt = jnp.matmul(x, weight).reshape(-1, heads, out_ch)
        row, col = (edge_index[0], edge_index[1])
        alpha_l = jnp.einsum('ehd,hd->eh', xt[row], attn_l)
        alpha_r = jnp.einsum('ehd,hd->eh', xt[col], attn_r)
        alpha = jax.nn.softmax(jax.nn.leaky_relu(alpha_l + alpha_r, 0.01), axis=1)
        tmp = jnp.einsum('nh,nhd->nd', alpha[:n], xt[col[:n]])
        out = jnp.broadcast_to(tmp[:, None, :], (n, heads, out_ch))
        return out.reshape(n, heads * out_ch)

    def _L3_ffn_ref(x, gate_w, gate_b, w1, b1, w2, b2, gamma, beta):
        import jax, jax.numpy as jnp
        import numpy as np
        B, S, H, F, E, K = (8, 128, 256, 512, 16, 2)
        EPS = 1e-05
        gate_logits = x @ gate_w + gate_b
        topk_vals, topk_idx = jax.lax.top_k(gate_logits, K)
        topk_w = jax.nn.softmax(topk_vals, axis=-1)
        h = jax.nn.relu(jnp.einsum('bsh,ehf->bsef', x, w1) + b1)
        expert_out = jnp.einsum('bsef,efh->bseh', h, w2) + b2
        sel = jnp.take_along_axis(expert_out, topk_idx[:, :, :, None], axis=2)
        moe = jnp.sum(topk_w[..., None] * sel, axis=2)
        y = x + moe
        mu = jnp.mean(y, axis=-1, keepdims=True)
        var = jnp.var(y, axis=-1, keepdims=True)
        return (y - mu) / jnp.sqrt(var + EPS) * gamma + beta
    edge_index = jnp.stack([src, dst])
    batch0 = jnp.zeros((625,), jnp.int32)
    x = x + _L0_gnn_ref(_layernorm(x, axis=-1), edge_index, L0_gnn_W1, L0_gnn_b1, L0_gnn_W2, L0_gnn_b2)
    x = x + _L0_ffn_ref(_layernorm(x, axis=-1)[None], L0_ffn_W_gat, L0_ffn_att_src, L0_ffn_att_dst, L0_ffn_b_gat, L0_ffn_ln_gamma, L0_ffn_ln_beta, L0_ffn_W1, L0_ffn_b1, L0_ffn_W2, L0_ffn_b2, L0_ffn_edge_index)[0]
    x = x + _L1_gnn_ref(_layernorm(x, axis=-1), edge_index, batch0, L1_gnn_W1, L1_gnn_b1, L1_gnn_W2, L1_gnn_b2, L1_gnn_W3, L1_gnn_b3)
    x = x + _L1_ffn_ref(_layernorm(x, axis=-1)[None], L1_ffn_attention_mask, L1_ffn_wr, L1_ffn_br, L1_ffn_w1, L1_ffn_b1, L1_ffn_w2, L1_ffn_b2)[0]
    x = x + _L2_gnn_ref(_layernorm(x, axis=-1), L2_gnn_W_self, L2_gnn_W_neigh, src, dst)
    x = x + _L2_ffn_ref(_layernorm(x, axis=-1)[None], L2_ffn_gate_w, L2_ffn_gate_b, L2_ffn_w1, L2_ffn_b1, L2_ffn_w2, L2_ffn_b2)[0]
    x = x + _L3_gnn_ref(_layernorm(x, axis=-1), edge_index, L3_gnn_weight, L3_gnn_attn_l, L3_gnn_attn_r)
    x = x + _L3_ffn_ref(_layernorm(x, axis=-1)[None], L3_ffn_gate_w, L3_ffn_gate_b, L3_ffn_w1, L3_ffn_b1, L3_ffn_w2, L3_ffn_b2, L3_ffn_gamma, L3_ffn_beta)[0]
    return x

_drawn_inputs = setup_inputs


def setup_inputs(seed=0):
    import zlib

    import numpy as np

    out = dict(_drawn_inputs(seed))
    spreads = {'L0_gnn_b1': (0.0, 0.1),
     'L0_gnn_b2': (0.0, 0.1),
     'L0_ffn_b_gat': (0.0, 0.1),
     'L0_ffn_ln_gamma': (1.0, 0.2),
     'L0_ffn_ln_beta': (0.0, 0.1),
     'L0_ffn_b1': (0.0, 0.1),
     'L0_ffn_b2': (0.0, 0.1),
     'L1_gnn_b1': (0.0, 0.1),
     'L1_gnn_b2': (0.0, 0.1),
     'L1_gnn_b3': (0.0, 0.1),
     'L1_ffn_b1': (0.0, 0.8),
     'L1_ffn_b2': (0.0, 0.425),
     'L2_ffn_gate_b': (0.0, 0.1),
     'L2_ffn_b1': (0.0, 0.8),
     'L2_ffn_b2': (0.0, 0.8),
     'L3_ffn_gate_b': (0.0, 0.371),
     'L3_ffn_b1': (0.0, 0.8),
     'L3_ffn_b2': (0.0, 0.369),
     'L3_ffn_gamma': (1.0, 0.2),
     'L3_ffn_beta': (0.0, 0.287)}
    factors = {'L0_ffn_att_src': 3.824, 'L0_ffn_att_dst': 8.0, 'L1_ffn_w1': 2.713, 'L3_ffn_w1': 3.077}
    for name, (base, spread) in spreads.items():
        noise = np.random.default_rng([zlib.crc32(name.encode()), seed]).standard_normal(out[name].shape)
        drawn = base * np.exp(spread * noise) if base else spread * noise
        out[name] = jnp.asarray(drawn.astype(out[name].dtype))
    for name, factor in factors.items():
        out[name] = (out[name] * factor).astype(out[name].dtype)
    return out
```

```python
from contextlib import ExitStack

import concourse.bass as bass
from concourse import mybir

ALU = mybir.AluOpType
ACT = mybir.ActivationFunctionType
AX = mybir.AxisListType
F32 = mybir.dt.float32
F16 = mybir.dt.float16
BF16 = mybir.dt.bfloat16
I32 = mybir.dt.int32
U32 = mybir.dt.uint32

N = 625
NP = 125
T = 5
D = 256
KD = D // 128
PIECES = [(0, 313), (313, 312)]
BANK = 512
EPS = 1e-5
BIG = 1e30
STOP = 8
BIAS_COLUMNS = [("L0_gnn_b1", 4), ("L0_ffn_b1", 16), ("L1_gnn_b1", 2), ("L1_gnn_b2", 2), ("L1_ffn_b1", 8),
                ("L2_ffn_b1", 64), ("L3_ffn_b1", 64), ("L1_ffn_wr", 2)]


def graph_mlp_stack(nc, a, out):
    E1 = a["src"].shape[0]
    EP1, ET1, EU1 = 125, E1 // 125, 5
    E2 = a["L0_ffn_edge_index"].shape[1]
    EP2, ET2, EU2 = 128, E2 // 128, 4
    HALF, BASE = (N + 1) // 2, 4096

    def groups(tiles, unroll, parts):
        most, left, got = (BASE - 1) // parts // unroll, tiles // unroll, []
        while left:
            got.append(min(most, left))
            left -= got[-1]
        return got
    X0, F0 = 4, 512
    HEADS = 4
    F1 = 1024
    KEEP1 = int(0.5 * N) - 1
    X2, F2 = 8, 1024
    CAP = -(-5 * N // (4 * X2))
    SL = X2 * CAP
    X3, F3 = 16, 512
    MAXK = 32
    HD3 = 64
    W3C = D + 2 * HEADS

    ctx = ExitStack()
    with ctx:
        def sb(name, shape, dt=F32):
            return ctx.enter_context(nc.sbuf_tensor(name, shape, dt))

        sems = {}

        def sem(name):
            if name not in sems:
                sems[name] = ctx.enter_context(nc.semaphore(name))
            return sems[name]

        ps = ctx.enter_context(nc.psum_tensor("ps", [128, 8, BANK], F32))
        psb = ps[:, :, :].bitcast(BF16)

        iota = sb("iota", [128, SL], F16)
        ident = sb("ident", [128, 128])
        ones = sb("ones", [128, 128])
        identb = sb("identb", [128, 128], BF16)
        onesb = sb("onesb", [128, 128], BF16)
        tri = sb("tri", [128, 128], BF16)
        zerob = sb("zerob", [1, BANK], BF16)
        node = sb("node", [128, T])
        epsc = sb("epsc", [128, 1])
        digc = sb("digc", [128, 1])
        desc = sb("desc", [128, X3])

        R1 = sb("R1", [128, 6250])
        R2 = sb("R2", [128, 12288])
        R3 = sb("R3", [128, 5250])
        RW = sb("RW", [128, 8192])
        AT = sb("AT", [128, T, N])
        AHB = sb("AHB", [128, 2 * T * N])
        Ahat = AHB[:, 0:T * N].rearrange("p (t n) -> p t n", t=T)
        BT = AHB[:, T * N:].rearrange("p (t n) -> p t n", t=T)

        x = sb("x", [128, T, D])
        xn = sb("xn", [128, T, D])
        xnT = sb("xnT", [128, KD, N])
        aggT = sb("aggT", [128, KD, N])
        h2 = sb("h2", [128, T, D])
        gT = aggT[0:X3, 0, :]

        oh_s = R1[:, 0:EU1 * 320].bitcast(BF16).rearrange("p (u n) -> p u n", u=EU1)
        oh_d = R1[:, EU1 * 320:EU1 * 480].bitcast(BF16).rearrange("p (u n) -> p u n", u=EU1)
        sums = R2[:, 0:T * HALF].rearrange("p (t n) -> p t n", t=T)
        highi = R2[:, 1600:1600 + T * HALF].bitcast(I32).rearrange("p (t n) -> p t n", t=T)
        high = R2[:, 3900:3900 + T * HALF].rearrange("p (t n) -> p t n", t=T)
        idi1 = R3[:, 0:2 * ET1].bitcast(I32).rearrange("p (a t) -> p a t", a=2)
        idf1 = R3[:, 2 * ET1:5 * ET1].rearrange("p (a t) -> p a t", a=3)
        o2 = 5 * ET1
        idi2 = R3[:, o2:o2 + 2 * ET2].bitcast(I32).rearrange("p (a t) -> p a t", a=2)
        idf2 = R3[:, o2 + 2 * ET2:o2 + 5 * ET2].rearrange("p (a t) -> p a t", a=3)
        dinvr = R2[:, 3200:3200 + N]
        Bneg = R3[:, 2100:2100 + 1563].bitcast(BF16)[:, 0:T * N].rearrange("p (t n) -> p t n", t=T)
        maskb = R3[:, 3663:3663 + 1563].bitcast(BF16)[:, 0:T * N].rearrange("p (t n) -> p t n", t=T)
        dinvc = sb("dinvc", [128, T])
        rdeg = sb("rdeg", [128, T])
        dtmp = h2[:, :, 0:NP]

        h1T = R1[:, 0:2500].rearrange("p (m n) -> p m n", m=4)
        W01 = R1[:, 3300:3300 + 1024].rearrange("p (k n) -> p k n", k=2)
        W02 = R1[:, 4400:4400 + 1024].rearrange("p (k n) -> p k n", k=4)
        bcols = sb("bcols", [128, sum(n for _, n in BIAS_COLUMNS)])
        bcol, at0 = {}, 0
        for name, n in BIAS_COLUMNS:
            bcol[name] = bcols[:, at0:at0 + n]
            at0 += n
        b01 = bcol["L0_gnn_b1"]
        b02 = sb("b02", [128, D])

        Wg = sb("Wg", [128, KD, 16])
        gatc = sb("gatc", [128, 5, 16])
        hg = sb("hg", [128, T, 16])
        haug = sb("haug", [128, T, HEADS, 5])
        prod = sb("prod", [128, T, 16])
        asd = sb("asd", [128, 7, T, HEADS])
        prow = R2[:, 0:2500].rearrange("p (h n) -> p h n", h=HEADS)
        qrow = R2[:, 2500:5000].rearrange("p (h n) -> p h n", h=HEADS)
        EE = R2[:, 5000:11250].rearrange("p (b t n) -> p b t n", b=2, t=T)
        arow = R2[:, 5000:7500].rearrange("p (h n) -> p h n", h=HEADS)
        junk = R3[:, 3700:3700 + 2 * N].rearrange("p (b n) -> p b n", b=2)
        t1 = R3[:, 0:2 * N].rearrange("p (b n) -> p b n", b=2)
        vv = R3[:, 2 * N:4 * N].rearrange("p (b n) -> p b n", b=2)
        ev = R3[:, 4 * N:6 * N].rearrange("p (b n) -> p b n", b=2)
        scr = sb("scr", [128, 7, T, 16])
        sca = sb("sca", [128, 16, T])
        FWs = [RW[:, e * 2048:(e + 1) * 2048] for e in range(X0)]
        FW1 = [w[:, 0:1024].rearrange("p (k n) -> p k n", k=KD) for w in FWs]
        FW2 = [w[:, 1024:2048].rearrange("p (k n) -> p k n", k=4) for w in FWs]
        f0b1 = bcol["L0_ffn_b1"]
        f0b2 = sb("f0b2", [X0, D])
        hh = R1[:, 0:5000].rearrange("p (b m n) -> p b m n", b=2, m=4)
        gate = sb("gate", [128, T, X3])

        Wc = sb("Wc", [128, 3, KD, D])
        bc12 = [bcol["L1_gnn_b1"], bcol["L1_gnn_b2"]]
        bc3 = sb("bc3", [128, D])
        M1 = RW[:, 0:2048].rearrange("p (k n) -> p k n", k=KD)
        M2 = RW[:, 2048:4096].rearrange("p (k n) -> p k n", k=8)
        m1b = bcol["L1_ffn_b1"]
        m2b = RW[:, 7696:7696 + D]
        wr = bcol["L1_ffn_wr"]
        br = sb("br", [128, 1])
        ltmask = AHB[:, T * N:T * N + 1563].bitcast(BF16)[:, 0:T * N].rearrange("p (t n) -> p t n", t=T)
        wrow = R3[:, 0:N]
        wj = R3[:, N:3 * N].rearrange("p (b n) -> p b n", b=2)
        hT = R1[:, 0:5000].rearrange("p (m n) -> p m n", m=8)
        wcol = sb("wcol", [128, T])
        rk = sb("rk", [128, 4, T])

        Wsn = RW[:, 4096:5120].rearrange("p (k n) -> p k n", k=KD)
        hn = R3[:, 0:1280].rearrange("p (t n) -> p t n", t=T)
        wk = R3[:, 1280:3840].rearrange("p (b t n) -> p b t n", b=2, t=T)
        top8 = sb("top8", [128, T, 4, 8])
        G2 = sb("G2", [128, KD, X2])
        g2b = sb("g2b", [128, X2])
        f2b1 = bcol["L2_ffn_b1"]
        f2b2 = RW[:, 5120:7168].rearrange("p (e n) -> p e n", e=X2)
        ohb = sb("ohb", [128, T, X2], BF16)
        slot = sb("slot", [128, T])
        prk = sb("prk", [128, T])
        SC = R1[:, 0:T * SL].rearrange("p (t s) -> p t s", t=T)
        ST = AHB[:, 0:X2 * N].rearrange("p (e n) -> p e n", e=X2)
        srow = AHB[:, X2 * N:(X2 + 1) * N]
        XbT = R3[:, 0:KD * SL].rearrange("p (k s) -> p k s", k=KD)
        hTe = R3[:, 1568:1568 + 1568].rearrange("p (b m s) -> p b m s", b=2, m=8)
        ybuf = R3[:, 3136:3136 + 2048].rearrange("p (e n) -> p e n", e=X2)
        F2W = R2[:, 0:8192].rearrange("p (b n) -> p b n", b=2)
        F2W1 = [F2W[:, b, 0:2048].rearrange("p (k n) -> p k n", k=KD) for b in range(2)]
        F2W2 = [F2W[:, b, 2048:4096].rearrange("p (k n) -> p k n", k=8) for b in range(2)]
        cst4 = sb("cst4", [128, 2])
        bnow = sb("bnow", [128, 4, 8])

        W3 = RW[:, 7168:7168 + KD * W3C].rearrange("p (k n) -> p k n", k=KD)
        att3 = Wc[:, 0, :, :]
        pr3 = h2[:, 0:2, :]
        Gc = R1[:, 0:T * N].rearrange("p (t n) -> p t n", t=T)
        Gr = R1[:, T * N:2 * T * N].rearrange("p (t n) -> p t n", t=T)
        rci = AHB[:, 0:2 * N].bitcast(I32).rearrange("p (a n) -> p a n", a=2)
        rcf = AHB[:, 2 * N:4 * N].rearrange("p (a n) -> p a n", a=2)
        xt = R3[:, 0:T * W3C].rearrange("p (t n) -> p t n", t=T)
        z3 = sb("z3", [128, 3, T, HEADS])
        tmp3 = aggT[:, :, 0:T * HD3].rearrange("p b (t c) -> p b t c", t=T)
        G3 = sb("G3", [128, KD, X3])
        g3b = sb("g3b", [128, X3])
        f3b1 = bcol["L3_ffn_b1"]
        f3b2 = Wc[0:X3, 2, 0, :]
        gam = Wc[:, 1, 0, :]
        bet = Wc[:, 1, 1, :]
        F3W = R2[:, 4096:12288].rearrange("p (b n) -> p b n", b=4)
        F3W1 = [F3W[:, b, 0:1024].rearrange("p (k n) -> p k n", k=KD) for b in range(4)]
        F3W2 = [F3W[:, b, 1024:2048].rearrange("p (k n) -> p k n", k=4) for b in range(4)]

        st = sb("st", [128, T, 6])
        mv = sb("mv", [128, T, 2])
        sd = sb("sd", [128, T])
        rs = sb("rs", [128, T])

        def row(name, n):
            return a[name].rearrange("(a n) -> a n", a=1).broadcast_to([n, a[name].shape[0]])

        def kpn(ap):
            return ap.rearrange("(k p) n -> p k n", p=128)

        def tile(t):
            return slice(t * NP, (t + 1) * NP)

        block = ctx.enter_context(nc.Block())

        @block.sync
        def _(sp):
            def load(dst, src, s):
                if STOP < {"ld_gat": 2, "ld_f0": 2, "ld_g1": 3, "ld_s1": 4, "ld_s2": 6, "ld_s3": 7, "ld_f1": 4, "ld_g2": 5, "ld_f2b": 6, "ld_g3": 7}.get(s, 0):
                    return
                sp.dma_start(dst, src).then_inc(sem(s), 16)

            for i, name in enumerate(("src", "dst")):
                load(idi1[0:EP1, i, :], a[name].rearrange("(p t) -> p t", p=EP1), "ld_edges1")
            load(x[0:NP, :, :], a["x"].rearrange("(t p) n -> p t n", p=NP), "ld_x")
            for i in range(2):
                load(idi2[0:EP2, i, :], a["L0_ffn_edge_index"][i, :].rearrange("(p t) -> p t", p=EP2), "ld_edges2")
            load(W01, kpn(a["L0_gnn_W1"]), "ld_g0")
            load(W02, kpn(a["L0_gnn_W2"]), "ld_g0")
            load(b02[0:NP, :], row("L0_gnn_b2", NP), "ld_g0")
            load(bcols[:, :], a["bias_columns"], "ld_g0")
            load(Wg[:, :, :], kpn(a["L0_ffn_W_gat"]), "ld_gat")
            for i, name in enumerate(("L0_ffn_att_src", "L0_ffn_att_dst")):
                load(gatc[0:NP, i, :], a[name].rearrange("h (a e) -> a (h e)", a=1).broadcast_to([NP, 16]), "ld_gat")
            for i, name in enumerate(("L0_ffn_b_gat", "L0_ffn_ln_gamma", "L0_ffn_ln_beta")):
                load(gatc[0:NP, 2 + i, :], row(name, NP), "ld_gat")
            for e in range(X0):
                load(RW[:, e * 2048:(e + 1) * 2048], a["L0_experts"][e], "ld_f0")
            load(f0b2[:, :], a["L0_ffn_b2"], "ld_f0")
            for i in range(3):
                load(Wc[:, i, :, :], kpn(a[f"L1_gnn_W{i + 1}"]), "ld_g1")
            load(bc3[0:NP, :], row("L1_gnn_b3", NP), "ld_g1")
            load(br[0:NP, :], row("L1_ffn_br", NP), "ld_s1")
            load(G2[:, :, :], kpn(a["L2_ffn_gate_w"]), "ld_s2")
            load(g2b[0:NP, :], row("L2_ffn_gate_b", NP), "ld_s2")
            load(G3[:, :, :], kpn(a["L3_ffn_gate_w"]), "ld_s3")
            load(g3b[0:NP, :], row("L3_ffn_gate_b", NP), "ld_s3")
            if STOP >= 3:
                sp.wait_ge(sem("f0_out_mm"), T * (X0 + 1))
                load(m2b[0:NP, :], row("L1_ffn_b2", NP), "ld_f1")
                load(M1, kpn(a["L1_ffn_w1"]), "ld_f1")
                load(M2, kpn(a["L1_ffn_w2"]), "ld_f1")
                load(Wsn[:, :, 0:D], kpn(a["L2_gnn_W_self"]), "ld_g2")
                load(Wsn[:, :, D:2 * D], kpn(a["L2_gnn_W_neigh"]), "ld_g2")
                for e in range(X2):
                    load(f2b2[0:CAP, e, :], a["L2_ffn_b2"][e:e + 1, :].broadcast_to([CAP, D]), "ld_f2b")
                load(W3[:, :, 0:D], kpn(a["L3_gnn_weight"]), "ld_g3")

            def f2_load(e, b):
                load(F2W[:, b, :], e("L2_experts"), f"ld_f2w{b}")

            def f3_load(e, b):
                load(F3W[:, b, :], e("L3_experts"), f"ld_f3w{b}")

            def of(e):
                return lambda name: a[name][e]

            def at(e):
                return lambda name: a[name][bass.ds(e, 1)].rearrange("a p n -> (a p) n")

            if STOP >= 7:
                sp.wait_ge(sem("g1e_mm"), T)
                for i, name in enumerate(("L3_gnn_attn_r", "L3_gnn_attn_l")):
                    load(att3[:, i, :], a[name].rearrange("h (a e) -> a (h e)", a=1).broadcast_to([128, D]), "ld_s3")
                load(f3b2[:, :], a["L3_ffn_b2"], "ld_s3")
                load(gam[0:NP, :], row("L3_ffn_gamma", NP), "ld_s3")
                load(bet[0:NP, :], row("L3_ffn_beta", NP), "ld_s3")
            if STOP >= 6:
                f2_load(of(0), 0)
                f2_load(of(1), 1)
            if STOP >= 8:
                f3_load(of(2), 2)
                f3_load(of(3), 3)
            if STOP >= 6:
                with sp.Fori(1, X2 // 2) as i:
                    for b in range(2):
                        sp.wait_ge(sem("f2_out_mm"), 2 * i + b - 1)
                        f2_load(at(2 * i + b), b)
            if STOP >= 8:
                sp.wait_ge(sem("f2_out_mm"), X2)
                f3_load(of(0), 0)
                f3_load(of(1), 1)
                with sp.Fori(1, X3 // 4) as i:
                    for b in range(4):
                        sp.wait_ge(sem("f3_out_mm"), T * (4 * i + b - 3))
                        f3_load(at(4 * i + b), b)
            sp.wait_ge(sem("x_final"), 1)
            sp.dma_start(out.rearrange("(t p) n -> p t n", p=NP), x[0:NP, :, :]).then_inc(sem("stored"), 16)
            sp.wait_ge(sem("stored"), 16)

        @block.gpsimd
        def _(pool):
            pool.iota(iota[:, :], pattern=[[1, SL]], base=0, channel_multiplier=0,
                      allow_small_or_imprecise_dtypes=True).then_inc(sem("c_iota"), 1)
            pool.iota(node[:, :], pattern=[[NP, T]], base=0, channel_multiplier=1,
                      allow_small_or_imprecise_dtypes=True).then_inc(sem("c_iota"), 1)
            pool.iota(desc[:, :], pattern=[[-1, X3]], base=X3, channel_multiplier=0,
                      allow_small_or_imprecise_dtypes=True).then_inc(sem("c_iota"), 1)
            pool.memset(ones[:, :], 1.0).then_inc(sem("c_set"), 1)
            pool.memset(onesb[:, :], 1.0).then_inc(sem("c_set"), 1)
            pool.memset(zerob[:, :], 0.0).then_inc(sem("c_set"), 1)
            pool.memset(epsc[:, :], EPS).then_inc(sem("c_set"), 1)
            pool.memset(haug[:, :, :, 4:5], 1.0).then_inc(sem("c_set"), 1)
            pool.memset(digc[:, :], -0.5 * (BASE - 1) / BASE).then_inc(sem("c_set"), 1)
            pool.memset(AHB[:, T * N:], 0.0).then_inc(sem("c_set"), 1)
            pool.memset(AT[:, :, :], 0.0).then_inc(sem("c_set"), 1)

            def add_high(tag, C, tiles, unroll, parts):
                for g, _ in enumerate(groups(tiles, unroll, parts)):
                    pool.wait_ge(sem(f"high{tag}"), g + 1)
                    nc.gpsimd.tensor_tensor(C[0:NP, :, HALF:N], C[0:NP, :, HALF:N], high[0:NP, :, 0:N - HALF], ALU.add
                                            ).then_inc(sem(f"counted_high{tag}"), 1)

            pool.wait_ge(sem("c_set"), 8)
            add_high("1", AT, ET1, EU1, EP1)
            if STOP >= 2:
                add_high("2", BT, ET2, EU2, EP2)
            if STOP >= 7:
                pool.wait_ge(sem("x_l2"), 1)
                for i, name in enumerate(("dst", "src")):
                    pool.dma_start(rci[0:NP, i, :], a[name][0:N].rearrange("(a n) -> a n", a=1).broadcast_to([NP, N])
                                   ).then_inc(sem("ld_rc"), 16)

        @block.tensor
        def _(pe):
            def mm(o, l, r, k, last, **kw):
                return nc.tensor.matmul(o, l, r, start=(k == 0), stop=last, **kw)

            def count_edges(tag, tiles, unroll, parts):
                first_tile = 0
                for g, iters in enumerate(groups(tiles, unroll, parts)):
                    pe_order = BANKS[g % 2]

                    def body(i, fresh):
                        for j in range(unroll):
                            pe.wait_ge(sem(f"oh_ready{tag}"), 2 * (i * unroll + j) + 2 * first_tile + 2)
                            for k, (m, b) in enumerate(pe_order):
                                start = fresh and j == 0
                                if start and g and k == 0:
                                    pe.wait_ge(sem(f"flushed{tag}"), T * (g - 1))
                                if start and g and k == 3:
                                    pe.wait_ge(sem(f"flushed{tag}"), T * (g - 1) + 2)
                                last = nc.tensor.matmul(ps[:, b, 0:HALF], oh_s[0:parts, j, m * NP:m * NP + 128],
                                                        oh_d[0:parts, j, 0:HALF], start=start, stop=False,
                                                        skip_group_check=True)
                            last.then_inc(sem(f"oh_free{tag}"), 1)
                        return last

                    body(0, True)
                    if iters > 1:
                        with pe.Fori(1, iters) as i:
                            body(i, False)
                    for m, b in pe_order:
                        last = nc.tensor.matmul(ps[:, b, 0:2], zerob[0:1, 0:128], zerob[0:1, 0:2], start=False,
                                                stop=True, skip_group_check=True)
                    last.then_inc(sem(f"count_mm{tag}"), 1)
                    first_tile += iters * unroll

            turned = [0]

            def turn():
                n = turned[0]
                turned[0] += 1
                for t in range(T):
                    pe.wait_ge(sem("xn"), T * XN_OF_TURN[n] + t + 1)
                    for k in range(KD):
                        o = ps[:, k, t * NP:(t + 1) * NP] if t < 4 else ps[:, 2, k * NP:(k + 1) * NP]
                        last = nc.tensor.transpose(o, xn[0:NP, t, k * 128:(k + 1) * 128], ident[0:NP, 0:NP])
                    if t >= 3:
                        last.then_inc(sem("turn_mm"), 1)
                pe.wait_ge(sem("turn_a"), 2 * n + 2)
                pe.wait_ge(sem("turn_v"), n + 1)

            def agg_cols(rhs_rows, s, b0=0):
                for m in range(KD):
                    for q, (c, n) in enumerate(PIECES):
                        for t in range(T):
                            last = mm(ps[:, b0 + 2 * m + q, 0:n], rhs_rows[0:NP, t, m * 128:(m + 1) * 128],
                                      Ahat[0:NP, t, c:c + n], t, t == T - 1)
                        last.then_inc(sem(s), 1)

            def agg_rows(A, rhs_rows, s, b0=0):
                for t in range(T):
                    for k in range(T):
                        last = mm(ps[0:NP, b0 + t, 0:D], A[0:NP, k, tile(t)], rhs_rows[0:NP, k, :], k, k == T - 1)
                    last.then_inc(sem(s), 1)

            def lin_cols(W, XT, K, M, s, ring=8, b0=0, wait=None, n0=0):
                for m in range(M):
                    for q, (c, n) in enumerate(PIECES):
                        u = n0 + 2 * m + q
                        if wait and u >= ring:
                            pe.wait_ge(sem(wait), u - ring + 1)
                        for k in range(K):
                            last = mm(ps[:, b0 + u % ring, 0:n], W[:, k, m * 128:(m + 1) * 128], XT[:, k, c:c + n],
                                      k, k == K - 1)
                        last.then_inc(sem(s), 1)

            def lin_rows(XT, W, K, n, s, b0=0, ring=8, wait=None, n0=0):
                for t in range(T):
                    u = n0 + t
                    if wait and u >= ring:
                        pe.wait_ge(sem(wait), u - ring + 1)
                    for k in range(K):
                        last = mm(ps[0:NP, b0 + u % ring, 0:n], XT[:, k, tile(t)], W[:, k, 0:n], k, k == K - 1)
                    last.then_inc(sem(s), 1)

            pe.wait_ge(sem("c_set"), 8)
            pe.wait_ge(sem("c_mat"), 3)
            count_edges("1", ET1, EU1, EP1)
            pe.wait_ge(sem("counted1"), 1)
            pe.wait_ge(sem("counted_high1"), len(groups(ET1, EU1, EP1)))
            pe.wait_ge(sem("flushed1"), T * len(groups(ET1, EU1, EP1)))
            for q, (c, n) in enumerate(PIECES):
                for t in range(T):
                    mm(ps[0:NP, q, 0:n], ones[0:NP, 0:NP], AT[0:NP, t, c:c + n], t, t == T - 1)
            for d in range(T):
                for t in range(T):
                    last = mm(ps[0:NP, 2, d:d + 1], AT[0:NP, t, tile(d)], ones[0:NP, 0:1], t, t == T - 1)
            last.then_inc(sem("deg_mm"), 1)
            if STOP >= 2:
                pe.wait_ge(sem("deg_v"), 1)
                count_edges("2", ET2, EU2, EP2)
                for t in range(T):
                    pe.wait_ge(sem("maskb"), t + 1)
                    for d in range(T):
                        last = nc.tensor.transpose(psb[0:NP, d, t * (NP + 1):t * (NP + 1) + NP], maskb[0:NP, t, tile(d)], identb[0:NP, 0:NP])
                last.then_inc(sem("mask_mm"), 1)
                pe.wait_ge(sem("bneg"), T)

            pe.wait_ge(sem("xn"), T)
            pe.wait_ge(sem("ahat"), 1)
            agg_cols(xn, "g0a_mm")
            pe.wait_ge(sem("g0a_ev"), 4)
            pe.wait_ge(sem("ld_g0"), 64)
            lin_cols(W01, aggT, KD, 4, "g0b_mm")
            pe.wait_ge(sem("g0b_ev"), 8)
            lin_rows(h1T, W02, 4, D, "g0c_mm")
            pe.wait_ge(sem("g0c_ev"), T)
            agg_rows(Ahat, h2, "g0d_mm")

            def row_of(c4, h, t):
                o = ps[0:NP, 2 * h, tile(t)] if t < 4 else ps[0:NP, 2 * h + 1, 0:NP]
                return nc.tensor.matmul(o, c4[0:NP, t, h:h + 1].broadcast_to([NP, NP]), ident[0:NP, 0:NP],
                                        start=True, stop=True)

            if STOP >= 2:
                turn()
                pe.wait_ge(sem("ld_gat"), 96)
                for t in range(T):
                    for k in range(KD):
                        last = mm(ps[0:NP, 3, t * 16:(t + 1) * 16], xnT[:, k, tile(t)], Wg[:, k, :], k, k == KD - 1)
                last.then_inc(sem("gat_h_mm"), 1)
                pe.wait_ge(sem("asd"), 1)
                for h in range(HEADS):
                    for t in range(T):
                        last = row_of(asd[:, 0, :, :], h, t)
                    last.then_inc(sem("arow_mm"), 1)
                pe.wait_ge(sem("pq"), 1)
                for i in range(2):
                    for h in range(HEADS):
                        if i:
                            pe.wait_ge(sem("pqrow_ev"), h + 1)
                        for t in range(T):
                            last = row_of(asd[:, 4 + i, :, :], h, t)
                        last.then_inc(sem("pqrow_mm"), 1)
                pe.wait_ge(sem("pqrow_ev"), 8)
                for h in range(HEADS):
                    pe.wait_ge(sem("ee"), T * (h + 1))
                    for d in range(T):
                        for t in range(T):
                            last = mm(ps[0:NP, 6, d * 20 + h * 5:d * 20 + h * 5 + 5], EE[0:NP, h % 2, t, tile(d)],
                                      haug[0:NP, t, h, :], t, t == T - 1)
                    last.then_inc(sem("gat_mm"), 1)
                pe.wait_ge(sem("gate"), 1)
                for t in range(T):
                    last = nc.tensor.transpose(ps[0:X0, t // 4, (t % 4) * NP:(t % 4 + 1) * NP], gate[0:NP, t, 0:X0],
                                               ident[0:NP, 0:NP])
                last.then_inc(sem("gT_mm"), 1)
                pe.wait_ge(sem("gT_ev"), 2)
                pe.wait_ge(sem("ld_f0"), 80)
                for t in range(T):
                    if t == 4:
                        pe.wait_ge(sem("f0_out_ev"), 1)
                    nc.tensor.matmul(ps[0:NP, 4 + t % 4, 0:D], gT[0:X0, tile(t)], f0b2[:, :], start=True, stop=True
                                     ).then_inc(sem("f0_out_mm"), 1)
                for e in range(X0 + 1):
                    if e < X0:
                        lin_cols(FW1[e], xnT, KD, 4, "f0_hid_mm", ring=4, wait="f0_hid_ev", n0=8 * e)
                    if e >= 1:
                        pe.wait_ge(sem("f0_hid_ev"), 8 * e)
                        lin_rows(hh[:, (e - 1) % 2, :, :], FW2[e - 1], 4, D, "f0_out_mm", b0=4, ring=4,
                                 wait="f0_out_ev", n0=T * e)

            if STOP >= 3:
                pe.wait_ge(sem("xn"), 3 * T)
                agg_cols(xn, "g1a_mm")
                pe.wait_ge(sem("ld_g1"), 64)
                pe.wait_ge(sem("g1a_ev"), 4)
                lin_cols(Wc[:, 0, :, :], aggT, KD, 2, "g1b_mm", b0=4, ring=4)
                pe.wait_ge(sem("g1b_ev"), 4)
                lin_rows(h1T, Wc[:, 1, :, :], KD, D, "g1c_mm")
                pe.wait_ge(sem("g1c_ev"), T)
                agg_cols(h2, "g1d_mm")
                pe.wait_ge(sem("g1d_ev"), 4)
                lin_rows(aggT, Wc[:, 2, :, :], KD, D, "g1e_mm")
                pe.wait_ge(sem("g1e_ev"), T)
                agg_rows(Ahat, h2, "g1f_mm")

            if STOP >= 4:
                turn()
                pe.wait_ge(sem("ld_s1"), 16)
                for q, (c, n) in enumerate(PIECES):
                    for k in range(KD):
                        last = mm(ps[0:NP, 4 + q, 0:n], wr[:, k:k + 1].broadcast_to([128, NP]), xnT[:, k, c:c + n],
                                  k, k == KD - 1)
                last.then_inc(sem("wrow_mm"), 1)
                pe.wait_ge(sem("ld_f1"), 48)
                lin_cols(M1, xnT, KD, 8, "f1_hid_mm", ring=4, wait="f1_hid_ev")
                pe.wait_ge(sem("f1_hid_ev"), 16)
                pe.wait_ge(sem("wrow_ev"), 2)
                lin_rows(hT, M2, 8, D, "f1_out_mm")

            if STOP >= 5:
                turn()
                pe.wait_ge(sem("ld_g2"), 32)
                lin_rows(xnT, Wsn, KD, 2 * D, "g2a_mm", b0=3, ring=5)
                pe.wait_ge(sem("hs"), T)
                agg_rows(AT, hn, "g2b_mm")

            if STOP >= 6:
                turn()
                pe.wait_ge(sem("ld_s2"), 32)
                for t in range(T):
                    for k in range(KD):
                        last = mm(ps[0:NP, 3, t * X2:(t + 1) * X2], xnT[:, k, tile(t)], G2[:, k, :], k, k == KD - 1)
                last.then_inc(sem("lg2_mm"), 1)
                pe.wait_ge(sem("ohb"), 1)
                for t in range(T):
                    for s in range(t + 1):
                        last = mm(ps[0:NP, 4, t * X2:(t + 1) * X2], (tri if s == t else onesb)[0:NP, 0:NP],
                                  ohb[0:NP, s, :], s, s == t)
                last.then_inc(sem("pos_mm"), 1)
                pe.wait_ge(sem("slot"), 1)
                for t in range(T):
                    o = ps[0:NP, 5, tile(t)] if t < 4 else ps[0:NP, 6, 0:NP]
                    last = nc.tensor.matmul(o, slot[0:NP, t:t + 1].broadcast_to([NP, NP]), ident[0:NP, 0:NP],
                                            start=True, stop=True)
                last.then_inc(sem("srow_mm"), 1)
                pe.wait_ge(sem("sc"), T)
                for m in range(KD):
                    for q in range(2):
                        for t in range(T):
                            last = mm(ps[:, 2 * m + q, 0:SL // 2], xn[0:NP, t, m * 128:(m + 1) * 128],
                                      SC[0:NP, t, q * (SL // 2):(q + 1) * (SL // 2)], t, t == T - 1)
                        last.then_inc(sem("disp_mm"), 1)
                pe.wait_ge(sem("disp_ev"), 4)
                pe.wait_ge(sem("srow_ev"), 2)

                def f2_hid(e, b):
                    pe.wait_ge(sem(f"ld_f2w{b}"), 8 * (e - b) + 16)
                    for m in range(8):
                        for k in range(KD):
                            last = mm(ps[:, 2 * b + m // 4, (m % 4) * CAP:(m % 4 + 1) * CAP],
                                      F2W1[b][:, k, m * 128:(m + 1) * 128], XbT[:, k, bass.ds(e * CAP, CAP)],
                                      k, k == KD - 1)
                        if m % 4 == 3:
                            last.then_inc(sem("f2_hid_mm"), 1)

                def f2_out(e, b):
                    pe.wait_ge(sem("f2_hid_ev"), 8 * e + 8)
                    for k in range(8):
                        last = mm(ps[0:CAP, 4 + b, 0:D], hTe[:, b, k, :], F2W2[b][:, k, :], k, k == 7)
                    last.then_inc(sem("f2_out_mm"), 1)

                f2_hid(0, 0)
                f2_hid(1, 1)
                f2_out(0, 0)
                with pe.Fori(1, X2 // 2) as i:
                    f2_hid(2 * i, 0)
                    pe.wait_ge(sem("f2_out_ev"), 2 * i - 1)
                    f2_out(2 * i - 1, 1)
                    f2_hid(2 * i + 1, 1)
                    pe.wait_ge(sem("f2_out_ev"), 2 * i)
                    f2_out(2 * i, 0)
                f2_out(X2 - 1, 1)
                pe.wait_ge(sem("f2_out_ev"), X2)
                pe.wait_ge(sem("st"), X2)
                for t in range(T):
                    for e in range(X2):
                        last = mm(ps[0:NP, t, 0:D], ST[0:CAP, e, tile(t)], ybuf[0:CAP, e, :], e, e == X2 - 1)
                    last.then_inc(sem("comb_mm"), 1)

            if STOP >= 7:
                turn()
                pe.wait_ge(sem("w3"), 1)
                lin_rows(xnT, W3, KD, W3C, "g3a_mm", b0=3, ring=5)
                pe.wait_ge(sem("g3a_ev"), T)
                pe.wait_ge(sem("gcr"), 2 * T)
                for t in range(T):
                    for s in range(T):
                        mm(ps[0:NP, t, 0:D + HEADS], Gc[0:NP, s, tile(t)], xt[0:NP, s, 0:D + HEADS], s, s == T - 1,
                           skip_group_check=True)
                    for s in range(T):
                        last = nc.tensor.matmul(ps[0:NP, t, D:D + HEADS], Gr[0:NP, s, tile(t)], xt[0:NP, s, D + HEADS:W3C],
                                                start=False, stop=(s == T - 1), skip_group_check=True)
                    last.then_inc(sem("g3b_mm"), 1)

            if STOP >= 8:
                turn()
                pe.wait_ge(sem("ld_s3"), 112)
                for t in range(T):
                    for k in range(KD):
                        last = mm(ps[0:NP, 3, t * X3:(t + 1) * X3], xnT[:, k, tile(t)], G3[:, k, :], k, k == KD - 1)
                last.then_inc(sem("lg3_mm"), 1)
                pe.wait_ge(sem("gate"), 2)
                for t in range(T):
                    last = nc.tensor.transpose(ps[0:X3, t // 4, (t % 4) * NP:(t % 4 + 1) * NP], gate[0:NP, t, :],
                                               ident[0:NP, 0:NP])
                last.then_inc(sem("gT_mm"), 1)
                pe.wait_ge(sem("gT_ev"), 4)
                for t in range(T):
                    if t == 4:
                        pe.wait_ge(sem("f3_out_ev"), 1)
                    nc.tensor.matmul(ps[0:NP, 4 + t % 4, 0:D], gT[:, tile(t)], f3b2[:, :], start=True, stop=True
                                     ).then_inc(sem("f3_bias_mm"), 1)

                def f3_hid(e, b):
                    pe.wait_ge(sem(f"ld_f3w{b}"), 4 * (e - b) + 16)
                    for m in range(4):
                        for q, (c, n) in enumerate(PIECES):
                            u = 2 * m + q
                            if isinstance(e, int):
                                if 8 * e + u >= 4:
                                    pe.wait_ge(sem("f3_hid_ev"), 8 * e + u - 3)
                            else:
                                pe.wait_ge(sem("f3_hid_ev"), 8 * e + (u - 3))
                            for k in range(KD):
                                last = mm(ps[:, u % 4, 0:n], F3W1[b][:, k, m * 128:(m + 1) * 128], xnT[:, k, c:c + n],
                                          k, k == KD - 1)
                            last.then_inc(sem("f3_hid_mm"), 1)

                def f3_out(e, b):
                    pe.wait_ge(sem("f3_hid_ev"), 8 * e + 8)
                    for t in range(T):
                        pe.wait_ge(sem("f3_out_ev"), T * e + t + T - 3)
                        for k in range(4):
                            last = mm(ps[0:NP, 4 + (t + T * b + T) % 4, 0:D], hh[:, b % 2, k, tile(t)], F3W2[b][:, k, :],
                                      k, k == 3)
                        last.then_inc(sem("f3_out_mm"), 1)

                f3_hid(0, 0)
                with pe.Fori(0, X3 // 4 - 1) as i:
                    for b in range(4):
                        f3_hid(4 * i + b + 1, (b + 1) % 4)
                        f3_out(4 * i + b, b)
                for b in range(4):
                    if b < 3:
                        f3_hid(X3 - 4 + b + 1, b + 1)
                    f3_out(X3 - 4 + b, b)


        @block.scalar
        def _(act):
            def std(n):
                act.wait_ge(sem("ln_var"), n + 1)
                nc.scalar.activation(sd[0:NP, :], mv[0:NP, :, 1], ACT.Sqrt, bias=epsc[0:NP, :]).then_inc(sem("ln_std"), 1)

            turned = [0]

            def turn():
                n = turned[0]
                turned[0] += 1
                act.wait_ge(sem("turn_mm"), 2 * n + 1)
                nc.scalar.copy(xnT[:, 0, 0:4 * NP], ps[:, 0, 0:4 * NP]).then_inc(sem("turn_a"), 1)
                act.wait_ge(sem("turn_mm"), 2 * n + 2)
                nc.scalar.copy(xnT[:, :, 4 * NP:N], ps[:, 2, 0:2 * NP].rearrange("p (k n) -> p k n", k=2)
                               ).then_inc(sem("turn_a"), 1)

            def flush(tag, tiles, unroll, parts):
                for g, _ in enumerate(groups(tiles, unroll, parts)):
                    act.wait_ge(sem(f"count_mm{tag}"), g + 1)
                    if g:
                        act.wait_ge(sem(f"sums_used{tag}"), g)
                        act.wait_ge(sem(f"counted_high{tag}"), g)
                    for m, b in sorted(BANKS[g % 2], key=lambda mb: mb[1]):
                        nc.scalar.copy(sums[0:NP, m, :], ps[0:NP, b, 0:HALF]).then_inc(sem(f"flushed{tag}"), 1)
                    act.wait_ge(sem(f"flushed{tag}"), T * (g + 1))
                    nc.scalar.activation(highi[0:NP, :, :], sums[0:NP, :, :], ACT.Identity, scale=1.0 / BASE,
                                         bias=digc[0:NP, :]).then_inc(sem(f"rounded{tag}"), 1)
                    act.wait_ge(sem(f"rounded{tag}"), g + 1)
                    nc.scalar.copy(high[0:NP, :, :], highi[0:NP, :, :]).then_inc(sem(f"high{tag}"), 1)

            act.wait_ge(sem("c_set"), 8)
            flush("1", ET1, EU1, EP1)
            std(0)
            act.wait_ge(sem("deg1"), 1)
            nc.scalar.activation(dinvr[0:NP, :], dinvr[0:NP, :], ACT.Sqrt).then_inc(sem("deg_sqrt"), 1)
            nc.scalar.activation(dinvc[0:NP, :], dinvc[0:NP, :], ACT.Sqrt).then_inc(sem("deg_sqrt"), 1)
            if STOP >= 2:
                flush("2", ET2, EU2, EP2)

            def drain_cols(mm_sem, ev_sem, dst, func=ACT.Copy, bias=None, M=KD, b0=0):
                for m in range(M):
                    for q, (c, n) in enumerate(PIECES):
                        act.wait_ge(sem(mm_sem), 2 * m + q + 1)
                        kw = {} if bias is None else {"bias": bias[:, m:m + 1]}
                        nc.scalar.activation(dst[:, m, c:c + n], ps[:, b0 + 2 * m + q, 0:n], func, **kw
                                             ).then_inc(sem(ev_sem), 1)

            def drain_rows(mm_sem, ev_sem, dst, w, b0=0):
                for t in range(T):
                    act.wait_ge(sem(mm_sem), t + 1)
                    nc.scalar.copy(dst[0:NP, t, 0:w], ps[0:NP, b0 + t, 0:w]).then_inc(sem(ev_sem), 1)

            drain_cols("g0a_mm", "g0a_ev", aggT)
            act.wait_ge(sem("ld_g0"), 64)
            drain_cols("g0b_mm", "g0b_ev", h1T, ACT.Relu, b01, M=4)
            drain_rows("g0c_mm", "g0c_ev", h2, D)

            if STOP >= 2:
                std(1)
                turn()
                for h in range(HEADS):
                    act.wait_ge(sem("arow_mm"), h + 1)
                    nc.scalar.copy(arow[0:NP, h, 0:4 * NP], ps[0:NP, 2 * h, 0:4 * NP])
                    nc.scalar.copy(arow[0:NP, h, 4 * NP:N], ps[0:NP, 2 * h + 1, 0:NP]).then_inc(sem("arow_ev"), 1)
                for i, r in enumerate((prow, qrow)):
                    for h in range(HEADS):
                        act.wait_ge(sem("pqrow_mm"), 4 * i + h + 1)
                        nc.scalar.copy(r[0:NP, h, 0:4 * NP], ps[0:NP, 2 * h, 0:4 * NP])
                        nc.scalar.copy(r[0:NP, h, 4 * NP:N], ps[0:NP, 2 * h + 1, 0:NP]).then_inc(sem("pqrow_ev"), 1)
                for i in range(HEADS * T):
                    act.wait_ge(sem("vv"), i + 1)
                    if i >= 2:
                        act.wait_ge(sem("ee"), i - 1)
                    nc.scalar.activation(ev[0:NP, i % 2, :], vv[0:NP, i % 2, :], ACT.Exp).then_inc(sem("ev"), 1)
                act.wait_ge(sem("var16"), 1)
                nc.scalar.activation(sca[0:NP, 2, :], sca[0:NP, 1, :], ACT.Sqrt, scale=1.0 / 16, bias=epsc[0:NP, :]
                                     ).then_inc(sem("std16"), 1)
                act.wait_ge(sem("gd"), 1)
                nc.scalar.activation(sca[0:NP, 8, :], sca[0:NP, 7, :], ACT.Exp).then_inc(sem("ge"), 1)
                act.wait_ge(sem("gT_mm"), 1)
                nc.scalar.copy(gT[0:X0, 0:4 * NP], ps[0:X0, 0, 0:4 * NP]).then_inc(sem("gT_ev"), 1)
                nc.scalar.copy(gT[0:X0, 4 * NP:N], ps[0:X0, 1, 0:NP]).then_inc(sem("gT_ev"), 1)
                act.wait_ge(sem("ld_f0"), 80)
                for e in range(X0):
                    if e >= 2:
                        act.wait_ge(sem("f0_out_mm"), T * e)
                    for m in range(4):
                        for q, (c, n) in enumerate(PIECES):
                            u = 8 * e + 2 * m + q
                            act.wait_ge(sem("f0_hid_mm"), u + 1)
                            nc.scalar.activation(hh[:, e % 2, m, c:c + n], ps[:, u % 4, 0:n], ACT.Gelu,
                                                 bias=f0b1[:, 4 * e + m:4 * e + m + 1]).then_inc(sem("f0_hid_ev"), 1)

            if STOP >= 3:
                std(2)
                drain_cols("g1a_mm", "g1a_ev", aggT)
                act.wait_ge(sem("ld_g1"), 64)
                drain_cols("g1b_mm", "g1b_ev", h1T, ACT.Gelu_apprx_tanh, bc12[0], b0=4)
                drain_rows("g1c_mm", "g1c_ev", h2, D)
                drain_cols("g1d_mm", "g1d_ev", aggT, ACT.Gelu_apprx_tanh, bc12[1])
                drain_rows("g1e_mm", "g1e_ev", h2, D)
            if STOP >= 4:
                std(3)
                turn()
                act.wait_ge(sem("wrow_mm"), 1)
                act.wait_ge(sem("ld_s1"), 16)
                for q, (c, n) in enumerate(PIECES):
                    nc.scalar.activation(wrow[0:NP, c:c + n], ps[0:NP, 4 + q, 0:n], ACT.Identity, bias=br[0:NP, :]
                                         ).then_inc(sem("wrow_ev"), 1)
                for m in range(8):
                    for q, (c, n) in enumerate(PIECES):
                        u = 2 * m + q
                        act.wait_ge(sem("f1_hid_mm"), u + 1)
                        nc.scalar.activation(hT[:, m, c:c + n], ps[:, u % 4, 0:n], ACT.Gelu_apprx_tanh,
                                             bias=m1b[:, m:m + 1]).then_inc(sem("f1_hid_ev"), 1)
            if STOP >= 5:
                std(4)
                turn()
                for t in range(T):
                    act.wait_ge(sem("g2a_v"), t + 1)
                    nc.scalar.copy(hn[0:NP, t, :], ps[0:NP, 3 + t, D:2 * D]).then_inc(sem("hn"), 1)
            if STOP >= 6:
                std(5)
                turn()
                act.wait_ge(sem("l2d"), 1)
                nc.scalar.activation(scr[0:NP, 1, :, 0:X2], scr[0:NP, 0, :, 0:X2], ACT.Exp).then_inc(sem("l2e"), 1)
                act.wait_ge(sem("srow_mm"), 1)
                nc.scalar.copy(srow[0:NP, 0:4 * NP], ps[0:NP, 5, 0:4 * NP]).then_inc(sem("srow_ev"), 1)
                nc.scalar.copy(srow[0:NP, 4 * NP:N], ps[0:NP, 6, 0:NP]).then_inc(sem("srow_ev"), 1)
                for u in range(4):
                    act.wait_ge(sem("disp_mm"), u + 1)
                    nc.scalar.copy(XbT[:, u // 2, (u % 2) * (SL // 2):(u % 2 + 1) * (SL // 2)], ps[:, u, 0:SL // 2]
                                   ).then_inc(sem("disp_ev"), 1)
                act.wait_ge(sem("ld_s2"), 32)

                def f2_drain(e, b, first):
                    nc.scalar.copy(bnow[:, b, :], f2b1[:, bass.ds(8 * e, 8)]).then_inc(sem("f2_bias"), 1)
                    act.wait_ge(sem("f2_bias"), e + 1)
                    if not first:
                        act.wait_ge(sem("f2_out_mm"), e - 1)
                    for m in range(8):
                        if m % 4 == 0:
                            act.wait_ge(sem("f2_hid_mm"), 2 * e + m // 4 + 1)
                        nc.scalar.activation(hTe[:, b, m, :], ps[:, 2 * b + m // 4, (m % 4) * CAP:(m % 4 + 1) * CAP],
                                             ACT.Relu, bias=bnow[:, b, m:m + 1]).then_inc(sem("f2_hid_ev"), 1)

                for b in range(2):
                    f2_drain(b, b, True)
                with act.Fori(1, X2 // 2) as i:
                    for b in range(2):
                        f2_drain(2 * i + b, b, False)
            if STOP >= 7:
                std(6)
                turn()
                drain_rows("g3a_mm", "g3a_ev", xt, W3C, b0=3)
                act.wait_ge(sem("a3d"), 1)
                nc.scalar.activation(z3[0:NP, 1, :, :], z3[0:NP, 0, :, :], ACT.Exp).then_inc(sem("a3e"), 1)
            if STOP >= 8:
                std(7)
                turn()
                act.wait_ge(sem("gd"), 2)
                nc.scalar.activation(sca[0:NP, 8, :], sca[0:NP, 7, :], ACT.Exp).then_inc(sem("ge"), 1)
                act.wait_ge(sem("gT_mm"), 2)
                nc.scalar.copy(gT[0:X3, 0:4 * NP], ps[0:X3, 0, 0:4 * NP]).then_inc(sem("gT_ev"), 1)
                nc.scalar.copy(gT[0:X3, 4 * NP:N], ps[0:X3, 1, 0:NP]).then_inc(sem("gT_ev"), 1)

                def f3_drain(e, b, first):
                    nc.scalar.copy(bnow[:, b, 0:4], f3b1[:, bass.ds(4 * e, 4)]).then_inc(sem("f3_bias"), 1)
                    act.wait_ge(sem("f3_bias"), e + 1)
                    if not first:
                        act.wait_ge(sem("f3_out_mm"), T * e - T)
                    for m in range(4):
                        for q, (c, n) in enumerate(PIECES):
                            act.wait_ge(sem("f3_hid_mm"), 8 * e + 2 * m + q + 1)
                            nc.scalar.activation(hh[:, b % 2, m, c:c + n], ps[:, (2 * m + q) % 4, 0:n], ACT.Relu,
                                                 bias=bnow[:, b, m:m + 1]).then_inc(sem("f3_hid_ev"), 1)

                for b in range(4):
                    f3_drain(b, b, b < 2)
                with act.Fori(1, X3 // 4) as i:
                    for b in range(4):
                        f3_drain(4 * i + b, b, False)
                std(8)

        @block.vector
        def _(dve):
            V = nc.vector
            chain = [0]

            def link(ins):
                chain[0] += 1
                ins.then_inc(sem("dve_chain"), 1)
                dve.wait_ge(sem("dve_chain"), chain[0])

            norms = [0]

            def norm(src):
                n = norms[0]
                norms[0] += 1
                for t in range(T):
                    i = V.bn_stats(st[0:NP, t, :], src[0:NP, t, :])
                link(i)
                for t in range(T):
                    i = V.bn_aggr(mv[0:NP, t, :], st[0:NP, t, :])
                i.then_inc(sem("ln_var"), 1)
                dve.wait_ge(sem("ln_std"), n + 1)
                link(V.reciprocal(rs[0:NP, :], sd[0:NP, :]))
                for t in range(T):
                    V.tensor_scalar(xn[0:NP, t, :], src[0:NP, t, :], mv[0:NP, t, 0:1], rs[0:NP, t:t + 1],
                                    ALU.subtract, ALU.mult).then_inc(sem("xn"), 1)
                dve.wait_ge(sem("xn"), T * (n + 1))

            turned = [0]

            def turn():
                n = turned[0]
                turned[0] += 1
                dve.wait_ge(sem("turn_mm"), 2 * n + 1)
                V.tensor_copy(xnT[:, 1, 0:4 * NP], ps[:, 1, 0:4 * NP]).then_inc(sem("turn_v"), 1)

            def digits(parts, idf, idi):
                d, w = idf[0:parts, 1, :], idf[0:parts, 2, :]
                link(V.tensor_copy(d, idi[0:parts, 1, :]))
                link(V.tensor_scalar(w, d, float(HALF), float(BASE - 1), ALU.is_ge, ALU.mult))
                link(V.tensor_scalar(w, w, 1.0, None, ALU.add))
                link(V.scalar_tensor_tensor(out=w, in0=d, scalar=float(N), in1=w, op0=ALU.is_lt, op1=ALU.mult))
                h = sums[0:parts, 0, 0:idf.shape[2]]
                link(V.tensor_scalar(h, d, float(HALF), float(-HALF), ALU.is_ge, ALU.mult))
                link(V.tensor_tensor(d, d, h, ALU.add))

            def one_hots(tag, C, tiles, unroll, parts, idf):
                first_tile = 0

                def part(k, g):
                    if k == 0:
                        dve.wait_ge(sem(f"high{tag}"), g + 1)
                        link(V.scalar_tensor_tensor(out=sums[0:NP, :, :], in0=high[0:NP, :, :], scalar=float(-BASE),
                                                    in1=sums[0:NP, :, :], op0=ALU.mult, op1=ALU.add))
                    else:
                        V.tensor_tensor(C[0:NP, :, 0:HALF], C[0:NP, :, 0:HALF], sums[0:NP, :, :], ALU.add
                                        ).then_inc(sem(f"sums_used{tag}"), 1)

                for g, iters in enumerate(groups(tiles, unroll, parts)):
                    def body(i, fresh):
                        for j in range(unroll):
                            if not fresh:
                                dve.wait_ge(sem(f"oh_free{tag}"), i * unroll + (first_tile + j + 1 - unroll))
                            V.tensor_scalar(oh_s[0:parts, j, 0:N + 3], iota[0:parts, 0:N + 3],
                                            idf[0:parts, 0, bass.ds(i * unroll + (first_tile + j), 1)], None,
                                            ALU.is_equal).then_inc(sem(f"oh_ready{tag}"), 1)
                            V.tensor_scalar(oh_d[0:parts, j, 0:HALF], iota[0:parts, 0:HALF],
                                            idf[0:parts, 1, bass.ds(i * unroll + (first_tile + j), 1)],
                                            idf[0:parts, 2, bass.ds(i * unroll + (first_tile + j), 1)],
                                            ALU.is_equal, ALU.mult).then_inc(sem(f"oh_ready{tag}"), 1)

                    cuts = sorted({0, 1, min(4, iters), min(5, iters), iters})
                    for lo, hi in zip(cuts, cuts[1:]):
                        if lo == 0:
                            body(0, g == 0)
                        else:
                            with dve.Fori(lo, hi) as i:
                                body(i, False)
                        if g and hi == min(4, iters):
                            part(0, g - 1)
                        if g and hi == min(5, iters):
                            part(1, g - 1)
                    first_tile += iters * unroll
                part(0, g)
                part(1, g)
                dve.wait_ge(sem(f"sums_used{tag}"), g + 1)
                dve.wait_ge(sem(f"counted_high{tag}"), g + 1)

            def first_max(vals, E, oh, top, tmp):
                link(V.tensor_reduce(top, vals, AX.X, ALU.max))
                link(V.tensor_tensor(tmp, vals, top.unsqueeze(2).broadcast_to([NP, T, E]), ALU.is_equal))
                link(V.tensor_tensor(tmp, tmp, desc[0:NP, 0:E].unsqueeze(1).broadcast_to([NP, T, E]), ALU.mult))
                link(V.tensor_reduce(sca[0:NP, 15, :], tmp, AX.X, ALU.max))
                link(V.tensor_tensor(oh, tmp, sca[0:NP, 15, :].unsqueeze(2).broadcast_to([NP, T, E]), ALU.is_equal))

            def top2_gate(vals, E, n):
                oh1, oh2, tmp = (scr[0:NP, i, :, 0:E] for i in (3, 4, 5))
                first_max(vals, E, oh1, sca[0:NP, 5, :], tmp)
                link(V.scalar_tensor_tensor(out=scr[0:NP, 6, :, 0:E], in0=oh1, scalar=-3e38, in1=vals,
                                            op0=ALU.mult, op1=ALU.add))
                first_max(scr[0:NP, 6, :, 0:E], E, oh2, sca[0:NP, 6, :], tmp)
                V.tensor_tensor(sca[0:NP, 7, :], sca[0:NP, 6, :], sca[0:NP, 5, :], ALU.subtract).then_inc(sem("gd"), 1)
                dve.wait_ge(sem("ge"), n)
                link(V.tensor_scalar(sca[0:NP, 9, :], sca[0:NP, 8, :], 1.0, None, ALU.add))
                link(V.reciprocal(sca[0:NP, 10, :], sca[0:NP, 9, :]))
                link(V.tensor_tensor(sca[0:NP, 11, :], sca[0:NP, 8, :], sca[0:NP, 10, :], ALU.mult))
                V.tensor_tensor(oh1, oh1, sca[0:NP, 10, :].unsqueeze(2).broadcast_to([NP, T, E]), ALU.mult)
                link(V.tensor_tensor(oh2, oh2, sca[0:NP, 11, :].unsqueeze(2).broadcast_to([NP, T, E]), ALU.mult))
                link(V.tensor_tensor(gate[0:NP, :, 0:E], oh1, oh2, ALU.add))

            dve.wait_ge(sem("c_iota"), 3)
            V.tensor_scalar(ident[:, :], iota[:, 0:128], node[:, 0:1], None, ALU.is_equal).then_inc(sem("c_mat"), 1)
            V.tensor_scalar(identb[:, :], iota[:, 0:128], node[:, 0:1], None, ALU.is_equal).then_inc(sem("c_mat"), 1)
            V.tensor_scalar(tri[:, :], iota[:, 0:128], node[:, 0:1], None, ALU.is_ge).then_inc(sem("c_mat"), 1)
            dve.wait_ge(sem("ld_edges1"), 32)
            link(V.tensor_copy(idf1[0:EP1, 0, :], idi1[0:EP1, 0, :]))
            digits(EP1, idf1, idi1)
            dve.wait_ge(sem("c_set"), 8)
            one_hots("1", AT, ET1, EU1, EP1, idf1)
            V.memset(sca[0:NP, 13, :], 0.0).then_inc(sem("counted1"), 1)
            dve.wait_ge(sem("ld_x"), 16)
            dve.wait_ge(sem("c_set"), 8)
            norm(x)
            dve.wait_ge(sem("ld_edges2"), 32)
            digits(EP2, idf2, idi2)
            link(V.tensor_scalar(idf2[0:EP2, 0, :], idi2[0:EP2, 0, :], float(N - 1), None, ALU.min))
            dve.wait_ge(sem("deg_mm"), 1)
            for q, (c, n) in enumerate(PIECES):
                V.tensor_scalar(dinvr[0:NP, c:c + n], ps[0:NP, q, 0:n], 1.0, 1.0, ALU.add, ALU.max)
            link(V.tensor_scalar(rdeg[0:NP, :], ps[0:NP, 2, 0:T], 1.0, None, ALU.max))
            V.tensor_scalar(dinvc[0:NP, :], ps[0:NP, 2, 0:T], 1.0, 1.0, ALU.add, ALU.max).then_inc(sem("deg1"), 1)
            link(V.reciprocal(rdeg[0:NP, :], rdeg[0:NP, :]))
            dve.wait_ge(sem("deg_sqrt"), 2)
            V.reciprocal(dinvc[0:NP, :], dinvc[0:NP, :])
            link(V.reciprocal(dinvr[0:NP, :], dinvr[0:NP, :]))
            for t in range(T):
                V.scalar_tensor_tensor(out=Ahat[0:NP, t, :], in0=AT[0:NP, t, :], scalar=dinvc[0:NP, t:t + 1],
                                       in1=dinvr[0:NP, :], op0=ALU.mult, op1=ALU.mult)
                i = V.scalar_tensor_tensor(out=dtmp[0:NP, t, :], in0=ident[0:NP, 0:NP], scalar=dinvc[0:NP, t:t + 1],
                                           in1=dinvr[0:NP, tile(t)], op0=ALU.mult, op1=ALU.mult)
            link(i)
            for t in range(T):
                i = V.tensor_tensor(Ahat[0:NP, t, tile(t)], Ahat[0:NP, t, tile(t)], dtmp[0:NP, t, :], ALU.add)
            i.then_inc(sem("ahat"), 1)
            i = V.tensor_scalar(sca[0:NP, 0, :], dinvc[0:NP, :], 1.0, None, ALU.mult)
            i.then_inc(sem("deg_v"), 1)
            if STOP >= 2:
                one_hots("2", BT, ET2, EU2, EP2, idf2)
                for t in range(T):
                    i = V.tensor_tensor(BT[0:NP, t, tile(t)], BT[0:NP, t, tile(t)], ident[0:NP, 0:NP], ALU.add)
                link(i)
                for t in range(T):
                    V.tensor_scalar(maskb[0:NP, t, :], BT[0:NP, t, :], 1.0, None, ALU.min).then_inc(sem("maskb"), 1)
                dve.wait_ge(sem("mask_mm"), 1)
                for t in range(T):
                    V.tensor_scalar(Bneg[0:NP, t, :].rearrange("p (s c) -> p s c", c=NP),
                                    psb[0:NP, t, 0:T * (NP + 1)].rearrange("p (s c) -> p s c", c=NP + 1)[:, :, 0:NP], 1.0, BIG, ALU.subtract, ALU.mult
                                    ).then_inc(sem("bneg"), 1)

            def add_rows(mm_sem, b0=0, bank=lambda t: t):
                for t in range(T):
                    dve.wait_ge(sem(mm_sem), t + 1)
                    i = V.tensor_tensor(x[0:NP, t, :], ps[0:NP, b0 + bank(t), 0:D], x[0:NP, t, :], ALU.add)
                return i

            def add_bias(b):
                link(V.tensor_tensor(x[0:NP, :, :], x[0:NP, :, :], b[0:NP, :].unsqueeze(1).broadcast_to([NP, T, D]),
                                     ALU.add))

            dve.wait_ge(sem("ld_g0"), 64)
            add_bias(b02)
            last = add_rows("g0d_mm")

            if STOP >= 2:
                link(last)
                norm(x)
                turn()
                dve.wait_ge(sem("gat_h_mm"), 1)
                dve.wait_ge(sem("ld_gat"), 96)
                V.tensor_copy(haug[0:NP, :, :, 0:4], ps[0:NP, 3, 0:80].rearrange("p (t h c) -> p t h c", t=T, h=HEADS))
                link(V.tensor_copy(hg[0:NP, :, :].rearrange("p t c -> p (t c)"), ps[0:NP, 3, 0:80]))
                for i in range(2):
                    link(V.tensor_tensor(prod[0:NP, :, :], hg[0:NP, :, :],
                                         gatc[0:NP, i, :].unsqueeze(1).broadcast_to([NP, T, 16]), ALU.mult))
                    link(V.tensor_reduce(asd[0:NP, i, :, :].rearrange("p t h -> p (t h)"),
                                         prod[0:NP, :, :].rearrange("p t (h c) -> p (t h) c", c=4), AX.X, ALU.add))
                V.tensor_scalar(asd[0:NP, 6, :, :], asd[0:NP, 0, :, :], 0.2, None, ALU.mult).then_inc(sem("asd"), 1)
                n = 0
                for h in range(HEADS):
                    dve.wait_ge(sem("arow_ev"), h + 1)
                    for t in range(T):
                        link(V.tensor_tensor_reduce(out=junk[0:NP, n % 2, :], in0=Bneg[0:NP, t, :], in1=arow[0:NP, h, :],
                                                    scale=1.0, scalar=-3e38, op0=ALU.add, op1=ALU.max,
                                                    accum_out=asd[0:NP, 2, t, h:h + 1]))
                        n += 1
                link(V.tensor_tensor(asd[0:NP, 2, :, :], asd[0:NP, 2, :, :], asd[0:NP, 1, :, :], ALU.add))
                link(V.scalar_tensor_tensor(out=asd[0:NP, 3, :, :], in0=asd[0:NP, 2, :, :], scalar=0.2,
                                            in1=asd[0:NP, 2, :, :], op0=ALU.mult, op1=ALU.max))
                V.tensor_tensor(asd[0:NP, 4, :, :], asd[0:NP, 1, :, :], asd[0:NP, 3, :, :], ALU.subtract)
                V.scalar_tensor_tensor(out=asd[0:NP, 5, :, :], in0=asd[0:NP, 1, :, :], scalar=0.2,
                                       in1=asd[0:NP, 3, :, :], op0=ALU.mult, op1=ALU.subtract).then_inc(sem("pq"), 1)
                dve.wait_ge(sem("pqrow_ev"), 8)

                def weigh(i):
                    h, t = i // T, i % T
                    dve.wait_ge(sem("ev"), i + 1)
                    if t == 0 and h >= 2:
                        dve.wait_ge(sem("gat_mm"), h - 1)
                    V.tensor_tensor(EE[0:NP, h % 2, t, :], ev[0:NP, i % 2, :], BT[0:NP, t, :], ALU.mult
                                    ).then_inc(sem("ee"), 1)

                for i in range(HEADS * T):
                    h, t = i // T, i % T
                    link(V.tensor_scalar(t1[0:NP, i % 2, :], qrow[0:NP, h, :], asd[0:NP, 6, t, h:h + 1], None, ALU.add))
                    V.scalar_tensor_tensor(out=vv[0:NP, i % 2, :], in0=prow[0:NP, h, :],
                                           scalar=asd[0:NP, 0, t, h:h + 1], in1=t1[0:NP, i % 2, :],
                                           op0=ALU.add, op1=ALU.max).then_inc(sem("vv"), 1)
                    if i >= 1:
                        weigh(i - 1)
                weigh(HEADS * T - 1)
                dve.wait_ge(sem("gat_mm"), HEADS)
                g5 = ps[0:NP, 6, 0:100].rearrange("p (g c) -> p g c", c=5)
                link(V.tensor_scalar(scr[0:NP, 0, :, 0:4].rearrange("p t h -> p t h"),
                                     ps[0:NP, 6, 0:100].rearrange("p (t h c) -> p t h c", t=T, c=5)[:, :, :, 4],
                                     1e-16, None, ALU.add))
                link(V.reciprocal(asd[0:NP, 3, :, :], scr[0:NP, 0, :, 0:4]))
                agg = scr[0:NP, 1, :, :]
                link(V.tensor_tensor(agg.rearrange("p t c -> p (t c)").rearrange("p (g c) -> p g c", c=4),
                                     g5[:, :, 0:4],
                                     asd[0:NP, 3, :, :].rearrange("p t h -> p (t h)").unsqueeze(2).broadcast_to([NP, 20, 4]),
                                     ALU.mult))

                def wide(i):
                    return gatc[0:NP, i, :].unsqueeze(1).broadcast_to([NP, T, 16])

                def tall(c):
                    return sca[0:NP, c, :].unsqueeze(2).broadcast_to([NP, T, 16])

                link(V.tensor_tensor(agg, agg, wide(2), ALU.add))
                link(V.tensor_reduce(sca[0:NP, 0, :], agg, AX.X, ALU.add))
                link(V.tensor_scalar(sca[0:NP, 0, :], sca[0:NP, 0, :], 1.0 / 16, None, ALU.mult))
                link(V.tensor_tensor(agg, agg, tall(0), ALU.subtract))
                link(V.tensor_tensor(scr[0:NP, 2, :, :], agg, agg, ALU.mult))
                V.tensor_reduce(sca[0:NP, 1, :], scr[0:NP, 2, :, :], AX.X, ALU.add).then_inc(sem("var16"), 1)
                dve.wait_ge(sem("std16"), 1)
                link(V.reciprocal(sca[0:NP, 3, :], sca[0:NP, 2, :]))
                link(V.tensor_tensor(agg, agg, tall(3), ALU.mult))
                link(V.tensor_tensor(agg, agg, wide(3), ALU.mult))
                link(V.tensor_tensor(agg, agg, wide(4), ALU.add))
                link(V.tensor_reduce(scr[0:NP, 0, :, 0:4], agg.rearrange("p t (h c) -> p t c h", c=4), AX.X, ALU.add))
                link(V.tensor_scalar(scr[0:NP, 2, :, 0:4], scr[0:NP, 0, :, 0:4], 0.25, None, ALU.mult))
                top2_gate(scr[0:NP, 2, :, 0:4], X0, 1)
                V.tensor_scalar(sca[0:NP, 12, :], sca[0:NP, 11, :], 1.0, None, ALU.mult).then_inc(sem("gate"), 1)
                for t in range(T):
                    dve.wait_ge(sem("f0_out_mm"), t + 1)
                    i = V.tensor_tensor(x[0:NP, t, :], ps[0:NP, 4 + t % 4, 0:D], x[0:NP, t, :], ALU.add)
                    i.then_inc(sem("f0_out_ev"), 1)
                for e in range(X0):
                    for t in range(T):
                        n = T * (e + 1) + t
                        dve.wait_ge(sem("f0_out_mm"), n + 1)
                        dve.wait_ge(sem("f0_out_ev"), n - T + 1)
                        i = V.scalar_tensor_tensor(out=x[0:NP, t, :], in0=ps[0:NP, 4 + n % 4, 0:D],
                                                   scalar=gate[0:NP, t, e:e + 1], in1=x[0:NP, t, :],
                                                   op0=ALU.mult, op1=ALU.add)
                        i.then_inc(sem("f0_out_ev"), 1)
                last = V.tensor_scalar(sca[0:NP, 13, :], sca[0:NP, 11, :], 1.0, None, ALU.mult)
                dve.wait_ge(sem("f0_out_ev"), T * (X0 + 1))

            if STOP >= 3:
                norm(x)
                dve.wait_ge(sem("ld_g1"), 64)
                add_bias(bc3)
                last = add_rows("g1f_mm")
            if STOP >= 4:
                link(last)
                norm(x)
                link(V.tensor_tensor(x[0:NP, :, :], x[0:NP, :, :], xn[0:NP, :, :], ALU.add))
                for t in range(T):
                    i = V.tensor_scalar(ltmask[0:NP, t, :], iota[0:NP, 0:N], node[0:NP, t:t + 1], None, ALU.is_lt)
                turn()
                dve.wait_ge(sem("wrow_ev"), 2)
                for t in range(T):
                    i = V.tensor_tensor_reduce(out=dtmp[0:NP, t, :], in0=wrow[0:NP, tile(t)], in1=ident[0:NP, 0:NP],
                                               scale=1.0, scalar=0.0, op0=ALU.mult, op1=ALU.add,
                                               accum_out=wcol[0:NP, t:t + 1])
                link(i)
                for t in range(T):
                    i = V.tensor_scalar(wj[0:NP, 0, :], wrow[0:NP, :], wcol[0:NP, t:t + 1], 0.0, ALU.is_gt, ALU.add,
                                        accum_out=rk[0:NP, 0, t:t + 1])
                    link(i)
                    i = V.scalar_tensor_tensor(out=wj[0:NP, 1, :], in0=wrow[0:NP, :], scalar=wcol[0:NP, t:t + 1],
                                               in1=ltmask[0:NP, t, :], op0=ALU.is_equal, op1=ALU.mult,
                                               accum_out=rk[0:NP, 1, t:t + 1])
                    link(i)
                link(V.tensor_tensor(rk[0:NP, 2, :], rk[0:NP, 0, :], rk[0:NP, 1, :], ALU.add))
                link(V.scalar_tensor_tensor(out=rk[0:NP, 3, :], in0=rk[0:NP, 2, :], scalar=float(KEEP1),
                                            in1=wcol[0:NP, :], op0=ALU.is_lt, op1=ALU.mult))
                dve.wait_ge(sem("ld_f1"), 48)
                for t in range(T):
                    dve.wait_ge(sem("f1_out_mm"), t + 1)
                    i = V.tensor_tensor(h2[0:NP, t, :], ps[0:NP, t, 0:D], m2b[0:NP, :], ALU.add)
                link(i)
                for t in range(T):
                    last = V.scalar_tensor_tensor(out=x[0:NP, t, :], in0=h2[0:NP, t, :], scalar=rk[0:NP, 3, t:t + 1],
                                                  in1=x[0:NP, t, :], op0=ALU.mult, op1=ALU.add)

            if STOP >= 5:
                link(last)
                norm(x)
                turn()
                for t in range(T):
                    dve.wait_ge(sem("g2a_mm"), t + 1)
                    V.tensor_tensor(x[0:NP, t, :], ps[0:NP, 3 + t, 0:D], x[0:NP, t, :], ALU.add
                                    ).then_inc(sem("g2a_v"), 1)
                for t in range(T):
                    dve.wait_ge(sem("hn"), t + 1)
                    at = hn[0:NP, t, :]
                    for r in range(MAXK // 8):
                        link(V.max(top8[0:NP, t, r, :], at))
                        to = wk[0:NP, r % 2, t, :]
                        link(V.match_replace(to, top8[0:NP, t, r, :], at, -3e38))
                        at = to
                    V.scalar_tensor_tensor(out=hn[0:NP, t, :], in0=at, scalar=-3e38, in1=hn[0:NP, t, :],
                                           op0=ALU.is_equal, op1=ALU.mult).then_inc(sem("hs"), 1)
                for t in range(T):
                    dve.wait_ge(sem("g2b_mm"), t + 1)
                    last = V.scalar_tensor_tensor(out=x[0:NP, t, :], in0=ps[0:NP, t, 0:D], scalar=rdeg[0:NP, t:t + 1],
                                                  in1=x[0:NP, t, :], op0=ALU.mult, op1=ALU.add)
            if STOP >= 6:
                link(last)
                norm(x)
                turn()
                dve.wait_ge(sem("lg2_mm"), 1)
                dve.wait_ge(sem("ld_s2"), 32)
                lg, ex, oh = scr[0:NP, 0, :, 0:X2], scr[0:NP, 1, :, 0:X2], scr[0:NP, 2, :, 0:X2]

                def each(c):
                    return sca[0:NP, c, :].unsqueeze(2).broadcast_to([NP, T, X2])

                link(V.tensor_tensor(lg, ps[0:NP, 3, 0:T * X2].rearrange("p (t e) -> p t e", t=T),
                                     g2b[0:NP, :].unsqueeze(1).broadcast_to([NP, T, X2]), ALU.add))
                link(V.tensor_reduce(sca[0:NP, 0, :], lg, AX.X, ALU.max))
                V.tensor_tensor(lg, lg, each(0), ALU.subtract).then_inc(sem("l2d"), 1)
                dve.wait_ge(sem("l2e"), 1)
                link(V.tensor_reduce(sca[0:NP, 1, :], ex, AX.X, ALU.add))
                link(V.reciprocal(sca[0:NP, 2, :], sca[0:NP, 1, :]))
                link(V.tensor_tensor(ex, ex, each(2), ALU.mult))
                first_max(ex, X2, oh, sca[0:NP, 3, :], scr[0:NP, 5, :, 0:X2])
                V.tensor_copy(ohb[0:NP, :, :], oh).then_inc(sem("ohb"), 1)
                link(V.tensor_tensor(scr[0:NP, 3, :, 0:X2], oh,
                                     iota[0:NP, 0:SL:CAP].unsqueeze(1).broadcast_to([NP, T, X2]), ALU.mult))
                link(V.tensor_reduce(sca[0:NP, 4, :], scr[0:NP, 3, :, 0:X2], AX.X, ALU.add))
                dve.wait_ge(sem("pos_mm"), 1)
                link(V.tensor_tensor(scr[0:NP, 4, :, 0:X2], ps[0:NP, 4, 0:T * X2].rearrange("p (t e) -> p t e", t=T),
                                     oh, ALU.mult))
                link(V.tensor_reduce(sca[0:NP, 5, :], scr[0:NP, 4, :, 0:X2], AX.X, ALU.add))
                link(V.tensor_scalar(sca[0:NP, 6, :], sca[0:NP, 5, :], float(CAP), None, ALU.is_le))
                V.tensor_tensor(prk[0:NP, :], sca[0:NP, 3, :], sca[0:NP, 6, :], ALU.mult)
                link(V.tensor_tensor(sca[0:NP, 7, :], sca[0:NP, 4, :], sca[0:NP, 5, :], ALU.add))
                link(V.tensor_tensor(sca[0:NP, 8, :], sca[0:NP, 7, :], sca[0:NP, 6, :], ALU.mult))
                link(V.tensor_scalar(slot[0:NP, :], sca[0:NP, 8, :], 1.0, None, ALU.subtract))
                V.tensor_scalar(sca[0:NP, 9, :], sca[0:NP, 8, :], 1.0, None, ALU.subtract).then_inc(sem("slot"), 1)
                for t in range(T):
                    V.tensor_scalar(SC[0:NP, t, :], iota[0:NP, 0:SL], slot[0:NP, t:t + 1], None, ALU.is_equal
                                    ).then_inc(sem("sc"), 1)
                dve.wait_ge(sem("srow_ev"), 2)
                for e in range(X2):
                    V.tensor_scalar(ST[0:CAP, e, :], srow[0:CAP, :], float(e * CAP), node[0:CAP, 0:1],
                                    ALU.subtract, ALU.is_equal).then_inc(sem("st"), 1)
                dve.wait_ge(sem("ld_f2b"), 16 * X2)

                with dve.Fori(0, X2 // 2) as i:
                    for b in range(2):
                        dve.wait_ge(sem("f2_out_mm"), 2 * i + b + 1)
                        V.tensor_tensor(ybuf[0:CAP, bass.ds(2 * i + b, 1), :].rearrange("p a n -> p (a n)"),
                                        ps[0:CAP, 4 + b, 0:D],
                                        f2b2[0:CAP, bass.ds(2 * i + b, 1), :].rearrange("p a n -> p (a n)"), ALU.add
                                        ).then_inc(sem("f2_out_ev"), 1)
                V.memset(cst4[:, 0:1], 1e4)
                V.memset(cst4[:, 1:2], -1e4)
                V.memset(h2[0:NP, :, :], 0.0)
                for t in range(T):
                    dve.wait_ge(sem("comb_mm"), t + 1)
                    i = V.tensor_scalar(xn[0:NP, t, :], ps[0:NP, t, 0:D], prk[0:NP, t:t + 1], None, ALU.mult)
                link(i)
                mi = R1[:, 0:T * D].bitcast(I32).rearrange("p (t n) -> p t n", t=T)[0:NP]
                y = xn[0:NP, :, :]
                link(V.tensor_tensor(mi, y, y, ALU.is_equal))
                link(V.copy_predicated(h2[0:NP, :, :], mi, y))
                for c, (op, lim) in enumerate(((ALU.is_gt, 3.4028234e38), (ALU.is_lt, -3.4028234e38))):
                    link(V.tensor_scalar(mi, y, lim, None, op))
                    link(V.copy_predicated(h2[0:NP, :, :], mi, cst4[0:NP, c:c + 1].unsqueeze(2).broadcast_to([NP, T, D])))
                link(V.tensor_tensor(x[0:NP, :, :], x[0:NP, :, :], h2[0:NP, :, :], ALU.add))
                V.tensor_scalar(sca[0:NP, 9, :], sca[0:NP, 8, :], 1.0, None, ALU.subtract).then_inc(sem("x_l2"), 1)

            if STOP >= 7:
                norm(x)
                dve.wait_ge(sem("ld_g3"), 16)
                dve.wait_ge(sem("ld_s3"), 112)
                for i in range(2):
                    link(V.tensor_tensor(pr3, W3[:, :, 0:D], att3[:, i, :].unsqueeze(1).broadcast_to([128, KD, D]), ALU.mult))
                    for k in range(KD):
                        j = V.tensor_reduce(W3[:, k, D + HEADS * i:D + HEADS * (i + 1)],
                                            pr3[:, k, :].rearrange("p (h c) -> p h c", h=HEADS), AX.X, ALU.add)
                    link(j)
                V.tensor_scalar(sca[0:NP, 9, :], sca[0:NP, 8, :], 1.0, None, ALU.subtract).then_inc(sem("w3"), 1)
                turn()
                dve.wait_ge(sem("ld_rc"), 32)
                link(V.tensor_copy(rcf[0:NP, :, :], rci[0:NP, :, :]))
                for i, g in enumerate((Gc, Gr)):
                    for t in range(T):
                        V.tensor_scalar(g[0:NP, t, :], rcf[0:NP, i, :], node[0:NP, t:t + 1], None, ALU.is_equal
                                        ).then_inc(sem("gcr"), 1)
                for t in range(T):
                    dve.wait_ge(sem("g3b_mm"), t + 1)
                    i = V.tensor_copy(z3[0:NP, 0, t, :], ps[0:NP, t, D:D + HEADS])
                link(i)
                z = z3[0:NP, 0, :, :]

                def each4(c):
                    return sca[0:NP, c, :].unsqueeze(2).broadcast_to([NP, T, HEADS])

                link(V.scalar_tensor_tensor(out=z3[0:NP, 2, :, :], in0=z, scalar=0.01, in1=z, op0=ALU.mult, op1=ALU.max))
                link(V.tensor_reduce(sca[0:NP, 0, :], z3[0:NP, 2, :, :], AX.X, ALU.max))
                V.tensor_tensor(z, z3[0:NP, 2, :, :], each4(0), ALU.subtract).then_inc(sem("a3d"), 1)
                dve.wait_ge(sem("a3e"), 1)
                link(V.tensor_reduce(sca[0:NP, 1, :], z3[0:NP, 1, :, :], AX.X, ALU.add))
                link(V.reciprocal(sca[0:NP, 2, :], sca[0:NP, 1, :]))
                link(V.tensor_tensor(z3[0:NP, 2, :, :], z3[0:NP, 1, :, :], each4(2), ALU.mult))
                for h in range(HEADS):
                    for t in range(T):
                        xs = ps[0:NP, t, h * HD3:(h + 1) * HD3]
                        al = z3[0:NP, 2, t, h:h + 1]
                        if h == 0:
                            i = V.tensor_scalar(tmp3[0:NP, 0, t, :], xs, al, None, ALU.mult)
                        else:
                            i = V.scalar_tensor_tensor(out=tmp3[0:NP, h % 2, t, :], in0=xs, scalar=al,
                                                       in1=tmp3[0:NP, (h + 1) % 2, t, :], op0=ALU.mult, op1=ALU.add)
                    link(i)
                for t in range(T):
                    xv = x[0:NP, t, :].rearrange("p (h c) -> p h c", h=HEADS)
                    last = V.tensor_tensor(xv, xv, tmp3[0:NP, 1, t, :].unsqueeze(1).broadcast_to([NP, HEADS, HD3]), ALU.add)

            if STOP >= 8:
                link(last)
                norm(x)
                turn()
                dve.wait_ge(sem("lg3_mm"), 1)
                lg = scr[0:NP, 2, :, :]
                link(V.tensor_tensor(lg, ps[0:NP, 3, 0:T * X3].rearrange("p (t e) -> p t e", t=T),
                                     g3b[0:NP, :].unsqueeze(1).broadcast_to([NP, T, X3]), ALU.add))
                top2_gate(lg, X3, 2)
                V.tensor_scalar(sca[0:NP, 12, :], sca[0:NP, 11, :], 1.0, None, ALU.mult).then_inc(sem("gate"), 1)
                for t in range(T):
                    dve.wait_ge(sem("f3_bias_mm"), t + 1)
                    V.tensor_tensor(xn[0:NP, t, :], ps[0:NP, 4 + t % 4, 0:D], xn[0:NP, t, :], ALU.add
                                    ).then_inc(sem("f3_out_ev"), 1)

                def f3_sum(e, b):
                    for t in range(T):
                        dve.wait_ge(sem("f3_out_mm"), T * e + t + 1)
                        dve.wait_ge(sem("f3_out_ev"), T * e + t + 1)
                        V.scalar_tensor_tensor(out=xn[0:NP, t, :], in0=ps[0:NP, 4 + (t + T * b + T) % 4, 0:D],
                                               scalar=gate[0:NP, t, bass.ds(e, 1)], in1=xn[0:NP, t, :],
                                               op0=ALU.mult, op1=ALU.add).then_inc(sem("f3_out_ev"), 1)

                with dve.Fori(0, X3 // 4) as i:
                    for b in range(4):
                        f3_sum(4 * i + b, b)
                dve.wait_ge(sem("f3_out_ev"), T * (X3 + 1))
                norm(xn)
                link(V.tensor_scalar(sca[0:NP, 12, :], sca[0:NP, 11, :], 1.0, None, ALU.mult))
                link(V.tensor_tensor(xn[0:NP, :, :], xn[0:NP, :, :], gam[0:NP, :].unsqueeze(1).broadcast_to([NP, T, D]),
                                     ALU.mult))
                V.tensor_tensor(x[0:NP, :, :], x[0:NP, :, :], bet[0:NP, :].unsqueeze(1).broadcast_to([NP, T, D]), ALU.add)
                link(V.tensor_scalar(sca[0:NP, 13, :], sca[0:NP, 11, :], 1.0, None, ALU.mult))
                last = V.tensor_tensor(x[0:NP, :, :], x[0:NP, :, :], xn[0:NP, :, :], ALU.add)
            link(V.tensor_scalar(sca[0:NP, 14, :], dinvc[0:NP, :], 1.0, None, ALU.mult))
            V.tensor_scalar(sca[0:NP, 14, :], dinvc[0:NP, :], 1.0, None, ALU.mult).then_inc(sem("x_final"), 1)


BANKS = [[(2, 2), (3, 3), (4, 4), (0, 0), (1, 1)], [(0, 5), (1, 6), (2, 7), (3, 0), (4, 1)]]
XN_OF_TURN = [1, 3, 4, 5, 6, 7]


_INS = ["x", "src", "dst", "L0_gnn_W1", "L0_gnn_W2", "L0_gnn_b2", "L0_ffn_W_gat", "L0_ffn_att_src", "L0_ffn_att_dst",
        "L0_ffn_b_gat", "L0_ffn_ln_gamma", "L0_ffn_ln_beta", "L0_ffn_b2", "L0_ffn_edge_index", "L1_gnn_W1",
        "L1_gnn_W2", "L1_gnn_W3", "L1_gnn_b3", "L1_ffn_br", "L1_ffn_w1", "L1_ffn_w2", "L1_ffn_b2",
        "L2_gnn_W_self", "L2_gnn_W_neigh", "L2_ffn_gate_w", "L2_ffn_gate_b", "L2_ffn_b2", "L3_gnn_weight",
        "L3_gnn_attn_l", "L3_gnn_attn_r", "L3_ffn_gate_w", "L3_ffn_gate_b", "L3_ffn_b2", "L3_ffn_gamma",
        "L3_ffn_beta"]
_EXPERTS = {"L0_experts": ("L0_ffn_W1", "L0_ffn_W2"), "L2_experts": ("L2_ffn_w1", "L2_ffn_w2"),
            "L3_experts": ("L3_ffn_w1", "L3_ffn_w2")}


def laid_out(np, inputs):
    arrays = {name: np.ascontiguousarray(inputs[name]) for name in _INS}

    def by_partition(w):
        e, k, n = w.shape
        return w.reshape(e, k // 128, 128, n).transpose(0, 2, 1, 3).reshape(e, 128, -1)

    for name, pair in _EXPERTS.items():
        arrays[name] = np.concatenate([by_partition(np.asarray(inputs[w])) for w in pair], axis=2)
    arrays["bias_columns"] = np.ascontiguousarray(
        np.concatenate([np.asarray(inputs[name]).reshape(-1, 128).T for name, _ in BIAS_COLUMNS], axis=1))
    return arrays


def kernel(**inputs):
    import numpy as _np
    import concourse.bacc as _bacc
    from concourse import mybir as _mybir
    from concourse.bass_utils import run_bass_kernel_spmd as _run

    nc = _bacc.Bacc("TRN2", target_bir_lowering=False, num_devices=1)
    arrays, args = {}, {}
    for name, v in laid_out(_np, inputs).items():
        arrays[f"in_{name}"] = v
        args[name] = nc.dram_tensor(f"in_{name}", v.shape, _mybir.dt.from_np(v.dtype), kind="ExternalInput").ap()
    out = nc.dram_tensor("out_x", (N, D), F32, kind="ExternalOutput").ap()
    graph_mlp_stack(nc, args, out)
    r = _run(nc, [arrays], core_ids=[0])
    return r.results[0]["out_x"]
```

```python
from contextlib import ExitStack

import concourse.bass as bass
from concourse import mybir

ALU = mybir.AluOpType
ACT = mybir.ActivationFunctionType
AX = mybir.AxisListType
F32 = mybir.dt.float32
F16 = mybir.dt.float16
BF16 = mybir.dt.bfloat16
I32 = mybir.dt.int32
U32 = mybir.dt.uint32

N = 625
NP = 125
T = 5
D = 256
KD = D // 128
PIECES = [(0, 313), (313, 312)]
BANK = 512
EPS = 1e-5
BIG = 1e30
STOP = 8
BIAS_COLUMNS = [("L0_gnn_b1", 4), ("L0_ffn_b1", 16), ("L1_gnn_b1", 2), ("L1_gnn_b2", 2), ("L1_ffn_b1", 8),
                ("L2_ffn_b1", 64), ("L1_ffn_wr", 2)]


def graph_mlp_stack(nc, a, out):
    E1 = a["src"].shape[0]
    EP1, ET1, EU1 = 125, E1 // 125, 5
    E2 = a["L0_ffn_edge_index"].shape[1]
    EP2, ET2, EU2 = 128, E2 // 128, 4
    HALF, BASE = (N + 1) // 2, 4096

    def groups(tiles, unroll, parts):
        most, left, got = (BASE - 1) // parts // unroll, tiles // unroll, []
        while left:
            got.append(min(most, left))
            left -= got[-1]
        return got
    X0, F0 = 4, 512
    HEADS = 4
    F1 = 1024
    KEEP1 = int(0.5 * N) - 1
    X2, F2 = 8, 1024
    CAP = -(-5 * N // (4 * X2))
    SL = X2 * CAP
    X3, F3 = 16, 512
    OV3 = (2 * N - X3) // 128
    J3 = X3 + OV3
    W3E = KD * F3 + F3 // 128 * D + F3 // 128
    MAXK = 32
    HD3 = 64
    W3C = D + 2 * HEADS

    ctx = ExitStack()
    with ctx:
        def sb(name, shape, dt=F32):
            return ctx.enter_context(nc.sbuf_tensor(name, shape, dt))

        sems = {}

        def sem(name):
            if name not in sems:
                sems[name] = ctx.enter_context(nc.semaphore(name))
            return sems[name]

        ps = ctx.enter_context(nc.psum_tensor("ps", [128, 8, BANK], F32))
        psb = ps[:, :, :].bitcast(BF16)

        iota = sb("iota", [128, SL], F16)
        ident = sb("ident", [128, 128])
        ones = sb("ones", [128, 128])
        identb = sb("identb", [128, 128], BF16)
        onesb = sb("onesb", [128, 128], BF16)
        tri = sb("tri", [128, 128], BF16)
        zerob = sb("zerob", [1, BANK], BF16)
        node = sb("node", [128, T])
        epsc = sb("epsc", [128, 1])
        digc = sb("digc", [128, 1])
        desc = sb("desc", [128, X3])

        R1 = sb("R1", [128, 6250])
        R2 = sb("R2", [128, 12304])
        R3 = sb("R3", [128, 5250])
        RW = sb("RW", [128, 8192])
        AT = sb("AT", [128, T, N])
        AHB = sb("AHB", [128, 2 * T * N])
        Ahat = AHB[:, 0:T * N].rearrange("p (t n) -> p t n", t=T)
        BT = AHB[:, T * N:].rearrange("p (t n) -> p t n", t=T)

        x = sb("x", [128, T, D])
        xn = sb("xn", [128, T, D])
        xnT = sb("xnT", [128, KD, N])
        aggT = sb("aggT", [128, KD, N])
        h2 = sb("h2", [128, T, D])
        gT = aggT[0:X3, 0, :]

        oh_s = R1[:, 0:EU1 * 320].bitcast(BF16).rearrange("p (u n) -> p u n", u=EU1)
        oh_d = R1[:, EU1 * 320:EU1 * 480].bitcast(BF16).rearrange("p (u n) -> p u n", u=EU1)
        sums = R2[:, 0:T * HALF].rearrange("p (t n) -> p t n", t=T)
        highi = R2[:, 1600:1600 + T * HALF].bitcast(I32).rearrange("p (t n) -> p t n", t=T)
        high = R2[:, 3900:3900 + T * HALF].rearrange("p (t n) -> p t n", t=T)
        idi1 = R3[:, 0:2 * ET1].bitcast(I32).rearrange("p (a t) -> p a t", a=2)
        idf1 = R3[:, 2 * ET1:5 * ET1].rearrange("p (a t) -> p a t", a=3)
        o2 = 5 * ET1
        idi2 = R3[:, o2:o2 + 2 * ET2].bitcast(I32).rearrange("p (a t) -> p a t", a=2)
        idf2 = R3[:, o2 + 2 * ET2:o2 + 5 * ET2].rearrange("p (a t) -> p a t", a=3)
        dinvr = R2[:, 3200:3200 + N]
        Bneg = R3[:, 2100:2100 + 1563].bitcast(BF16)[:, 0:T * N].rearrange("p (t n) -> p t n", t=T)
        maskb = R3[:, 3663:3663 + 1563].bitcast(BF16)[:, 0:T * N].rearrange("p (t n) -> p t n", t=T)
        dinvc = sb("dinvc", [128, T])
        rdeg = sb("rdeg", [128, T])
        dtmp = h2[:, :, 0:NP]

        h1T = R1[:, 0:2500].rearrange("p (m n) -> p m n", m=4)
        W01 = R1[:, 3300:3300 + 1024].rearrange("p (k n) -> p k n", k=2)
        W02 = R1[:, 4400:4400 + 1024].rearrange("p (k n) -> p k n", k=4)
        bcols = sb("bcols", [128, sum(n for _, n in BIAS_COLUMNS)])
        bcol, at0 = {}, 0
        for name, n in BIAS_COLUMNS:
            bcol[name] = bcols[:, at0:at0 + n]
            at0 += n
        b01 = bcol["L0_gnn_b1"]
        b02 = sb("b02", [128, D])

        Wg = sb("Wg", [128, KD, 16])
        gatc = sb("gatc", [128, 5, 16])
        hg = sb("hg", [128, T, 16])
        haug = sb("haug", [128, T, HEADS, 5])
        prod = sb("prod", [128, T, 16])
        asd = sb("asd", [128, 7, T, HEADS])
        prow = R2[:, 0:2500].rearrange("p (h n) -> p h n", h=HEADS)
        qrow = R2[:, 2500:5000].rearrange("p (h n) -> p h n", h=HEADS)
        EE = R2[:, 5000:11250].rearrange("p (b t n) -> p b t n", b=2, t=T)
        arow = R2[:, 5000:7500].rearrange("p (h n) -> p h n", h=HEADS)
        junk = R3[:, 3700:3700 + 2 * N].rearrange("p (b n) -> p b n", b=2)
        t1 = R3[:, 0:2 * N].rearrange("p (b n) -> p b n", b=2)
        vv = R3[:, 2 * N:4 * N].rearrange("p (b n) -> p b n", b=2)
        ev = R3[:, 4 * N:6 * N].rearrange("p (b n) -> p b n", b=2)
        scr = sb("scr", [128, 7, T, 16])
        sca = sb("sca", [128, 16, T])
        FWs = [RW[:, e * 2048:(e + 1) * 2048] for e in range(X0)]
        FW1 = [w[:, 0:1024].rearrange("p (k n) -> p k n", k=KD) for w in FWs]
        FW2 = [w[:, 1024:2048].rearrange("p (k n) -> p k n", k=4) for w in FWs]
        f0b1 = bcol["L0_ffn_b1"]
        f0b2 = sb("f0b2", [X0, D])
        hh = R1[:, 0:5000].rearrange("p (b m n) -> p b m n", b=2, m=4)
        gate = sb("gate", [128, T, X3])

        Wc = sb("Wc", [128, 3, KD, D])
        bc12 = [bcol["L1_gnn_b1"], bcol["L1_gnn_b2"]]
        bc3 = sb("bc3", [128, D])
        M1 = RW[:, 0:2048].rearrange("p (k n) -> p k n", k=KD)
        M2 = RW[:, 2048:4096].rearrange("p (k n) -> p k n", k=8)
        m1b = bcol["L1_ffn_b1"]
        m2b = RW[:, 7696:7696 + D]
        wr = bcol["L1_ffn_wr"]
        br = sb("br", [128, 1])
        ltmask = AHB[:, T * N:T * N + 1563].bitcast(BF16)[:, 0:T * N].rearrange("p (t n) -> p t n", t=T)
        wrow = R3[:, 0:N]
        wj = R3[:, N:3 * N].rearrange("p (b n) -> p b n", b=2)
        hT = R1[:, 0:5000].rearrange("p (m n) -> p m n", m=8)
        wcol = sb("wcol", [128, T])
        rk = sb("rk", [128, 4, T])

        Wsn = RW[:, 4096:5120].rearrange("p (k n) -> p k n", k=KD)
        hn = R3[:, 0:1280].rearrange("p (t n) -> p t n", t=T)
        wk = R3[:, 1280:3840].rearrange("p (b t n) -> p b t n", b=2, t=T)
        top8 = sb("top8", [128, T, 4, 8])
        G2 = sb("G2", [128, KD, X2])
        g2b = sb("g2b", [128, X2])
        f2b1 = bcol["L2_ffn_b1"]
        f2b2 = RW[:, 5120:7168].rearrange("p (e n) -> p e n", e=X2)
        ohb = sb("ohb", [128, T, X2], BF16)
        slot = sb("slot", [128, T])
        prk = sb("prk", [128, T])
        SC = R1[:, 0:T * SL].rearrange("p (t s) -> p t s", t=T)
        ST = AHB[:, 0:X2 * N].rearrange("p (e n) -> p e n", e=X2)
        srow = AHB[:, X2 * N:(X2 + 1) * N]
        XbT = R3[:, 0:KD * SL].rearrange("p (k s) -> p k s", k=KD)
        hTe = R3[:, 1568:1568 + 1568].rearrange("p (b m s) -> p b m s", b=2, m=8)
        ybuf = R3[:, 3136:3136 + 2048].rearrange("p (e n) -> p e n", e=X2)
        F2W = R2[:, 0:8192].rearrange("p (b n) -> p b n", b=2)
        F2W1 = [F2W[:, b, 0:2048].rearrange("p (k n) -> p k n", k=KD) for b in range(2)]
        F2W2 = [F2W[:, b, 2048:4096].rearrange("p (k n) -> p k n", k=8) for b in range(2)]
        cst4 = sb("cst4", [128, 2])
        bnow = sb("bnow", [128, 4, 8])

        W3 = RW[:, 7168:7168 + KD * W3C].rearrange("p (k n) -> p k n", k=KD)
        att3 = Wc[:, 0, :, :]
        pr3 = h2[:, 0:2, :]
        Gc = R1[:, 0:T * N].rearrange("p (t n) -> p t n", t=T)
        Gr = R1[:, T * N:2 * T * N].rearrange("p (t n) -> p t n", t=T)
        rci = RW[:, 0:2 * N].bitcast(I32).rearrange("p (a n) -> p a n", a=2)
        rcf = RW[:, 2 * N:4 * N].rearrange("p (a n) -> p a n", a=2)
        xt = R3[:, 0:T * W3C].rearrange("p (t n) -> p t n", t=T)
        z3 = sb("z3", [128, 3, T, HEADS])
        tmp3 = aggT[:, :, 0:T * HD3].rearrange("p b (t c) -> p b t c", t=T)
        G3 = sb("G3", [128, KD, X3])
        g3b = sb("g3b", [128, X3])
        f3b2 = Wc[0:X3, 2, 0, :]
        gam = Wc[:, 1, 0, :]
        bet = Wc[:, 1, 1, :]
        F3W = R2[:, 4096:4096 + 4 * W3E].rearrange("p (b n) -> p b n", b=4)
        F3W1 = [F3W[:, b, 0:1024].rearrange("p (k n) -> p k n", k=KD) for b in range(4)]
        F3W2 = [F3W[:, b, 1024:2048].rearrange("p (k n) -> p k n", k=4) for b in range(4)]
        F3B1 = [F3W[:, b, 2048:2052] for b in range(4)]
        xg = R1[:, 0:1024].rearrange("p (b n) -> p b n", b=4)
        xgT = R1[:, 1024:1536].rearrange("p (b k n) -> p b k n", b=2, k=KD)
        hx = R1[:, 1536:2560].rearrange("p (b m n) -> p b m n", b=2, m=4)
        yo = R1[:, 2560:3584].rearrange("p (b n) -> p b n", b=4)
        yg = R3[:, 0:2 * T * D].rearrange("p (t c n) -> p t c n", t=T, c=2)
        oh3 = R3[:, 2560:2560 + 2 * T * X3].rearrange("p (c t e) -> p c t e", c=2, t=T)
        rank3 = R3[:, 2720:2800].rearrange("p (t e) -> p t e", t=T)
        place3 = R3[:, 2800:2880].rearrange("p (t e) -> p t e", t=T)
        ohp3 = R3[:, 2880:3040].rearrange("p (c t e) -> p c t e", c=2, t=T)
        more3 = R3[:, 3040:3104].rearrange("p (e j) -> p e j", j=4)
        less3 = R3[:, 3104:3360].rearrange("p (e f) -> p e f", e=X3)
        e3 = R3[:, 3360:3360 + 5 * X3].rearrange("p (i e) -> p i e", i=5)
        below3 = R3[:, 3440:3440 + OV3 * X3].rearrange("p (k e) -> p k e", k=OV3)
        idf3 = R3[:, 3600:3600 + OV3]
        m3b = sb("m3b", [128, T, X3], BF16)
        row3 = sb("row3", [128, 2, T], U32)
        id3 = sb("id3", [128, OV3], U32)
        rows3 = nc.dram_tensor("slot_rows", (J3 * 128, D), F32, kind="Internal").ap()
        outs3 = nc.dram_tensor("slot_outputs", (J3 * 128, D), F32, kind="Internal").ap()

        st = sb("st", [128, T, 6])
        mv = sb("mv", [128, T, 2])
        sd = sb("sd", [128, T])
        rs = sb("rs", [128, T])

        def row(name, n):
            return a[name].rearrange("(a n) -> a n", a=1).broadcast_to([n, a[name].shape[0]])

        def kpn(ap):
            return ap.rearrange("(k p) n -> p k n", p=128)

        def tile(t):
            return slice(t * NP, (t + 1) * NP)

        block = ctx.enter_context(nc.Block())

        @block.sync
        def _(sp):
            def load(dst, src, s):
                if STOP < {"ld_gat": 2, "ld_f0": 2, "ld_g1": 3, "ld_s1": 4, "ld_s2": 6, "ld_s3": 7, "ld_f1": 4, "ld_g2": 5, "ld_f2b": 6, "ld_g3": 7}.get(s, 0):
                    return
                sp.dma_start(dst, src).then_inc(sem(s), 16)

            for i, name in enumerate(("src", "dst")):
                load(idi1[0:EP1, i, :], a[name].rearrange("(p t) -> p t", p=EP1), "ld_edges1")
            load(x[0:NP, :, :], a["x"].rearrange("(t p) n -> p t n", p=NP), "ld_x")
            for i in range(2):
                load(idi2[0:EP2, i, :], a["L0_ffn_edge_index"][i, :].rearrange("(p t) -> p t", p=EP2), "ld_edges2")
            load(W01, kpn(a["L0_gnn_W1"]), "ld_g0")
            load(W02, kpn(a["L0_gnn_W2"]), "ld_g0")
            load(b02[0:NP, :], row("L0_gnn_b2", NP), "ld_g0")
            load(bcols[:, :], a["bias_columns"], "ld_g0")
            if STOP >= 8:
                sp.wait_ge(sem("zeros"), 1)
                for t in range(T):
                    sp.dma_start(rows3.rearrange("(p c r) n -> p c (r n)", p=128, c=T)[:, t, :],
                                 h2[:, :, :].rearrange("p t n -> p (t n)")).then_inc(sem("zeroed"), 16)
            load(Wg[:, :, :], kpn(a["L0_ffn_W_gat"]), "ld_gat")
            for i, name in enumerate(("L0_ffn_att_src", "L0_ffn_att_dst")):
                load(gatc[0:NP, i, :], a[name].rearrange("h (a e) -> a (h e)", a=1).broadcast_to([NP, 16]), "ld_gat")
            for i, name in enumerate(("L0_ffn_b_gat", "L0_ffn_ln_gamma", "L0_ffn_ln_beta")):
                load(gatc[0:NP, 2 + i, :], row(name, NP), "ld_gat")
            for e in range(X0):
                load(RW[:, e * 2048:(e + 1) * 2048], a["L0_experts"][e], "ld_f0")
            load(f0b2[:, :], a["L0_ffn_b2"], "ld_f0")
            for i in range(3):
                load(Wc[:, i, :, :], kpn(a[f"L1_gnn_W{i + 1}"]), "ld_g1")
            load(bc3[0:NP, :], row("L1_gnn_b3", NP), "ld_g1")
            load(br[0:NP, :], row("L1_ffn_br", NP), "ld_g1")
            load(G2[:, :, :], kpn(a["L2_ffn_gate_w"]), "ld_s2")
            load(g2b[0:NP, :], row("L2_ffn_gate_b", NP), "ld_s2")
            load(G3[:, :, :], kpn(a["L3_ffn_gate_w"]), "ld_s3")
            load(g3b[0:NP, :], row("L3_ffn_gate_b", NP), "ld_s3")
            if STOP >= 3:
                sp.wait_ge(sem("f0_out_mm"), T * (X0 + 1))
                load(m2b[0:NP, :], row("L1_ffn_b2", NP), "ld_f1")
                load(M1, kpn(a["L1_ffn_w1"]), "ld_f1")
                load(M2, kpn(a["L1_ffn_w2"]), "ld_f1")
                load(Wsn[:, :, 0:D], kpn(a["L2_gnn_W_self"]), "ld_late")
                load(Wsn[:, :, D:2 * D], kpn(a["L2_gnn_W_neigh"]), "ld_late")
                for e in range(X2):
                    load(f2b2[0:CAP, e, :], a["L2_ffn_b2"][e:e + 1, :].broadcast_to([CAP, D]), "ld_late")
                load(W3[:, :, 0:D], kpn(a["L3_gnn_weight"]), "ld_late")

            def f2_load(e, b, half):
                c = slice(half * KD * F2, (half + 1) * KD * F2)
                load(F2W[:, b, c], e("L2_experts")[:, c], f"ld_f2w{b}{half}")

            def f3_load(e, b):
                load(F3W[:, b, :], e("L3_experts"), f"ld_f3w{b}")

            def of(e):
                return lambda name: a[name][e]

            def at(e):
                return lambda name: a[name][bass.ds(e, 1)].rearrange("a p n -> (a p) n")

            if STOP >= 7:
                sp.wait_ge(sem("g1e_mm"), T)
                for i, name in enumerate(("L3_gnn_attn_r", "L3_gnn_attn_l")):
                    load(att3[:, i, :], a[name].rearrange("h (a e) -> a (h e)", a=1).broadcast_to([128, D]), "ld_s3")
                load(f3b2[:, :], a["L3_ffn_b2"], "ld_s3")
                load(gam[0:NP, :], row("L3_ffn_gamma", NP), "ld_s3")
                load(bet[0:NP, :], row("L3_ffn_beta", NP), "ld_s3")
            if STOP >= 6:
                for e in range(2):
                    for half in range(2):
                        f2_load(of(e), e, half)
            if STOP >= 8:
                f3_load(of(2), 2)
                f3_load(of(3), 3)
            if STOP >= 6:
                with sp.Fori(1, X2 // 2) as i:
                    for b in range(2):
                        sp.wait_ge(sem("f2_hid_mm"), 4 * i + 2 * b - 2)
                        f2_load(at(2 * i + b), b, 0)
                        sp.wait_ge(sem("f2_out_mm"), 2 * i + b - 1)
                        f2_load(at(2 * i + b), b, 1)
            if STOP >= 8:
                sp.wait_ge(sem("f2_out_mm"), X2)
                f3_load(of(0), 0)
                f3_load(of(1), 1)
                sp.wait_ge(sem("scattered"), 16 * 2 * T)

                def slot3(ap, j):
                    return ap.rearrange("(j p) n -> j p n", p=128)[bass.ds(j, 1)].rearrange("a p n -> (a p) n")

                def f3_slot(j, b):
                    if isinstance(j, int):
                        if j + 4 < J3:
                            sp.wait_ge(sem("xg_mm"), j + 1)
                            sp.dma_start(xg[:, b, :], rows3[(j + 4) * 128:(j + 5) * 128, :]).then_inc(sem(f"ld_xg{b}"), 16)
                        if j + 4 < X3:
                            sp.wait_ge(sem("f3_out_mm"), j + 1)
                            f3_load(of(j + 4), b)
                        sp.wait_ge(sem("f3_out_ev"), T + j + 1)
                        sp.dma_start(outs3[j * 128:(j + 1) * 128, :], yo[:, b, :]).then_inc(sem(f"st_y{b}"), 16)
                        return
                    sp.wait_ge(sem("xg_mm"), j + 1)
                    sp.dma_start(xg[:, b, :], slot3(rows3, j + 4)).then_inc(sem(f"ld_xg{b}"), 16)
                    sp.wait_ge(sem("f3_out_mm"), j + 1)
                    f3_load(at(j + 4), b)
                    sp.wait_ge(sem("f3_out_ev"), j + T + 1)
                    sp.dma_start(slot3(outs3, j), yo[:, b, :]).then_inc(sem(f"st_y{b}"), 16)

                for b in range(4):
                    sp.dma_start(xg[:, b, :], rows3[b * 128:(b + 1) * 128, :]).then_inc(sem(f"ld_xg{b}"), 16)
                with sp.Fori(0, X3 // 4 - 1) as i:
                    for b in range(4):
                        f3_slot(4 * i + b, b)
                for j in range(X3 - 4, J3):
                    f3_slot(j, j % 4)
            sp.wait_ge(sem("x_final"), 1)
            sp.dma_start(out.rearrange("(t p) n -> p t n", p=NP), x[0:NP, :, :]).then_inc(sem("stored"), 16)
            sp.wait_ge(sem("stored"), 16)

        @block.gpsimd
        def _(pool):
            pool.iota(iota[:, :], pattern=[[1, SL]], base=0, channel_multiplier=0,
                      allow_small_or_imprecise_dtypes=True).then_inc(sem("c_iota"), 1)
            pool.iota(node[:, :], pattern=[[NP, T]], base=0, channel_multiplier=1,
                      allow_small_or_imprecise_dtypes=True).then_inc(sem("c_iota"), 1)
            pool.iota(desc[:, :], pattern=[[-1, X3]], base=X3, channel_multiplier=0,
                      allow_small_or_imprecise_dtypes=True).then_inc(sem("c_iota"), 1)
            pool.memset(ones[:, :], 1.0).then_inc(sem("c_set"), 1)
            pool.memset(onesb[:, :], 1.0).then_inc(sem("c_set"), 1)
            pool.memset(zerob[:, :], 0.0).then_inc(sem("c_set"), 1)
            pool.memset(epsc[:, :], EPS).then_inc(sem("c_set"), 1)
            pool.memset(haug[:, :, :, 4:5], 1.0).then_inc(sem("c_set"), 1)
            pool.memset(digc[:, :], -0.5 * (BASE - 1) / BASE).then_inc(sem("c_set"), 1)
            pool.memset(AHB[:, T * N:], 0.0).then_inc(sem("c_set"), 1)
            pool.memset(AT[:, :, :], 0.0).then_inc(sem("c_set"), 1)
            pool.memset(h2[:, :, :], 0.0).then_inc(sem("zeros"), 1)

            def add_high(tag, C, tiles, unroll, parts):
                for g, _ in enumerate(groups(tiles, unroll, parts)):
                    pool.wait_ge(sem(f"high{tag}"), g + 1)
                    nc.gpsimd.tensor_tensor(C[0:NP, :, HALF:N], C[0:NP, :, HALF:N], high[0:NP, :, 0:N - HALF], ALU.add
                                            ).then_inc(sem(f"counted_high{tag}"), 1)

            pool.wait_ge(sem("c_set"), 8)
            add_high("1", AT, ET1, EU1, EP1)
            if STOP >= 2:
                add_high("2", BT, ET2, EU2, EP2)
            if STOP >= 7:
                pool.wait_ge(sem("f1_out_mm"), T)
                for i, name in enumerate(("dst", "src")):
                    pool.dma_start(rci[0:NP, i, :], a[name][0:N].rearrange("(a n) -> a n", a=1).broadcast_to([NP, N])
                                   ).then_inc(sem("ld_rc"), 16)
            if STOP >= 8:
                pool.wait_ge(sem("zeroed"), 16 * T)
                pool.wait_ge(sem("row3"), 1)
                for t in range(T):
                    for c in range(2):
                        pool.indirect_dma_start(out=rows3, out_offset=bass.IndirectOffsetOnAxis(ap=row3[0:NP, c, t:t + 1], axis=0),
                                                in_=xn[0:NP, t, :], in_offset=None).then_inc(sem("scattered"), 16)
                pool.wait_ge(sem("id3"), 1)
                weights = a["L3_experts"].rearrange("e p n -> (e p) n")
                for k in range(OV3):
                    j, b = X3 + k, (X3 + k) % 4
                    pool.wait_ge(sem("f3_out_mm"), j - 3)
                    pool.indirect_dma_start(out=F3W[:, b, :], out_offset=None, in_=weights,
                                            in_offset=bass.IndirectOffsetOnAxis(ap=id3[:, k:k + 1], axis=0)
                                            ).then_inc(sem(f"ld_more{b}"), 16)
                for b in range(4):
                    pool.wait_ge(sem(f"st_y{b}"), 16 * len(range(b, J3, 4)))
                for t in range(T):
                    for c in range(2):
                        pool.indirect_dma_start(out=yg[0:NP, t, c, :], out_offset=None, in_=outs3,
                                                in_offset=bass.IndirectOffsetOnAxis(ap=row3[0:NP, c, t:t + 1], axis=0)
                                                ).then_inc(sem("ld_yg"), 16)

        @block.tensor
        def _(pe):
            def mm(o, l, r, k, last, **kw):
                return nc.tensor.matmul(o, l, r, start=(k == 0), stop=last, **kw)

            def count_edges(tag, tiles, unroll, parts):
                first_tile = 0
                for g, iters in enumerate(groups(tiles, unroll, parts)):
                    pe_order = BANKS[g % 2]

                    def body(i, fresh):
                        for j in range(unroll):
                            pe.wait_ge(sem(f"oh_ready{tag}"), 2 * (i * unroll + j) + 2 * first_tile + 2)
                            for k, (m, b) in enumerate(pe_order):
                                start = fresh and j == 0
                                if start and g and k == 0:
                                    pe.wait_ge(sem(f"flushed{tag}"), T * (g - 1))
                                if start and g and k == 3:
                                    pe.wait_ge(sem(f"flushed{tag}"), T * (g - 1) + 2)
                                last = nc.tensor.matmul(ps[:, b, 0:HALF], oh_s[0:parts, j, m * NP:m * NP + 128],
                                                        oh_d[0:parts, j, 0:HALF], start=start, stop=False,
                                                        skip_group_check=True)
                            last.then_inc(sem(f"oh_free{tag}"), 1)
                        return last

                    body(0, True)
                    if iters > 1:
                        with pe.Fori(1, iters) as i:
                            body(i, False)
                    for m, b in pe_order:
                        last = nc.tensor.matmul(ps[:, b, 0:2], zerob[0:1, 0:128], zerob[0:1, 0:2], start=False,
                                                stop=True, skip_group_check=True)
                    last.then_inc(sem(f"count_mm{tag}"), 1)
                    first_tile += iters * unroll

            turned = [0]

            def turn():
                n = turned[0]
                turned[0] += 1
                for t in range(T):
                    pe.wait_ge(sem("xn"), T * XN_OF_TURN[n] + t + 1)
                    for k in range(KD):
                        o = ps[:, k, t * NP:(t + 1) * NP] if t < 4 else ps[:, 2, k * NP:(k + 1) * NP]
                        last = nc.tensor.transpose(o, xn[0:NP, t, k * 128:(k + 1) * 128], ident[0:NP, 0:NP])
                    if t >= 3:
                        last.then_inc(sem("turn_mm"), 1)
                pe.wait_ge(sem("turn_a"), 2 * n + 2)
                pe.wait_ge(sem("turn_v"), n + 1)

            def agg_cols(rhs_rows, s, b0=0):
                for m in range(KD):
                    for q, (c, n) in enumerate(PIECES):
                        for t in range(T):
                            last = mm(ps[:, b0 + 2 * m + q, 0:n], rhs_rows[0:NP, t, m * 128:(m + 1) * 128],
                                      Ahat[0:NP, t, c:c + n], t, t == T - 1)
                        last.then_inc(sem(s), 1)

            def agg_rows(A, rhs_rows, s, b0=0):
                for t in range(T):
                    for k in range(T):
                        last = mm(ps[0:NP, b0 + t, 0:D], A[0:NP, k, tile(t)], rhs_rows[0:NP, k, :], k, k == T - 1)
                    last.then_inc(sem(s), 1)

            def lin_cols(W, XT, K, M, s, ring=8, b0=0, wait=None, n0=0):
                for m in range(M):
                    for q, (c, n) in enumerate(PIECES):
                        u = n0 + 2 * m + q
                        if wait and u >= ring:
                            pe.wait_ge(sem(wait), u - ring + 1)
                        for k in range(K):
                            last = mm(ps[:, b0 + u % ring, 0:n], W[:, k, m * 128:(m + 1) * 128], XT[:, k, c:c + n],
                                      k, k == K - 1)
                        last.then_inc(sem(s), 1)

            def lin_rows(XT, W, K, n, s, b0=0, ring=8, wait=None, n0=0):
                for t in range(T):
                    u = n0 + t
                    if wait and u >= ring:
                        pe.wait_ge(sem(wait), u - ring + 1)
                    for k in range(K):
                        last = mm(ps[0:NP, b0 + u % ring, 0:n], XT[:, k, tile(t)], W[:, k, 0:n], k, k == K - 1)
                    last.then_inc(sem(s), 1)

            pe.wait_ge(sem("c_set"), 8)
            pe.wait_ge(sem("c_mat"), 3)
            count_edges("1", ET1, EU1, EP1)
            pe.wait_ge(sem("counted1"), 1)
            pe.wait_ge(sem("counted_high1"), len(groups(ET1, EU1, EP1)))
            pe.wait_ge(sem("flushed1"), T * len(groups(ET1, EU1, EP1)))
            for q, (c, n) in enumerate(PIECES):
                for t in range(T):
                    mm(ps[0:NP, q, 0:n], ones[0:NP, 0:NP], AT[0:NP, t, c:c + n], t, t == T - 1)
            for d in range(T):
                for t in range(T):
                    last = mm(ps[0:NP, 2, d:d + 1], AT[0:NP, t, tile(d)], ones[0:NP, 0:1], t, t == T - 1)
            last.then_inc(sem("deg_mm"), 1)
            if STOP >= 2:
                pe.wait_ge(sem("deg_v"), 1)
                count_edges("2", ET2, EU2, EP2)
                pe.wait_ge(sem("flushed2"), T * len(groups(ET2, EU2, EP2)))

            pe.wait_ge(sem("xn"), T)
            pe.wait_ge(sem("ahat"), 1)
            agg_cols(xn, "g0a_mm")
            pe.wait_ge(sem("g0a_ev"), 4)
            pe.wait_ge(sem("ld_g0"), 64)
            lin_cols(W01, aggT, KD, 4, "g0b_mm")
            pe.wait_ge(sem("g0b_ev"), 8)
            lin_rows(h1T, W02, 4, D, "g0c_mm")
            pe.wait_ge(sem("g0c_ev"), T)

            def turn_mask(ds):
                for d in ds:
                    for t in range(T):
                        last = nc.tensor.transpose(psb[0:NP, 5 + d % 3, t * (NP + 1):t * (NP + 1) + NP],
                                                   maskb[0:NP, t, tile(d)], identb[0:NP, 0:NP])
                last.then_inc(sem("mask_mm"), 1)

            pe.wait_ge(sem("maskb"), T)
            turn_mask((0, 1, 2))
            agg_rows(Ahat, h2, "g0d_mm")
            pe.wait_ge(sem("bneg"), 2)
            turn_mask((3, 4))

            def row_of(c4, h, t):
                o = ps[0:NP, 2 * h, tile(t)] if t < 4 else ps[0:NP, 2 * h + 1, 0:NP]
                return nc.tensor.matmul(o, c4[0:NP, t, h:h + 1].broadcast_to([NP, NP]), ident[0:NP, 0:NP],
                                        start=True, stop=True)

            if STOP >= 2:
                turn()
                pe.wait_ge(sem("ld_gat"), 96)
                for t in range(T):
                    for k in range(KD):
                        last = mm(ps[0:NP, 3, t * 16:(t + 1) * 16], xnT[:, k, tile(t)], Wg[:, k, :], k, k == KD - 1)
                last.then_inc(sem("gat_h_mm"), 1)
                pe.wait_ge(sem("asd"), 1)
                for h in range(HEADS):
                    for t in range(T):
                        last = row_of(asd[:, 0, :, :], h, t)
                    last.then_inc(sem("arow_mm"), 1)
                pe.wait_ge(sem("arow_ev"), HEADS)
                pe.wait_ge(sem("ld_f0"), 80)
                for e in range(2):
                    lin_cols(FW1[e], xnT, KD, 4, "f0_hid_mm", ring=4, wait="f0_hid_ev", n0=8 * e)
                pe.wait_ge(sem("f0_hid_ev"), 16)
                pe.wait_ge(sem("pq"), 1)
                for i in range(2):
                    for h in range(HEADS):
                        if i:
                            pe.wait_ge(sem("pqrow_ev"), h + 1)
                        for t in range(T):
                            last = row_of(asd[:, 4 + i, :, :], h, t)
                        last.then_inc(sem("pqrow_mm"), 1)
                pe.wait_ge(sem("pqrow_ev"), 8)
                for h in range(HEADS):
                    pe.wait_ge(sem("ee"), T * (h + 1))
                    for d in range(T):
                        for t in range(T):
                            last = mm(ps[0:NP, 6, d * 20 + h * 5:d * 20 + h * 5 + 5], EE[0:NP, h % 2, t, tile(d)],
                                      haug[0:NP, t, h, :], t, t == T - 1)
                    last.then_inc(sem("gat_mm"), 1)
                pe.wait_ge(sem("gate"), 1)
                for t in range(T):
                    last = nc.tensor.transpose(ps[0:X0, t // 4, (t % 4) * NP:(t % 4 + 1) * NP], gate[0:NP, t, 0:X0],
                                               ident[0:NP, 0:NP])
                last.then_inc(sem("gT_mm"), 1)
                pe.wait_ge(sem("gT_ev"), 2)
                pe.wait_ge(sem("ld_f0"), 80)
                for t in range(T):
                    if t == 4:
                        pe.wait_ge(sem("f0_out_ev"), 1)
                    nc.tensor.matmul(ps[0:NP, 4 + t % 4, 0:D], gT[0:X0, tile(t)], f0b2[:, :], start=True, stop=True
                                     ).then_inc(sem("f0_out_mm"), 1)
                for e in range(X0 + 1):
                    if 2 <= e < X0:
                        lin_cols(FW1[e], xnT, KD, 4, "f0_hid_mm", ring=4, wait="f0_hid_ev", n0=8 * e)
                    if e >= 1:
                        pe.wait_ge(sem("f0_hid_ev"), 8 * e)
                        lin_rows(hh[:, (e - 1) % 2, :, :], FW2[e - 1], 4, D, "f0_out_mm", b0=4, ring=4,
                                 wait="f0_out_ev", n0=T * e)

            if STOP >= 3:
                pe.wait_ge(sem("xn"), 3 * T)
                agg_cols(xn, "g1a_mm")
                pe.wait_ge(sem("ld_g1"), 80)
                pe.wait_ge(sem("g1a_ev"), 4)
                lin_cols(Wc[:, 0, :, :], aggT, KD, 2, "g1b_mm", b0=4, ring=4)
                pe.wait_ge(sem("g1b_ev"), 4)
                lin_rows(h1T, Wc[:, 1, :, :], KD, D, "g1c_mm")
                pe.wait_ge(sem("g1c_ev"), T)
                agg_cols(h2, "g1d_mm")
                pe.wait_ge(sem("g1d_ev"), 4)
                lin_rows(aggT, Wc[:, 2, :, :], KD, D, "g1e_mm")
                pe.wait_ge(sem("g1e_ev"), T)
                agg_rows(Ahat, h2, "g1f_mm")

            if STOP >= 4:
                turn()
                pe.wait_ge(sem("ld_g1"), 80)
                for q, (c, n) in enumerate(PIECES):
                    for k in range(KD):
                        last = mm(ps[0:NP, 4 + q, 0:n], wr[:, k:k + 1].broadcast_to([128, NP]), xnT[:, k, c:c + n],
                                  k, k == KD - 1)
                last.then_inc(sem("wrow_mm"), 1)
                pe.wait_ge(sem("ld_f1"), 48)
                lin_cols(M1, xnT, KD, 8, "f1_hid_mm", ring=4, wait="f1_hid_ev")
                pe.wait_ge(sem("f1_hid_ev"), 16)
                pe.wait_ge(sem("wrow_ev"), 2)
                lin_rows(hT, M2, 8, D, "f1_out_mm")

            if STOP >= 5:
                turn()
                pe.wait_ge(sem("ld_late"), 16 * (3 + X2))
                lin_rows(xnT, Wsn, KD, 2 * D, "g2a_mm", b0=3, ring=5)
                pe.wait_ge(sem("hn"), T)
                for s in range(T):
                    pe.wait_ge(sem("hs"), s + 1)
                    for t in range(T):
                        last = mm(ps[0:NP, t, 0:D], AT[0:NP, s, tile(t)], hn[0:NP, s, :], s, s == T - 1)
                        if s == T - 1:
                            last.then_inc(sem("g2b_mm"), 1)

            if STOP >= 6:
                turn()
                pe.wait_ge(sem("ld_s2"), 32)
                for t in range(T):
                    for k in range(KD):
                        last = mm(ps[0:NP, 3, t * X2:(t + 1) * X2], xnT[:, k, tile(t)], G2[:, k, :], k, k == KD - 1)
                last.then_inc(sem("lg2_mm"), 1)
                pe.wait_ge(sem("ohb"), 1)
                for t in range(T):
                    for s in range(t + 1):
                        last = mm(ps[0:NP, 4, t * X2:(t + 1) * X2], (tri if s == t else onesb)[0:NP, 0:NP],
                                  ohb[0:NP, s, :], s, s == t)
                last.then_inc(sem("pos_mm"), 1)
                pe.wait_ge(sem("slot"), 1)
                for t in range(T):
                    o = ps[0:NP, 5, tile(t)] if t < 4 else ps[0:NP, 6, 0:NP]
                    last = nc.tensor.matmul(o, slot[0:NP, t:t + 1].broadcast_to([NP, NP]), ident[0:NP, 0:NP],
                                            start=True, stop=True)
                last.then_inc(sem("srow_mm"), 1)
                pe.wait_ge(sem("sc"), T)
                for m in range(KD):
                    for q in range(2):
                        for t in range(T):
                            last = mm(ps[:, 2 * m + q, 0:SL // 2], xn[0:NP, t, m * 128:(m + 1) * 128],
                                      SC[0:NP, t, q * (SL // 2):(q + 1) * (SL // 2)], t, t == T - 1)
                        last.then_inc(sem("disp_mm"), 1)
                pe.wait_ge(sem("disp_ev"), 4)
                pe.wait_ge(sem("srow_ev"), 2)

                def f2_hid(e, b):
                    pe.wait_ge(sem(f"ld_f2w{b}0"), 8 * (e - b) + 16)
                    for m in range(8):
                        for k in range(KD):
                            last = mm(ps[:, 2 * b + m // 4, (m % 4) * CAP:(m % 4 + 1) * CAP],
                                      F2W1[b][:, k, m * 128:(m + 1) * 128], XbT[:, k, bass.ds(e * CAP, CAP)],
                                      k, k == KD - 1)
                        if m % 4 == 3:
                            last.then_inc(sem("f2_hid_mm"), 1)

                def f2_out(e, b):
                    pe.wait_ge(sem(f"ld_f2w{b}1"), 8 * (e - b) + 16)
                    pe.wait_ge(sem("f2_hid_ev"), 8 * e + 8)
                    for k in range(8):
                        last = mm(ps[0:CAP, 4 + b, 0:D], hTe[:, b, k, :], F2W2[b][:, k, :], k, k == 7)
                    last.then_inc(sem("f2_out_mm"), 1)

                f2_hid(0, 0)
                f2_hid(1, 1)
                f2_out(0, 0)
                with pe.Fori(1, X2 // 2) as i:
                    f2_hid(2 * i, 0)
                    pe.wait_ge(sem("f2_out_ev"), 2 * i - 1)
                    f2_out(2 * i - 1, 1)
                    f2_hid(2 * i + 1, 1)
                    pe.wait_ge(sem("f2_out_ev"), 2 * i)
                    f2_out(2 * i, 0)
                f2_out(X2 - 1, 1)
                pe.wait_ge(sem("f2_out_ev"), X2)
                pe.wait_ge(sem("st"), X2)
                for t in range(T):
                    for e in range(X2):
                        last = mm(ps[0:NP, t, 0:D], ST[0:CAP, e, tile(t)], ybuf[0:CAP, e, :], e, e == X2 - 1)
                    last.then_inc(sem("comb_mm"), 1)

            if STOP >= 7:
                turn()
                pe.wait_ge(sem("w3"), 1)
                lin_rows(xnT, W3, KD, W3C, "g3a_mm", b0=3, ring=5)
                pe.wait_ge(sem("g3a_ev"), T)
                pe.wait_ge(sem("gcr"), 2 * T)
                for t in range(T):
                    for s in range(T):
                        mm(ps[0:NP, t, 0:D + HEADS], Gc[0:NP, s, tile(t)], xt[0:NP, s, 0:D + HEADS], s, s == T - 1,
                           skip_group_check=True)
                    for s in range(T):
                        last = nc.tensor.matmul(ps[0:NP, t, D:D + HEADS], Gr[0:NP, s, tile(t)], xt[0:NP, s, D + HEADS:W3C],
                                                start=False, stop=(s == T - 1), skip_group_check=True)
                    last.then_inc(sem("g3b_mm"), 1)

            if STOP >= 8:
                turn()
                pe.wait_ge(sem("ld_s3"), 112)
                for t in range(T):
                    for k in range(KD):
                        last = mm(ps[0:NP, 3, t * X3:(t + 1) * X3], xnT[:, k, tile(t)], G3[:, k, :], k, k == KD - 1)
                last.then_inc(sem("lg3_mm"), 1)
                pe.wait_ge(sem("m3b"), 1)
                for t in range(T):
                    for s in range(t + 1):
                        mm(ps[:, 4, t * X3:(t + 1) * X3], (tri if s == t else onesb)[0:NP, :], m3b[0:NP, s, :], s, s == t)
                for s in range(T):
                    last = mm(ps[:, 4, 128:128 + X3], onesb[0:NP, :], m3b[0:NP, s, :], s, s == T - 1)
                last.then_inc(sem("rank_mm"), 1)
                pe.wait_ge(sem("gate"), 2)
                for t in range(T):
                    last = nc.tensor.transpose(ps[0:X3, t // 4, (t % 4) * NP:(t % 4 + 1) * NP], gate[0:NP, t, :],
                                               ident[0:NP, 0:NP])
                last.then_inc(sem("gT_mm"), 1)
                pe.wait_ge(sem("gT_ev"), 4)
                for t in range(T):
                    last = nc.tensor.matmul(ps[0:NP, 5 + t // 2, (t % 2) * D:(t % 2 + 1) * D], gT[:, tile(t)],
                                            f3b2[:, :], start=True, stop=True)
                last.then_inc(sem("f3_bias_mm"), 1)

                def f3_rows(j, s, b):
                    pe.wait_ge(sem(f"ld_xg{b}"), 4 * (j - b) + 16)
                    if not (isinstance(j, int) and j < 2):
                        pe.wait_ge(sem("xgT_ev"), j - 1)
                    for k in range(KD):
                        last = nc.tensor.transpose(ps[:, s, k * 128:(k + 1) * 128], xg[:, b, k * 128:(k + 1) * 128],
                                                   ident[:, :])
                    last.then_inc(sem("xg_mm"), 1)

                def f3_hid(j, s, b, first):
                    if first:
                        pe.wait_ge(sem(f"ld_f3w{b}"), 4 * (j - b) + 16)
                    else:
                        pe.wait_ge(sem(f"ld_more{b}"), 4 * (j - b) + (16 - 4 * X3))
                    pe.wait_ge(sem("xgT_ev"), j + 1)
                    if not (isinstance(j, int) and j < 2):
                        pe.wait_ge(sem("f3_hid_ev"), 4 * j - 4)
                    for m in range(4):
                        for k in range(KD):
                            last = mm(ps[:, 2 + 4 * s + m // 2, (m % 2) * 128:(m % 2 + 1) * 128], F3W1[b][:, k, m * 128:(m + 1) * 128],
                                      xgT[:, s, k, :], k, k == KD - 1)
                        if m % 2:
                            last.then_inc(sem("f3_hid_mm"), 1)

                def f3_out(j, s, b):
                    pe.wait_ge(sem("f3_out_ev"), j + T - 1)
                    for k in range(4):
                        pe.wait_ge(sem("f3_hid_ev"), 4 * j + k + 1)
                        last = mm(ps[:, 4 + s, 0:D], hx[:, s, k, :], F3W2[b][:, k, :], k, k == 3)
                    last.then_inc(sem("f3_out_mm"), 1)

                def f3_step(j, b, first):
                    if not isinstance(j, int) or j + 1 < J3:
                        f3_rows(j + 1, (b + 1) % 2, (b + 1) % 4)
                    f3_hid(j, b % 2, b, first)
                    if not isinstance(j, int) or j:
                        f3_out(j - 1, (b + 1) % 2, (b + 3) % 4)

                pe.wait_ge(sem("f3_out_ev"), T)
                f3_rows(0, 0, 0)
                for j in range(4):
                    f3_step(j, j, True)
                with pe.Fori(1, X3 // 4) as i:
                    for b in range(4):
                        f3_step(4 * i + b, b, True)
                with pe.Fori(X3 // 4, J3 // 4) as i:
                    for b in range(4):
                        f3_step(4 * i + b, b, False)
                for j in range(J3 // 4 * 4, J3):
                    f3_step(j, j % 4, False)
                f3_out(J3 - 1, (J3 - 1) % 2, (J3 - 1) % 4)


        @block.scalar
        def _(act):
            def std(n):
                act.wait_ge(sem("ln_var"), n + 1)
                nc.scalar.activation(sd[0:NP, :], mv[0:NP, :, 1], ACT.Sqrt, bias=epsc[0:NP, :]).then_inc(sem("ln_std"), 1)

            turned = [0]

            def turn():
                n = turned[0]
                turned[0] += 1
                act.wait_ge(sem("turn_mm"), 2 * n + 1)
                nc.scalar.copy(xnT[:, 0, 0:4 * NP], ps[:, 0, 0:4 * NP]).then_inc(sem("turn_a"), 1)
                act.wait_ge(sem("turn_mm"), 2 * n + 2)
                nc.scalar.copy(xnT[:, :, 4 * NP:N], ps[:, 2, 0:2 * NP].rearrange("p (k n) -> p k n", k=2)
                               ).then_inc(sem("turn_a"), 1)

            def flush(tag, tiles, unroll, parts):
                for g, _ in enumerate(groups(tiles, unroll, parts)):
                    act.wait_ge(sem(f"count_mm{tag}"), g + 1)
                    if g:
                        act.wait_ge(sem(f"sums_used{tag}"), g)
                        act.wait_ge(sem(f"counted_high{tag}"), g)
                    for m, b in sorted(BANKS[g % 2], key=lambda mb: mb[1]):
                        nc.scalar.copy(sums[0:NP, m, :], ps[0:NP, b, 0:HALF]).then_inc(sem(f"flushed{tag}"), 1)
                    act.wait_ge(sem(f"flushed{tag}"), T * (g + 1))
                    nc.scalar.activation(highi[0:NP, :, :], sums[0:NP, :, :], ACT.Identity, scale=1.0 / BASE,
                                         bias=digc[0:NP, :]).then_inc(sem(f"rounded{tag}"), 1)
                    act.wait_ge(sem(f"rounded{tag}"), g + 1)
                    nc.scalar.copy(high[0:NP, :, :], highi[0:NP, :, :]).then_inc(sem(f"high{tag}"), 1)

            act.wait_ge(sem("c_set"), 8)
            flush("1", ET1, EU1, EP1)
            std(0)
            act.wait_ge(sem("deg1"), 1)
            nc.scalar.activation(dinvr[0:NP, :], dinvr[0:NP, :], ACT.Sqrt).then_inc(sem("deg_sqrt"), 1)
            nc.scalar.activation(dinvc[0:NP, :], dinvc[0:NP, :], ACT.Sqrt).then_inc(sem("deg_sqrt"), 1)
            if STOP >= 2:
                flush("2", ET2, EU2, EP2)

            def drain_cols(mm_sem, ev_sem, dst, func=ACT.Copy, bias=None, M=KD, b0=0):
                for m in range(M):
                    for q, (c, n) in enumerate(PIECES):
                        act.wait_ge(sem(mm_sem), 2 * m + q + 1)
                        kw = {} if bias is None else {"bias": bias[:, m:m + 1]}
                        nc.scalar.activation(dst[:, m, c:c + n], ps[:, b0 + 2 * m + q, 0:n], func, **kw
                                             ).then_inc(sem(ev_sem), 1)

            def drain_rows(mm_sem, ev_sem, dst, w, b0=0):
                for t in range(T):
                    act.wait_ge(sem(mm_sem), t + 1)
                    nc.scalar.copy(dst[0:NP, t, 0:w], ps[0:NP, b0 + t, 0:w]).then_inc(sem(ev_sem), 1)

            drain_cols("g0a_mm", "g0a_ev", aggT)
            act.wait_ge(sem("ld_g0"), 64)
            drain_cols("g0b_mm", "g0b_ev", h1T, ACT.Relu, b01, M=4)
            drain_rows("g0c_mm", "g0c_ev", h2, D)

            if STOP >= 2:
                std(1)
                turn()
                for h in range(HEADS):
                    act.wait_ge(sem("arow_mm"), h + 1)
                    nc.scalar.copy(arow[0:NP, h, 0:4 * NP], ps[0:NP, 2 * h, 0:4 * NP])
                    nc.scalar.copy(arow[0:NP, h, 4 * NP:N], ps[0:NP, 2 * h + 1, 0:NP]).then_inc(sem("arow_ev"), 1)

                def f0_drain(e):
                    for m in range(4):
                        for q, (c, n) in enumerate(PIECES):
                            u = 8 * e + 2 * m + q
                            act.wait_ge(sem("f0_hid_mm"), u + 1)
                            nc.scalar.activation(hh[:, e % 2, m, c:c + n], ps[:, u % 4, 0:n], ACT.Gelu,
                                                 bias=f0b1[:, 4 * e + m:4 * e + m + 1]).then_inc(sem("f0_hid_ev"), 1)

                act.wait_ge(sem("ld_f0"), 80)
                f0_drain(0)
                f0_drain(1)
                for i, r in enumerate((prow, qrow)):
                    for h in range(HEADS):
                        act.wait_ge(sem("pqrow_mm"), 4 * i + h + 1)
                        nc.scalar.copy(r[0:NP, h, 0:4 * NP], ps[0:NP, 2 * h, 0:4 * NP])
                        nc.scalar.copy(r[0:NP, h, 4 * NP:N], ps[0:NP, 2 * h + 1, 0:NP]).then_inc(sem("pqrow_ev"), 1)
                for i in range(HEADS * T):
                    act.wait_ge(sem("vv"), i + 1)
                    if i >= 2:
                        act.wait_ge(sem("ee"), i - 1)
                    nc.scalar.activation(ev[0:NP, i % 2, :], vv[0:NP, i % 2, :], ACT.Exp).then_inc(sem("ev"), 1)
                act.wait_ge(sem("var16"), 1)
                nc.scalar.activation(sca[0:NP, 2, :], sca[0:NP, 1, :], ACT.Sqrt, scale=1.0 / 16, bias=epsc[0:NP, :]
                                     ).then_inc(sem("std16"), 1)
                act.wait_ge(sem("to_exp"), 1)
                nc.scalar.activation(sca[0:NP, 8, :], sca[0:NP, 7, :], ACT.Exp).then_inc(sem("exped"), 1)
                act.wait_ge(sem("gT_mm"), 1)
                nc.scalar.copy(gT[0:X0, 0:4 * NP], ps[0:X0, 0, 0:4 * NP]).then_inc(sem("gT_ev"), 1)
                nc.scalar.copy(gT[0:X0, 4 * NP:N], ps[0:X0, 1, 0:NP]).then_inc(sem("gT_ev"), 1)
                for e in range(2, X0):
                    act.wait_ge(sem("f0_out_mm"), T * e)
                    f0_drain(e)

            if STOP >= 3:
                std(2)
                drain_cols("g1a_mm", "g1a_ev", aggT)
                act.wait_ge(sem("ld_g1"), 80)
                drain_cols("g1b_mm", "g1b_ev", h1T, ACT.Gelu_apprx_tanh, bc12[0], b0=4)
                drain_rows("g1c_mm", "g1c_ev", h2, D)
                drain_cols("g1d_mm", "g1d_ev", aggT, ACT.Gelu_apprx_tanh, bc12[1])
                drain_rows("g1e_mm", "g1e_ev", h2, D)
            if STOP >= 4:
                std(3)
                turn()
                act.wait_ge(sem("wrow_mm"), 1)
                act.wait_ge(sem("ld_g1"), 80)
                for q, (c, n) in enumerate(PIECES):
                    nc.scalar.activation(wrow[0:NP, c:c + n], ps[0:NP, 4 + q, 0:n], ACT.Identity, bias=br[0:NP, :]
                                         ).then_inc(sem("wrow_ev"), 1)
                for m in range(8):
                    for q, (c, n) in enumerate(PIECES):
                        u = 2 * m + q
                        act.wait_ge(sem("f1_hid_mm"), u + 1)
                        nc.scalar.activation(hT[:, m, c:c + n], ps[:, u % 4, 0:n], ACT.Gelu_apprx_tanh,
                                             bias=m1b[:, m:m + 1]).then_inc(sem("f1_hid_ev"), 1)
            if STOP >= 5:
                std(4)
                turn()
                for t in range(T):
                    act.wait_ge(sem("g2a_v"), t + 1)
                    nc.scalar.copy(hn[0:NP, t, :], ps[0:NP, 3 + t, D:2 * D]).then_inc(sem("hn"), 1)
            if STOP >= 6:
                std(5)
                turn()
                act.wait_ge(sem("to_exp"), 2)
                nc.scalar.activation(scr[0:NP, 1, :, 0:X2], scr[0:NP, 0, :, 0:X2], ACT.Exp).then_inc(sem("exped"), 1)
                act.wait_ge(sem("srow_mm"), 1)
                nc.scalar.copy(srow[0:NP, 0:4 * NP], ps[0:NP, 5, 0:4 * NP]).then_inc(sem("srow_ev"), 1)
                nc.scalar.copy(srow[0:NP, 4 * NP:N], ps[0:NP, 6, 0:NP]).then_inc(sem("srow_ev"), 1)
                for u in range(4):
                    act.wait_ge(sem("disp_mm"), u + 1)
                    nc.scalar.copy(XbT[:, u // 2, (u % 2) * (SL // 2):(u % 2 + 1) * (SL // 2)], ps[:, u, 0:SL // 2]
                                   ).then_inc(sem("disp_ev"), 1)
                act.wait_ge(sem("ld_s2"), 32)

                def f2_drain(e, b, first):
                    nc.scalar.copy(bnow[:, b, :], f2b1[:, bass.ds(8 * e, 8)]).then_inc(sem("f2_bias"), 1)
                    act.wait_ge(sem("f2_bias"), e + 1)
                    if not first:
                        act.wait_ge(sem("f2_out_mm"), e - 1)
                    for m in range(8):
                        if m % 4 == 0:
                            act.wait_ge(sem("f2_hid_mm"), 2 * e + m // 4 + 1)
                        nc.scalar.activation(hTe[:, b, m, :], ps[:, 2 * b + m // 4, (m % 4) * CAP:(m % 4 + 1) * CAP],
                                             ACT.Relu, bias=bnow[:, b, m:m + 1]).then_inc(sem("f2_hid_ev"), 1)

                for b in range(2):
                    f2_drain(b, b, True)
                with act.Fori(1, X2 // 2) as i:
                    for b in range(2):
                        f2_drain(2 * i + b, b, False)
            if STOP >= 7:
                std(6)
                turn()
                drain_rows("g3a_mm", "g3a_ev", xt, W3C, b0=3)
                act.wait_ge(sem("to_exp"), 3)
                nc.scalar.activation(z3[0:NP, 1, :, :], z3[0:NP, 0, :, :], ACT.Exp).then_inc(sem("exped"), 1)
            if STOP >= 8:
                std(7)
                turn()
                act.wait_ge(sem("to_exp"), 4)
                nc.scalar.activation(sca[0:NP, 8, :], sca[0:NP, 7, :], ACT.Exp).then_inc(sem("exped"), 1)
                act.wait_ge(sem("gT_mm"), 2)
                nc.scalar.copy(gT[0:X3, 0:4 * NP], ps[0:X3, 0, 0:4 * NP]).then_inc(sem("gT_ev"), 1)
                nc.scalar.copy(gT[0:X3, 4 * NP:N], ps[0:X3, 1, 0:NP]).then_inc(sem("gT_ev"), 1)

                def f3_drain(j, b):
                    if not (isinstance(j, int) and j < 2):
                        act.wait_ge(sem("f3_out_mm"), j - 1)
                    for m in range(4):
                        if m % 2 == 0:
                            act.wait_ge(sem("f3_hid_mm"), 2 * j + m // 2 + 1)
                        nc.scalar.activation(hx[:, b % 2, m, :],
                                             ps[:, 2 + 4 * (b % 2) + m // 2, (m % 2) * 128:(m % 2 + 1) * 128], ACT.Relu,
                                             bias=F3B1[b][:, m:m + 1]).then_inc(sem("f3_hid_ev"), 1)

                for j in range(4):
                    f3_drain(j, j)
                with act.Fori(1, J3 // 4) as i:
                    for b in range(4):
                        f3_drain(4 * i + b, b)
                for j in range(J3 // 4 * 4, J3):
                    f3_drain(j, j % 4)
                std(8)

        @block.vector
        def _(dve):
            V = nc.vector
            chain = [0]

            def link(ins):
                chain[0] += 1
                ins.then_inc(sem("dve_chain"), 1)
                dve.wait_ge(sem("dve_chain"), chain[0])

            norms = [0]

            def norm(src):
                n = norms[0]
                norms[0] += 1
                for t in range(T):
                    i = V.bn_stats(st[0:NP, t, :], src[0:NP, t, :])
                link(i)
                for t in range(T):
                    i = V.bn_aggr(mv[0:NP, t, :], st[0:NP, t, :])
                i.then_inc(sem("ln_var"), 1)
                dve.wait_ge(sem("ln_std"), n + 1)
                link(V.reciprocal(rs[0:NP, :], sd[0:NP, :]))
                for t in range(T):
                    V.tensor_scalar(xn[0:NP, t, :], src[0:NP, t, :], mv[0:NP, t, 0:1], rs[0:NP, t:t + 1],
                                    ALU.subtract, ALU.mult).then_inc(sem("xn"), 1)
                dve.wait_ge(sem("xn"), T * (n + 1))

            turned = [0]

            def turn():
                n = turned[0]
                turned[0] += 1
                dve.wait_ge(sem("turn_mm"), 2 * n + 1)
                V.tensor_copy(xnT[:, 1, 0:4 * NP], ps[:, 1, 0:4 * NP]).then_inc(sem("turn_v"), 1)

            def digits(parts, idf, idi):
                d, w = idf[0:parts, 1, :], idf[0:parts, 2, :]
                link(V.tensor_copy(d, idi[0:parts, 1, :]))
                link(V.tensor_scalar(w, d, float(HALF), float(BASE - 1), ALU.is_ge, ALU.mult))
                link(V.tensor_scalar(w, w, 1.0, None, ALU.add))
                link(V.scalar_tensor_tensor(out=w, in0=d, scalar=float(N), in1=w, op0=ALU.is_lt, op1=ALU.mult))
                h = sums[0:parts, 0, 0:idf.shape[2]]
                link(V.tensor_scalar(h, d, float(HALF), float(-HALF), ALU.is_ge, ALU.mult))
                link(V.tensor_tensor(d, d, h, ALU.add))

            def one_hots(tag, C, tiles, unroll, parts, idf):
                first_tile = 0

                def part(k, g):
                    if k == 0:
                        dve.wait_ge(sem(f"high{tag}"), g + 1)
                        link(V.scalar_tensor_tensor(out=sums[0:NP, :, :], in0=high[0:NP, :, :], scalar=float(-BASE),
                                                    in1=sums[0:NP, :, :], op0=ALU.mult, op1=ALU.add))
                    else:
                        V.tensor_tensor(C[0:NP, :, 0:HALF], C[0:NP, :, 0:HALF], sums[0:NP, :, :], ALU.add
                                        ).then_inc(sem(f"sums_used{tag}"), 1)

                for g, iters in enumerate(groups(tiles, unroll, parts)):
                    def body(i, fresh):
                        for j in range(unroll):
                            if not fresh:
                                dve.wait_ge(sem(f"oh_free{tag}"), i * unroll + (first_tile + j + 1 - unroll))
                            V.tensor_scalar(oh_s[0:parts, j, 0:N + 3], iota[0:parts, 0:N + 3],
                                            idf[0:parts, 0, bass.ds(i * unroll + (first_tile + j), 1)], None,
                                            ALU.is_equal).then_inc(sem(f"oh_ready{tag}"), 1)
                            V.tensor_scalar(oh_d[0:parts, j, 0:HALF], iota[0:parts, 0:HALF],
                                            idf[0:parts, 1, bass.ds(i * unroll + (first_tile + j), 1)],
                                            idf[0:parts, 2, bass.ds(i * unroll + (first_tile + j), 1)],
                                            ALU.is_equal, ALU.mult).then_inc(sem(f"oh_ready{tag}"), 1)

                    cuts = sorted({0, 1, min(4, iters), min(5, iters), iters})
                    for lo, hi in zip(cuts, cuts[1:]):
                        if lo == 0:
                            body(0, g == 0)
                        else:
                            with dve.Fori(lo, hi) as i:
                                body(i, False)
                        if g and hi == min(4, iters):
                            part(0, g - 1)
                        if g and hi == min(5, iters):
                            part(1, g - 1)
                    first_tile += iters * unroll
                part(0, g)
                part(1, g)
                dve.wait_ge(sem(f"sums_used{tag}"), g + 1)
                dve.wait_ge(sem(f"counted_high{tag}"), g + 1)

            def first_max(vals, E, oh, top, tmp):
                link(V.tensor_reduce(top, vals, AX.X, ALU.max))
                link(V.tensor_tensor(tmp, vals, top.unsqueeze(2).broadcast_to([NP, T, E]), ALU.is_equal))
                link(V.tensor_tensor(tmp, tmp, desc[0:NP, 0:E].unsqueeze(1).broadcast_to([NP, T, E]), ALU.mult))
                link(V.tensor_reduce(sca[0:NP, 15, :], tmp, AX.X, ALU.max))
                link(V.tensor_tensor(oh, tmp, sca[0:NP, 15, :].unsqueeze(2).broadcast_to([NP, T, E]), ALU.is_equal))

            def top2_gate(vals, E, n, chosen=None):
                oh1, oh2, tmp = (scr[0:NP, i, :, 0:E] for i in (3, 4, 5))
                first_max(vals, E, oh1, sca[0:NP, 5, :], tmp)
                link(V.scalar_tensor_tensor(out=scr[0:NP, 6, :, 0:E], in0=oh1, scalar=-3e38, in1=vals,
                                            op0=ALU.mult, op1=ALU.add))
                first_max(scr[0:NP, 6, :, 0:E], E, oh2, sca[0:NP, 6, :], tmp)
                if chosen is not None:
                    V.tensor_tensor(m3b[0:NP, :, :], oh1, oh2, ALU.add).then_inc(sem("m3b"), 1)
                    V.tensor_copy(chosen[:, 0, :, :], oh1)
                    V.tensor_copy(chosen[:, 1, :, :], oh2)
                V.tensor_tensor(sca[0:NP, 7, :], sca[0:NP, 6, :], sca[0:NP, 5, :], ALU.subtract).then_inc(sem("to_exp"), 1)
                dve.wait_ge(sem("exped"), n)
                link(V.tensor_scalar(sca[0:NP, 9, :], sca[0:NP, 8, :], 1.0, None, ALU.add))
                link(V.reciprocal(sca[0:NP, 10, :], sca[0:NP, 9, :]))
                link(V.tensor_tensor(sca[0:NP, 11, :], sca[0:NP, 8, :], sca[0:NP, 10, :], ALU.mult))
                V.tensor_tensor(oh1, oh1, sca[0:NP, 10, :].unsqueeze(2).broadcast_to([NP, T, E]), ALU.mult)
                link(V.tensor_tensor(oh2, oh2, sca[0:NP, 11, :].unsqueeze(2).broadcast_to([NP, T, E]), ALU.mult))
                link(V.tensor_tensor(gate[0:NP, :, 0:E], oh1, oh2, ALU.add))

            dve.wait_ge(sem("c_iota"), 3)
            V.tensor_scalar(ident[:, :], iota[:, 0:128], node[:, 0:1], None, ALU.is_equal).then_inc(sem("c_mat"), 1)
            V.tensor_scalar(identb[:, :], iota[:, 0:128], node[:, 0:1], None, ALU.is_equal).then_inc(sem("c_mat"), 1)
            V.tensor_scalar(tri[:, :], iota[:, 0:128], node[:, 0:1], None, ALU.is_ge).then_inc(sem("c_mat"), 1)
            dve.wait_ge(sem("ld_edges1"), 32)
            link(V.tensor_copy(idf1[0:EP1, 0, :], idi1[0:EP1, 0, :]))
            digits(EP1, idf1, idi1)
            dve.wait_ge(sem("c_set"), 8)
            one_hots("1", AT, ET1, EU1, EP1, idf1)
            V.memset(sca[0:NP, 13, :], 0.0).then_inc(sem("counted1"), 1)
            dve.wait_ge(sem("ld_x"), 16)
            dve.wait_ge(sem("c_set"), 8)
            norm(x)
            dve.wait_ge(sem("ld_edges2"), 32)
            digits(EP2, idf2, idi2)
            link(V.tensor_scalar(idf2[0:EP2, 0, :], idi2[0:EP2, 0, :], float(N - 1), None, ALU.min))
            if STOP >= 8:
                dve.wait_ge(sem("zeroed"), 16 * T)
            dve.wait_ge(sem("deg_mm"), 1)
            for q, (c, n) in enumerate(PIECES):
                V.tensor_scalar(dinvr[0:NP, c:c + n], ps[0:NP, q, 0:n], 1.0, 1.0, ALU.add, ALU.max)
            link(V.tensor_scalar(rdeg[0:NP, :], ps[0:NP, 2, 0:T], 1.0, None, ALU.max))
            V.tensor_scalar(dinvc[0:NP, :], ps[0:NP, 2, 0:T], 1.0, 1.0, ALU.add, ALU.max).then_inc(sem("deg1"), 1)
            link(V.reciprocal(rdeg[0:NP, :], rdeg[0:NP, :]))
            dve.wait_ge(sem("deg_sqrt"), 2)
            V.reciprocal(dinvc[0:NP, :], dinvc[0:NP, :])
            link(V.reciprocal(dinvr[0:NP, :], dinvr[0:NP, :]))
            for t in range(T):
                V.scalar_tensor_tensor(out=Ahat[0:NP, t, :], in0=AT[0:NP, t, :], scalar=dinvc[0:NP, t:t + 1],
                                       in1=dinvr[0:NP, :], op0=ALU.mult, op1=ALU.mult)
                i = V.scalar_tensor_tensor(out=dtmp[0:NP, t, :], in0=ident[0:NP, 0:NP], scalar=dinvc[0:NP, t:t + 1],
                                           in1=dinvr[0:NP, tile(t)], op0=ALU.mult, op1=ALU.mult)
            link(i)
            for t in range(T):
                i = V.tensor_tensor(Ahat[0:NP, t, tile(t)], Ahat[0:NP, t, tile(t)], dtmp[0:NP, t, :], ALU.add)
            i.then_inc(sem("ahat"), 1)
            i = V.tensor_scalar(sca[0:NP, 0, :], dinvc[0:NP, :], 1.0, None, ALU.mult)
            i.then_inc(sem("deg_v"), 1)
            if STOP >= 2:
                one_hots("2", BT, ET2, EU2, EP2, idf2)
                for t in range(T):
                    i = V.tensor_tensor(BT[0:NP, t, tile(t)], BT[0:NP, t, tile(t)], ident[0:NP, 0:NP], ALU.add)
                link(i)
                for t in range(T):
                    V.tensor_scalar(maskb[0:NP, t, :], BT[0:NP, t, :], 1.0, None, ALU.min).then_inc(sem("maskb"), 1)

            def mask(ts):
                for t in ts:
                    V.tensor_scalar(Bneg[0:NP, t, :].rearrange("p (s c) -> p s c", c=NP),
                                    psb[0:NP, 5 + t % 3, 0:T * (NP + 1)].rearrange("p (s c) -> p s c", c=NP + 1)[:, :, 0:NP],
                                    1.0, BIG, ALU.subtract, ALU.mult).then_inc(sem("bneg"), 1)

            dve.wait_ge(sem("mask_mm"), 1)
            mask((0, 1, 2))

            def add_rows(mm_sem, b0=0, bank=lambda t: t):
                for t in range(T):
                    dve.wait_ge(sem(mm_sem), t + 1)
                    i = V.tensor_tensor(x[0:NP, t, :], ps[0:NP, b0 + bank(t), 0:D], x[0:NP, t, :], ALU.add)
                return i

            def add_bias(b):
                link(V.tensor_tensor(x[0:NP, :, :], x[0:NP, :, :], b[0:NP, :].unsqueeze(1).broadcast_to([NP, T, D]),
                                     ALU.add))

            dve.wait_ge(sem("ld_g0"), 64)
            add_bias(b02)
            last = add_rows("g0d_mm")

            if STOP >= 2:
                link(last)
                norm(x)
                turn()
                dve.wait_ge(sem("mask_mm"), 2)
                mask((3, 4))
                dve.wait_ge(sem("gat_h_mm"), 1)
                dve.wait_ge(sem("ld_gat"), 96)
                V.tensor_copy(haug[0:NP, :, :, 0:4], ps[0:NP, 3, 0:80].rearrange("p (t h c) -> p t h c", t=T, h=HEADS))
                link(V.tensor_copy(hg[0:NP, :, :].rearrange("p t c -> p (t c)"), ps[0:NP, 3, 0:80]))
                for i in range(2):
                    link(V.tensor_tensor(prod[0:NP, :, :], hg[0:NP, :, :],
                                         gatc[0:NP, i, :].unsqueeze(1).broadcast_to([NP, T, 16]), ALU.mult))
                    link(V.tensor_reduce(asd[0:NP, i, :, :].rearrange("p t h -> p (t h)"),
                                         prod[0:NP, :, :].rearrange("p t (h c) -> p (t h) c", c=4), AX.X, ALU.add))
                V.tensor_scalar(asd[0:NP, 6, :, :], asd[0:NP, 0, :, :], 0.2, None, ALU.mult).then_inc(sem("asd"), 1)
                dve.wait_ge(sem("bneg"), T)
                n = 0
                for h in range(HEADS):
                    dve.wait_ge(sem("arow_ev"), h + 1)
                    for t in range(T):
                        link(V.tensor_tensor_reduce(out=junk[0:NP, n % 2, :], in0=Bneg[0:NP, t, :], in1=arow[0:NP, h, :],
                                                    scale=1.0, scalar=-3e38, op0=ALU.add, op1=ALU.max,
                                                    accum_out=asd[0:NP, 2, t, h:h + 1]))
                        n += 1
                link(V.tensor_tensor(asd[0:NP, 2, :, :], asd[0:NP, 2, :, :], asd[0:NP, 1, :, :], ALU.add))
                link(V.scalar_tensor_tensor(out=asd[0:NP, 3, :, :], in0=asd[0:NP, 2, :, :], scalar=0.2,
                                            in1=asd[0:NP, 2, :, :], op0=ALU.mult, op1=ALU.max))
                V.tensor_tensor(asd[0:NP, 4, :, :], asd[0:NP, 1, :, :], asd[0:NP, 3, :, :], ALU.subtract)
                V.scalar_tensor_tensor(out=asd[0:NP, 5, :, :], in0=asd[0:NP, 1, :, :], scalar=0.2,
                                       in1=asd[0:NP, 3, :, :], op0=ALU.mult, op1=ALU.subtract).then_inc(sem("pq"), 1)
                dve.wait_ge(sem("pqrow_ev"), 8)

                def weigh(i):
                    h, t = i // T, i % T
                    dve.wait_ge(sem("ev"), i + 1)
                    if t == 0 and h >= 2:
                        dve.wait_ge(sem("gat_mm"), h - 1)
                    V.tensor_tensor(EE[0:NP, h % 2, t, :], ev[0:NP, i % 2, :], BT[0:NP, t, :], ALU.mult
                                    ).then_inc(sem("ee"), 1)

                for i in range(HEADS * T):
                    h, t = i // T, i % T
                    link(V.tensor_scalar(t1[0:NP, i % 2, :], qrow[0:NP, h, :], asd[0:NP, 6, t, h:h + 1], None, ALU.add))
                    V.scalar_tensor_tensor(out=vv[0:NP, i % 2, :], in0=prow[0:NP, h, :],
                                           scalar=asd[0:NP, 0, t, h:h + 1], in1=t1[0:NP, i % 2, :],
                                           op0=ALU.add, op1=ALU.max).then_inc(sem("vv"), 1)
                    if i >= 1:
                        weigh(i - 1)
                weigh(HEADS * T - 1)
                dve.wait_ge(sem("gat_mm"), HEADS)
                g5 = ps[0:NP, 6, 0:100].rearrange("p (g c) -> p g c", c=5)
                link(V.tensor_scalar(scr[0:NP, 0, :, 0:4].rearrange("p t h -> p t h"),
                                     ps[0:NP, 6, 0:100].rearrange("p (t h c) -> p t h c", t=T, c=5)[:, :, :, 4],
                                     1e-16, None, ALU.add))
                link(V.reciprocal(asd[0:NP, 3, :, :], scr[0:NP, 0, :, 0:4]))
                agg = scr[0:NP, 1, :, :]
                link(V.tensor_tensor(agg.rearrange("p t c -> p (t c)").rearrange("p (g c) -> p g c", c=4),
                                     g5[:, :, 0:4],
                                     asd[0:NP, 3, :, :].rearrange("p t h -> p (t h)").unsqueeze(2).broadcast_to([NP, 20, 4]),
                                     ALU.mult))

                def wide(i):
                    return gatc[0:NP, i, :].unsqueeze(1).broadcast_to([NP, T, 16])

                def tall(c):
                    return sca[0:NP, c, :].unsqueeze(2).broadcast_to([NP, T, 16])

                link(V.tensor_tensor(agg, agg, wide(2), ALU.add))
                link(V.tensor_reduce(sca[0:NP, 0, :], agg, AX.X, ALU.add))
                link(V.tensor_scalar(sca[0:NP, 0, :], sca[0:NP, 0, :], 1.0 / 16, None, ALU.mult))
                link(V.tensor_tensor(agg, agg, tall(0), ALU.subtract))
                link(V.tensor_tensor(scr[0:NP, 2, :, :], agg, agg, ALU.mult))
                V.tensor_reduce(sca[0:NP, 1, :], scr[0:NP, 2, :, :], AX.X, ALU.add).then_inc(sem("var16"), 1)
                dve.wait_ge(sem("std16"), 1)
                link(V.reciprocal(sca[0:NP, 3, :], sca[0:NP, 2, :]))
                link(V.tensor_tensor(agg, agg, tall(3), ALU.mult))
                link(V.tensor_tensor(agg, agg, wide(3), ALU.mult))
                link(V.tensor_tensor(agg, agg, wide(4), ALU.add))
                link(V.tensor_reduce(scr[0:NP, 0, :, 0:4], agg.rearrange("p t (h c) -> p t c h", c=4), AX.X, ALU.add))
                link(V.tensor_scalar(scr[0:NP, 2, :, 0:4], scr[0:NP, 0, :, 0:4], 0.25, None, ALU.mult))
                top2_gate(scr[0:NP, 2, :, 0:4], X0, 1)
                V.tensor_scalar(sca[0:NP, 12, :], sca[0:NP, 11, :], 1.0, None, ALU.mult).then_inc(sem("gate"), 1)
                for t in range(T):
                    dve.wait_ge(sem("f0_out_mm"), t + 1)
                    i = V.tensor_tensor(x[0:NP, t, :], ps[0:NP, 4 + t % 4, 0:D], x[0:NP, t, :], ALU.add)
                    i.then_inc(sem("f0_out_ev"), 1)
                for e in range(X0):
                    for t in range(T):
                        n = T * (e + 1) + t
                        dve.wait_ge(sem("f0_out_mm"), n + 1)
                        dve.wait_ge(sem("f0_out_ev"), n - T + 1)
                        i = V.scalar_tensor_tensor(out=x[0:NP, t, :], in0=ps[0:NP, 4 + n % 4, 0:D],
                                                   scalar=gate[0:NP, t, e:e + 1], in1=x[0:NP, t, :],
                                                   op0=ALU.mult, op1=ALU.add)
                        i.then_inc(sem("f0_out_ev"), 1)
                last = V.tensor_scalar(sca[0:NP, 13, :], sca[0:NP, 11, :], 1.0, None, ALU.mult)
                dve.wait_ge(sem("f0_out_ev"), T * (X0 + 1))

            if STOP >= 3:
                norm(x)
                dve.wait_ge(sem("ld_g1"), 80)
                add_bias(bc3)
                last = add_rows("g1f_mm")
            if STOP >= 4:
                link(last)
                norm(x)
                link(V.tensor_tensor(x[0:NP, :, :], x[0:NP, :, :], xn[0:NP, :, :], ALU.add))
                for t in range(T):
                    i = V.tensor_scalar(ltmask[0:NP, t, :], iota[0:NP, 0:N], node[0:NP, t:t + 1], None, ALU.is_lt)
                turn()
                dve.wait_ge(sem("wrow_ev"), 2)
                for t in range(T):
                    i = V.tensor_tensor_reduce(out=dtmp[0:NP, t, :], in0=wrow[0:NP, tile(t)], in1=ident[0:NP, 0:NP],
                                               scale=1.0, scalar=0.0, op0=ALU.mult, op1=ALU.add,
                                               accum_out=wcol[0:NP, t:t + 1])
                link(i)
                for t in range(T):
                    i = V.tensor_scalar(wj[0:NP, 0, :], wrow[0:NP, :], wcol[0:NP, t:t + 1], 0.0, ALU.is_gt, ALU.add,
                                        accum_out=rk[0:NP, 0, t:t + 1])
                    link(i)
                    i = V.scalar_tensor_tensor(out=wj[0:NP, 1, :], in0=wrow[0:NP, :], scalar=wcol[0:NP, t:t + 1],
                                               in1=ltmask[0:NP, t, :], op0=ALU.is_equal, op1=ALU.mult,
                                               accum_out=rk[0:NP, 1, t:t + 1])
                    link(i)
                link(V.tensor_tensor(rk[0:NP, 2, :], rk[0:NP, 0, :], rk[0:NP, 1, :], ALU.add))
                link(V.scalar_tensor_tensor(out=rk[0:NP, 3, :], in0=rk[0:NP, 2, :], scalar=float(KEEP1),
                                            in1=wcol[0:NP, :], op0=ALU.is_lt, op1=ALU.mult))
                dve.wait_ge(sem("ld_f1"), 48)
                for t in range(T):
                    dve.wait_ge(sem("f1_out_mm"), t + 1)
                    i = V.tensor_tensor(h2[0:NP, t, :], ps[0:NP, t, 0:D], m2b[0:NP, :], ALU.add)
                link(i)
                for t in range(T):
                    last = V.scalar_tensor_tensor(out=x[0:NP, t, :], in0=h2[0:NP, t, :], scalar=rk[0:NP, 3, t:t + 1],
                                                  in1=x[0:NP, t, :], op0=ALU.mult, op1=ALU.add)

            if STOP >= 5:
                link(last)
                norm(x)
                turn()
                for t in range(T):
                    dve.wait_ge(sem("g2a_mm"), t + 1)
                    V.tensor_tensor(x[0:NP, t, :], ps[0:NP, 3 + t, 0:D], x[0:NP, t, :], ALU.add
                                    ).then_inc(sem("g2a_v"), 1)
                for t in range(T):
                    dve.wait_ge(sem("hn"), t + 1)
                    at = hn[0:NP, t, :]
                    for r in range(MAXK // 8):
                        link(V.max(top8[0:NP, t, r, :], at))
                        to = wk[0:NP, r % 2, t, :]
                        link(V.match_replace(to, top8[0:NP, t, r, :], at, -3e38))
                        at = to
                    V.scalar_tensor_tensor(out=hn[0:NP, t, :], in0=at, scalar=-3e38, in1=hn[0:NP, t, :],
                                           op0=ALU.is_equal, op1=ALU.mult).then_inc(sem("hs"), 1)
                for t in range(T):
                    dve.wait_ge(sem("g2b_mm"), t + 1)
                    last = V.scalar_tensor_tensor(out=x[0:NP, t, :], in0=ps[0:NP, t, 0:D], scalar=rdeg[0:NP, t:t + 1],
                                                  in1=x[0:NP, t, :], op0=ALU.mult, op1=ALU.add)
            if STOP >= 6:
                link(last)
                norm(x)
                turn()
                dve.wait_ge(sem("lg2_mm"), 1)
                dve.wait_ge(sem("ld_s2"), 32)
                lg, ex, oh = scr[0:NP, 0, :, 0:X2], scr[0:NP, 1, :, 0:X2], scr[0:NP, 2, :, 0:X2]

                def each(c):
                    return sca[0:NP, c, :].unsqueeze(2).broadcast_to([NP, T, X2])

                link(V.tensor_tensor(lg, ps[0:NP, 3, 0:T * X2].rearrange("p (t e) -> p t e", t=T),
                                     g2b[0:NP, :].unsqueeze(1).broadcast_to([NP, T, X2]), ALU.add))
                link(V.tensor_reduce(sca[0:NP, 0, :], lg, AX.X, ALU.max))
                V.tensor_tensor(lg, lg, each(0), ALU.subtract).then_inc(sem("to_exp"), 1)
                dve.wait_ge(sem("exped"), 2)
                link(V.tensor_reduce(sca[0:NP, 1, :], ex, AX.X, ALU.add))
                link(V.reciprocal(sca[0:NP, 2, :], sca[0:NP, 1, :]))
                link(V.tensor_tensor(ex, ex, each(2), ALU.mult))
                first_max(ex, X2, oh, sca[0:NP, 3, :], scr[0:NP, 5, :, 0:X2])
                V.tensor_copy(ohb[0:NP, :, :], oh).then_inc(sem("ohb"), 1)
                link(V.tensor_tensor(scr[0:NP, 3, :, 0:X2], oh,
                                     iota[0:NP, 0:SL:CAP].unsqueeze(1).broadcast_to([NP, T, X2]), ALU.mult))
                link(V.tensor_reduce(sca[0:NP, 4, :], scr[0:NP, 3, :, 0:X2], AX.X, ALU.add))
                dve.wait_ge(sem("pos_mm"), 1)
                link(V.tensor_tensor(scr[0:NP, 4, :, 0:X2], ps[0:NP, 4, 0:T * X2].rearrange("p (t e) -> p t e", t=T),
                                     oh, ALU.mult))
                link(V.tensor_reduce(sca[0:NP, 5, :], scr[0:NP, 4, :, 0:X2], AX.X, ALU.add))
                link(V.tensor_scalar(sca[0:NP, 6, :], sca[0:NP, 5, :], float(CAP), None, ALU.is_le))
                V.tensor_tensor(prk[0:NP, :], sca[0:NP, 3, :], sca[0:NP, 6, :], ALU.mult)
                link(V.tensor_tensor(sca[0:NP, 7, :], sca[0:NP, 4, :], sca[0:NP, 5, :], ALU.add))
                link(V.tensor_tensor(sca[0:NP, 8, :], sca[0:NP, 7, :], sca[0:NP, 6, :], ALU.mult))
                link(V.tensor_scalar(slot[0:NP, :], sca[0:NP, 8, :], 1.0, None, ALU.subtract))
                V.tensor_scalar(sca[0:NP, 9, :], sca[0:NP, 8, :], 1.0, None, ALU.subtract).then_inc(sem("slot"), 1)
                for t in range(T):
                    V.tensor_scalar(SC[0:NP, t, :], iota[0:NP, 0:SL], slot[0:NP, t:t + 1], None, ALU.is_equal
                                    ).then_inc(sem("sc"), 1)
                dve.wait_ge(sem("srow_ev"), 2)
                for e in range(X2):
                    V.tensor_scalar(ST[0:CAP, e, :], srow[0:CAP, :], float(e * CAP), node[0:CAP, 0:1],
                                    ALU.subtract, ALU.is_equal).then_inc(sem("st"), 1)
                dve.wait_ge(sem("ld_late"), 16 * (3 + X2))
                dve.wait_ge(sem("ld_s3"), 112)
                for i in range(2):
                    link(V.tensor_tensor(pr3, W3[:, :, 0:D], att3[:, i, :].unsqueeze(1).broadcast_to([128, KD, D]), ALU.mult))
                    for k in range(KD):
                        j = V.tensor_reduce(W3[:, k, D + HEADS * i:D + HEADS * (i + 1)],
                                            pr3[:, k, :].rearrange("p (h c) -> p h c", h=HEADS), AX.X, ALU.add)
                    link(j)
                V.tensor_scalar(sca[0:NP, 9, :], sca[0:NP, 8, :], 1.0, None, ALU.subtract).then_inc(sem("w3"), 1)
                dve.wait_ge(sem("disp_mm"), 4)
                dve.wait_ge(sem("ld_rc"), 32)
                link(V.tensor_copy(rcf[0:NP, :, :], rci[0:NP, :, :]))
                for i, g in enumerate((Gc, Gr)):
                    for t in range(T):
                        V.tensor_scalar(g[0:NP, t, :], rcf[0:NP, i, :], node[0:NP, t:t + 1], None, ALU.is_equal
                                        ).then_inc(sem("gcr"), 1)

                with dve.Fori(0, X2 // 2) as i:
                    for b in range(2):
                        dve.wait_ge(sem("f2_out_mm"), 2 * i + b + 1)
                        V.tensor_tensor(ybuf[0:CAP, bass.ds(2 * i + b, 1), :].rearrange("p a n -> p (a n)"),
                                        ps[0:CAP, 4 + b, 0:D],
                                        f2b2[0:CAP, bass.ds(2 * i + b, 1), :].rearrange("p a n -> p (a n)"), ALU.add
                                        ).then_inc(sem("f2_out_ev"), 1)
                V.memset(cst4[:, 0:1], 1e4)
                V.memset(cst4[:, 1:2], -1e4)
                V.memset(h2[0:NP, :, :], 0.0)
                for t in range(T):
                    dve.wait_ge(sem("comb_mm"), t + 1)
                    i = V.tensor_scalar(xn[0:NP, t, :], ps[0:NP, t, 0:D], prk[0:NP, t:t + 1], None, ALU.mult)
                link(i)
                mi = RW[:, 4 * N:4 * N + T * D].bitcast(I32).rearrange("p (t n) -> p t n", t=T)[0:NP]
                y = xn[0:NP, :, :]
                link(V.tensor_tensor(mi, y, y, ALU.is_equal))
                link(V.copy_predicated(h2[0:NP, :, :], mi, y))
                for c, (op, lim) in enumerate(((ALU.is_gt, 3.4028234e38), (ALU.is_lt, -3.4028234e38))):
                    link(V.tensor_scalar(mi, y, lim, None, op))
                    link(V.copy_predicated(h2[0:NP, :, :], mi, cst4[0:NP, c:c + 1].unsqueeze(2).broadcast_to([NP, T, D])))
                link(V.tensor_tensor(x[0:NP, :, :], x[0:NP, :, :], h2[0:NP, :, :], ALU.add))
                V.tensor_scalar(sca[0:NP, 9, :], sca[0:NP, 8, :], 1.0, None, ALU.subtract).then_inc(sem("x_l2"), 1)

            if STOP >= 7:
                norm(x)
                turn()
                for t in range(T):
                    dve.wait_ge(sem("g3b_mm"), t + 1)
                    i = V.tensor_copy(z3[0:NP, 0, t, :], ps[0:NP, t, D:D + HEADS])
                link(i)
                z = z3[0:NP, 0, :, :]

                def each4(c):
                    return sca[0:NP, c, :].unsqueeze(2).broadcast_to([NP, T, HEADS])

                link(V.scalar_tensor_tensor(out=z3[0:NP, 2, :, :], in0=z, scalar=0.01, in1=z, op0=ALU.mult, op1=ALU.max))
                link(V.tensor_reduce(sca[0:NP, 0, :], z3[0:NP, 2, :, :], AX.X, ALU.max))
                V.tensor_tensor(z, z3[0:NP, 2, :, :], each4(0), ALU.subtract).then_inc(sem("to_exp"), 1)
                dve.wait_ge(sem("exped"), 3)
                link(V.tensor_reduce(sca[0:NP, 1, :], z3[0:NP, 1, :, :], AX.X, ALU.add))
                link(V.reciprocal(sca[0:NP, 2, :], sca[0:NP, 1, :]))
                link(V.tensor_tensor(z3[0:NP, 2, :, :], z3[0:NP, 1, :, :], each4(2), ALU.mult))
                for h in range(HEADS):
                    for t in range(T):
                        xs = ps[0:NP, t, h * HD3:(h + 1) * HD3]
                        al = z3[0:NP, 2, t, h:h + 1]
                        if h == 0:
                            i = V.tensor_scalar(tmp3[0:NP, 0, t, :], xs, al, None, ALU.mult)
                        else:
                            i = V.scalar_tensor_tensor(out=tmp3[0:NP, h % 2, t, :], in0=xs, scalar=al,
                                                       in1=tmp3[0:NP, (h + 1) % 2, t, :], op0=ALU.mult, op1=ALU.add)
                    link(i)
                for t in range(T):
                    xv = x[0:NP, t, :].rearrange("p (h c) -> p h c", h=HEADS)
                    last = V.tensor_tensor(xv, xv, tmp3[0:NP, 1, t, :].unsqueeze(1).broadcast_to([NP, HEADS, HD3]), ALU.add)

            if STOP >= 8:
                link(last)
                norm(x)
                turn()
                dve.wait_ge(sem("lg3_mm"), 1)
                lg = scr[0:NP, 2, :, :]
                link(V.tensor_tensor(lg, ps[0:NP, 3, 0:T * X3].rearrange("p (t e) -> p t e", t=T),
                                     g3b[0:NP, :].unsqueeze(1).broadcast_to([NP, T, X3]), ALU.add))
                top2_gate(lg, X3, 4, oh3[0:NP])
                V.tensor_scalar(sca[0:NP, 12, :], sca[0:NP, 11, :], 1.0, None, ALU.mult).then_inc(sem("gate"), 1)
                dve.wait_ge(sem("rank_mm"), 1)
                V.tensor_scalar(rank3[0:NP, :, :], ps[0:NP, 4, 0:T * X3].rearrange("p (t e) -> p t e", t=T), 1.0, None,
                                ALU.subtract)
                more, before, upto, numb, shift = (e3[:, i, :] for i in range(5))
                link(V.tensor_copy(numb, ps[:, 4, 128:128 + X3]))
                V.tensor_tensor(more3[:, :, :], numb.unsqueeze(2).broadcast_to([128, X3, 4]),
                                iota[:, 128:640:128].unsqueeze(1).broadcast_to([128, X3, 4]), ALU.is_gt)
                link(V.tensor_tensor(less3[:, :, :], iota[:, 0:X3].unsqueeze(1).broadcast_to([128, X3, X3]),
                                     iota[:, 0:X3].unsqueeze(2).broadcast_to([128, X3, X3]), ALU.is_lt))
                link(V.tensor_reduce(more, more3[:, :, :], AX.X, ALU.add))
                link(V.tensor_tensor(less3[:, :, :], less3[:, :, :], more.unsqueeze(1).broadcast_to([128, X3, X3]),
                                     ALU.mult))
                link(V.tensor_reduce(before, less3[:, :, :], AX.X, ALU.add))
                link(V.tensor_tensor(shift, before, iota[:, 0:X3], ALU.subtract))
                link(V.tensor_scalar(shift, shift, float(X3 - 1), 128.0, ALU.add, ALU.mult))
                link(V.scalar_tensor_tensor(out=place3[0:NP, :, :], in0=rank3[0:NP, :, :], scalar=128.0,
                                            in1=shift[0:NP, :].unsqueeze(1).broadcast_to([NP, T, X3]),
                                            op0=ALU.is_ge, op1=ALU.mult))
                link(V.tensor_tensor(place3[0:NP, :, :], place3[0:NP, :, :], rank3[0:NP, :, :], ALU.add))
                link(V.scalar_tensor_tensor(out=place3[0:NP, :, :], in0=iota[0:NP, 0:X3].unsqueeze(1).broadcast_to([NP, T, X3]),
                                            scalar=128.0, in1=place3[0:NP, :, :], op0=ALU.mult, op1=ALU.add))
                for c in range(2):
                    i = V.tensor_tensor(ohp3[0:NP, c, :, :], oh3[0:NP, c, :, :], place3[0:NP, :, :], ALU.mult)
                link(i)
                for c in range(2):
                    i = V.tensor_reduce(scr[0:NP, 0, c:c + 1, 0:T], ohp3[0:NP, c:c + 1, :, :], AX.X, ALU.add)
                link(i)
                V.tensor_copy(row3[0:NP, :, :], scr[0:NP, 0, 0:2, 0:T]).then_inc(sem("row3"), 1)
                link(V.tensor_tensor(upto, before, more, ALU.add))
                link(V.tensor_tensor(below3[:, :, :], upto.unsqueeze(1).broadcast_to([128, OV3, X3]),
                                     iota[:, 0:OV3].unsqueeze(2).broadcast_to([128, OV3, X3]), ALU.is_le))
                link(V.tensor_reduce(idf3, below3[:, :, :], AX.X, ALU.add))
                link(V.tensor_scalar(idf3, idf3, float(X3 - 1), 128.0, ALU.min, ALU.mult))
                link(V.tensor_scalar(idf3, idf3, node[:, 0:1], None, ALU.add))
                V.tensor_copy(id3[:, :], idf3).then_inc(sem("id3"), 1)
                dve.wait_ge(sem("f3_bias_mm"), 1)
                for t in range(T):
                    V.tensor_tensor(h2[0:NP, t, :], ps[0:NP, 5 + t // 2, (t % 2) * D:(t % 2 + 1) * D], xn[0:NP, t, :],
                                    ALU.add).then_inc(sem("f3_out_ev"), 1)

                def f3_turn(j, s):
                    dve.wait_ge(sem("xg_mm"), j + 1)
                    if not (isinstance(j, int) and j < 2):
                        dve.wait_ge(sem("f3_hid_mm"), 2 * j - 2)
                    V.tensor_copy(xgT[:, s, :, :], ps[:, s, 0:D].rearrange("p (k n) -> p k n", k=KD)
                                  ).then_inc(sem("xgT_ev"), 1)

                def f3_step(j, b):
                    if not isinstance(j, int) or j + 2 < J3:
                        f3_turn(j + 2, b % 2)
                    dve.wait_ge(sem("f3_out_mm"), j + 1)
                    if not (isinstance(j, int) and j < 4):
                        dve.wait_ge(sem(f"st_y{b}"), 4 * (j - b))
                    V.tensor_copy(yo[:, b, :], ps[:, 4 + b % 2, 0:D]).then_inc(sem("f3_out_ev"), 1)

                f3_turn(0, 0)
                f3_turn(1, 1)
                for j in range(4):
                    f3_step(j, j)
                with dve.Fori(1, (J3 - 2) // 4) as i:
                    for b in range(4):
                        f3_step(4 * i + b, b)
                for j in range((J3 - 2) // 4 * 4, J3):
                    f3_step(j, j % 4)
                dve.wait_ge(sem("ld_yg"), 16 * 2 * T)
                for c in range(2):
                    for t in range(T):
                        i = V.scalar_tensor_tensor(out=h2[0:NP, t, :], in0=yg[0:NP, t, c, :],
                                                   scalar=sca[0:NP, 10 + c, t:t + 1], in1=h2[0:NP, t, :],
                                                   op0=ALU.mult, op1=ALU.add)
                    link(i)
                norm(h2)
                link(V.tensor_scalar(sca[0:NP, 12, :], sca[0:NP, 11, :], 1.0, None, ALU.mult))
                link(V.tensor_tensor(xn[0:NP, :, :], xn[0:NP, :, :], gam[0:NP, :].unsqueeze(1).broadcast_to([NP, T, D]),
                                     ALU.mult))
                V.tensor_tensor(x[0:NP, :, :], x[0:NP, :, :], bet[0:NP, :].unsqueeze(1).broadcast_to([NP, T, D]), ALU.add)
                link(V.tensor_scalar(sca[0:NP, 13, :], sca[0:NP, 11, :], 1.0, None, ALU.mult))
                last = V.tensor_tensor(x[0:NP, :, :], x[0:NP, :, :], xn[0:NP, :, :], ALU.add)
            link(V.tensor_scalar(sca[0:NP, 14, :], dinvc[0:NP, :], 1.0, None, ALU.mult))
            V.tensor_scalar(sca[0:NP, 14, :], dinvc[0:NP, :], 1.0, None, ALU.mult).then_inc(sem("x_final"), 1)


BANKS = [[(2, 2), (3, 3), (4, 4), (0, 0), (1, 1)], [(0, 5), (1, 6), (2, 7), (3, 0), (4, 1)]]
XN_OF_TURN = [1, 3, 4, 5, 6, 7]


_INS = ["x", "src", "dst", "L0_gnn_W1", "L0_gnn_W2", "L0_gnn_b2", "L0_ffn_W_gat", "L0_ffn_att_src", "L0_ffn_att_dst",
        "L0_ffn_b_gat", "L0_ffn_ln_gamma", "L0_ffn_ln_beta", "L0_ffn_b2", "L0_ffn_edge_index", "L1_gnn_W1",
        "L1_gnn_W2", "L1_gnn_W3", "L1_gnn_b3", "L1_ffn_br", "L1_ffn_w1", "L1_ffn_w2", "L1_ffn_b2",
        "L2_gnn_W_self", "L2_gnn_W_neigh", "L2_ffn_gate_w", "L2_ffn_gate_b", "L2_ffn_b2", "L3_gnn_weight",
        "L3_gnn_attn_l", "L3_gnn_attn_r", "L3_ffn_gate_w", "L3_ffn_gate_b", "L3_ffn_b2", "L3_ffn_gamma",
        "L3_ffn_beta"]
_EXPERTS = {"L0_experts": ("L0_ffn_W1", "L0_ffn_W2"), "L2_experts": ("L2_ffn_w1", "L2_ffn_w2"),
            "L3_experts": ("L3_ffn_w1", "L3_ffn_w2", "L3_ffn_b1")}


def laid_out(np, inputs):
    arrays = {name: np.ascontiguousarray(inputs[name]) for name in _INS}

    def by_partition(w):
        if w.ndim == 2:
            w = w[:, :, None]
        e, k, n = w.shape
        return w.reshape(e, k // 128, 128, n).transpose(0, 2, 1, 3).reshape(e, 128, -1)

    for name, pair in _EXPERTS.items():
        arrays[name] = np.concatenate([by_partition(np.asarray(inputs[w])) for w in pair], axis=2)
    arrays["bias_columns"] = np.ascontiguousarray(
        np.concatenate([np.asarray(inputs[name]).reshape(-1, 128).T for name, _ in BIAS_COLUMNS], axis=1))
    return arrays


def kernel(**inputs):
    import numpy as _np
    import concourse.bacc as _bacc
    from concourse import mybir as _mybir
    from concourse.bass_utils import run_bass_kernel_spmd as _run

    nc = _bacc.Bacc("TRN2", target_bir_lowering=False, num_devices=1)
    arrays, args = {}, {}
    for name, v in laid_out(_np, inputs).items():
        arrays[f"in_{name}"] = v
        args[name] = nc.dram_tensor(f"in_{name}", v.shape, _mybir.dt.from_np(v.dtype), kind="ExternalInput").ap()
    out = nc.dram_tensor("out_x", (N, D), F32, kind="ExternalOutput").ap()
    graph_mlp_stack(nc, args, out)
    r = _run(nc, [arrays], core_ids=[0])
    return r.results[0]["out_x"]
```

```python
from contextlib import ExitStack

import concourse.bass as bass
from concourse import mybir

ALU = mybir.AluOpType
ACT = mybir.ActivationFunctionType
AX = mybir.AxisListType
F32 = mybir.dt.float32
F16 = mybir.dt.float16
BF16 = mybir.dt.bfloat16
I32 = mybir.dt.int32
U32 = mybir.dt.uint32

N = 625
NP = 125
T = 5
D = 256
KD = D // 128
PIECES = [(0, 313), (313, 312)]
BANK = 512
EPS = 1e-5
BIG = 1e30
BIAS_COLUMNS = [("L0_gnn_b1", 4), ("L0_ffn_b1", 16), ("L1_gnn_b1", 2), ("L1_gnn_b2", 2), ("L1_ffn_b1", 8),
                ("L2_ffn_b1", 64), ("L1_ffn_wr", 2)]


def graph_mlp_stack(nc, a, out):
    E1 = a["src"].shape[0]
    EP1, ET1, EU1 = 125, E1 // 125, 5
    E2 = a["L0_ffn_edge_index"].shape[1]
    EP2, ET2, EU2 = 128, E2 // 128, 8
    HALF, BASE = (N + 1) // 2, 4096

    def groups(graph, tiles, unroll, parts, before=0):
        steps, most, first, got = tiles // unroll, (BASE - 1) // parts // unroll, 0, []
        count = -(-steps // most)
        for k in range(count):
            iters = steps // count + ((k - count // 2) % count >= -steps % count)
            got.append((graph, parts, unroll, first, iters, before + first))
            first += iters * unroll
        return got

    GROUPS = groups(0, ET1, EU1, EP1) + groups(1, ET2, EU2, EP2, before=ET1)
    GA, GALL = sum(g[0] == 0 for g in GROUPS), len(GROUPS)
    X0, F0 = 4, 512
    HEADS = 4
    KEEP1 = int(0.5 * N) - 1
    X2, F2 = 8, 1024
    CAP = -(-5 * N // (4 * X2))
    SL = X2 * CAP
    X3, F3 = 16, 512
    OV3 = (2 * N - X3) // 128
    J3 = X3 + OV3
    W3E = KD * F3 + F3 // 128 * D + F3 // 128
    MAXK = 32
    HD3 = 64
    W3C = D + 2 * HEADS

    ctx = ExitStack()
    with ctx:
        def sb(name, shape, dt=F32):
            return ctx.enter_context(nc.sbuf_tensor(name, shape, dt))

        sems = {}

        def sem(name):
            if name not in sems:
                sems[name] = ctx.enter_context(nc.semaphore(name))
            return sems[name]

        ps = ctx.enter_context(nc.psum_tensor("ps", [128, 8, BANK], F32))
        psb = ps[:, :, :].bitcast(BF16)

        iota = sb("iota", [128, SL], F16)
        ident = sb("ident", [128, 128])
        ones = sb("ones", [128, 128])
        identb = sb("identb", [128, 128], BF16)
        onesb = sb("onesb", [128, 128], BF16)
        tri = sb("tri", [128, 128], BF16)
        zerob = sb("zerob", [1, BANK], BF16)
        node = sb("node", [128, T])
        epsc = sb("epsc", [128, 1])
        digc = sb("digc", [128, 1])
        desc = sb("desc", [128, X3])

        R1 = sb("R1", [128, 6250])
        R2 = sb("R2", [128, 12304])
        R3 = sb("R3", [128, 5250])
        RW = sb("RW", [128, 8192])
        AT = sb("AT", [128, T, N])
        AHB = sb("AHB", [128, 2 * T * N])
        Ahat = AHB[:, 0:T * N].rearrange("p (t n) -> p t n", t=T)
        BT = AHB[:, T * N:].rearrange("p (t n) -> p t n", t=T)

        x = sb("x", [128, T, D])
        xn = sb("xn", [128, T, D])
        xnT = sb("xnT", [128, KD, N])
        aggT = sb("aggT", [128, KD, N])
        h2 = sb("h2", [128, T, D])
        gT = aggT[0:X3, 0, :]

        oh_s = R1[:, 0:EU2 * 320].bitcast(BF16).rearrange("p (u n) -> p u n", u=EU2)
        oh_d = R2[:, 7100:7100 + EU2 * 160].bitcast(BF16).rearrange("p (u n) -> p u n", u=EU2)
        sums2 = [R2[:, c:c + T * HALF].rearrange("p (t n) -> p t n", t=T) for c in (0, 8400)]
        highi = R2[:, 1600:1600 + T * HALF].bitcast(I32).rearrange("p (t n) -> p t n", t=T)
        high = R2[:, 3900:3900 + T * HALF].rearrange("p (t n) -> p t n", t=T)
        nhigh = R2[:, 5500:5500 + T * HALF].rearrange("p (t n) -> p t n", t=T)
        idi1 = R3[:, 0:2 * ET1].bitcast(I32).rearrange("p (a t) -> p a t", a=2)
        idf1 = R3[:, 2 * ET1:5 * ET1].rearrange("p (a t) -> p a t", a=3)
        o2 = 5 * ET1
        idi2 = R3[:, o2:o2 + 2 * ET2].bitcast(I32).rearrange("p (a t) -> p a t", a=2)
        digs = R3[:, 2200:2200 + ET2]
        idf2 = R3[:, o2 + 2 * ET2:o2 + 5 * ET2].rearrange("p (a t) -> p a t", a=3)
        dinvr = R2[:, 3200:3200 + N]
        Bneg = R3[:, 2100:2100 + 1563].bitcast(BF16)[:, 0:T * N].rearrange("p (t n) -> p t n", t=T)
        maskb = R3[:, 3663:3663 + 1563].bitcast(BF16)[:, 0:T * N].rearrange("p (t n) -> p t n", t=T)
        dinvc = sb("dinvc", [128, T])
        rdeg = sb("rdeg", [128, T])
        dtmp = h2[:, :, 0:NP]

        h1T = R1[:, 0:2500].rearrange("p (m n) -> p m n", m=4)
        W01 = R1[:, 3300:3300 + 1024].rearrange("p (k n) -> p k n", k=2)
        W02 = R1[:, 4400:4400 + 1024].rearrange("p (k n) -> p k n", k=4)
        bcols = sb("bcols", [128, sum(n for _, n in BIAS_COLUMNS)])
        bcol, at0 = {}, 0
        for name, n in BIAS_COLUMNS:
            bcol[name] = bcols[:, at0:at0 + n]
            at0 += n
        b01 = bcol["L0_gnn_b1"]
        b02 = sb("b02", [128, D])

        Wg = sb("Wg", [128, KD, 16])
        gatc = sb("gatc", [128, 5, 16])
        hg = sb("hg", [128, T, 16])
        haug = R2[:, 11250:11250 + T * HEADS * 20].rearrange("p (t h c) -> p t h c", t=T, h=HEADS)
        gatT = R2[0:20, 11650:11650 + N]
        prod = sb("prod", [128, T, 16])
        asd = sb("asd", [128, 7, T, HEADS])
        prow = R2[:, 0:2500].rearrange("p (h n) -> p h n", h=HEADS)
        qrow = R2[:, 2500:5000].rearrange("p (h n) -> p h n", h=HEADS)
        EE = R2[:, 5000:11250].rearrange("p (b t n) -> p b t n", b=2, t=T)
        arow = R2[:, 5000:7500].rearrange("p (h n) -> p h n", h=HEADS)
        junk = R3[:, 3700:3700 + 2 * N].rearrange("p (b n) -> p b n", b=2)
        up = R3[:, 0:2 * N].rearrange("p (b n) -> p b n", b=2)
        uq = R3[:, 2 * N:4 * N].rearrange("p (b n) -> p b n", b=2)
        ev = R3[:, 4 * N:6 * N].rearrange("p (b n) -> p b n", b=2)
        scr = sb("scr", [128, 7, T, 16])
        sca = sb("sca", [128, 16, T])
        FWs = [RW[:, e * 2048:(e + 1) * 2048] for e in range(X0)]
        FW1 = [w[:, 0:1024].rearrange("p (k n) -> p k n", k=KD) for w in FWs]
        FW2 = [w[:, 1024:2048].rearrange("p (k n) -> p k n", k=4) for w in FWs]
        f0b1 = bcol["L0_ffn_b1"]
        f0b2 = sb("f0b2", [X0, D])
        hh = [h.rearrange("p (m n) -> p m n", m=4) for h in (R1[:, 0:2500], R1[:, 2500:5000], R2[:, 5000:7500])]
        gate = sb("gate", [128, T, X3])

        Wc = sb("Wc", [128, 3, KD, D])
        bc12 = [bcol["L1_gnn_b1"], bcol["L1_gnn_b2"]]
        bc3 = sb("bc3", [128, D])
        M1 = RW[:, 0:2048].rearrange("p (k n) -> p k n", k=KD)
        M2 = RW[:, 2048:4096].rearrange("p (k n) -> p k n", k=8)
        m1b = bcol["L1_ffn_b1"]
        m2b = RW[:, 7696:7696 + D]
        wr = bcol["L1_ffn_wr"]
        br = sb("br", [128, 1])
        ltmask = AHB[:, T * N:T * N + 1563].bitcast(BF16)[:, 0:T * N].rearrange("p (t n) -> p t n", t=T)
        wrow = R3[:, 0:N]
        wj = R3[:, N:3 * N].rearrange("p (b n) -> p b n", b=2)
        hT = R1[:, 0:5000].rearrange("p (m n) -> p m n", m=8)
        wcol = sb("wcol", [128, T])
        rk = sb("rk", [128, 4, T])

        Wsn = RW[:, 4096:5120].rearrange("p (k n) -> p k n", k=KD)
        hn = R3[:, 0:1280].rearrange("p (t n) -> p t n", t=T)
        wk = R3[:, 1280:3840].rearrange("p (b t n) -> p b t n", b=2, t=T)
        top8 = sb("top8", [128, T, 4, 8])
        G2 = sb("G2", [128, KD, X2])
        g2b = sb("g2b", [128, X2])
        f2b1 = bcol["L2_ffn_b1"]
        f2b2 = RW[:, 5120:7168].rearrange("p (e n) -> p e n", e=X2)
        ohb = sb("ohb", [128, T, X2], BF16)
        slot = sb("slot", [128, T])
        prk = sb("prk", [128, T])
        SC = R1[:, 0:T * SL].rearrange("p (t s) -> p t s", t=T)
        ST = AHB[:, 0:X2 * N].rearrange("p (e n) -> p e n", e=X2)
        srow = AHB[:, X2 * N:(X2 + 1) * N]
        XbT = R3[:, 0:KD * SL].rearrange("p (k s) -> p k s", k=KD)
        hTe = R3[:, 1568:1568 + 1568].rearrange("p (b m s) -> p b m s", b=2, m=8)
        ybuf = R3[:, 3136:3136 + 2048].rearrange("p (e n) -> p e n", e=X2)
        F2W = R2[:, 0:8192].rearrange("p (b n) -> p b n", b=2)
        F2W1 = [F2W[:, b, 0:2048].rearrange("p (k n) -> p k n", k=KD) for b in range(2)]
        F2W2 = [F2W[:, b, 2048:4096].rearrange("p (k n) -> p k n", k=8) for b in range(2)]
        cst4 = sb("cst4", [128, 2])
        bnow = sb("bnow", [128, 4, 8])

        W3 = RW[:, 7168:7168 + KD * W3C].rearrange("p (k n) -> p k n", k=KD)
        att3 = Wc[:, 0, :, :]
        pr3 = h2[:, 0:2, :]
        Gc = R1[:, 0:T * N].rearrange("p (t n) -> p t n", t=T)
        Gr = R1[:, T * N:2 * T * N].rearrange("p (t n) -> p t n", t=T)
        rci = RW[:, 0:2 * N].bitcast(I32).rearrange("p (a n) -> p a n", a=2)
        rcf = RW[:, 2 * N:4 * N].rearrange("p (a n) -> p a n", a=2)
        xt = R3[:, 0:T * W3C].rearrange("p (t n) -> p t n", t=T)
        z3 = sb("z3", [128, 3, T, HEADS])
        tmp3 = aggT[:, :, 0:T * HD3].rearrange("p b (t c) -> p b t c", t=T)
        G3 = sb("G3", [128, KD, X3])
        g3b = sb("g3b", [128, X3])
        f3b2 = Wc[0:X3, 2, 0, :]
        gam = Wc[:, 1, 0, :]
        bet = Wc[:, 1, 1, :]
        F3W = R2[:, 4096:4096 + 4 * W3E].rearrange("p (b n) -> p b n", b=4)
        F3W1 = [F3W[:, b, 0:1024].rearrange("p (k n) -> p k n", k=KD) for b in range(4)]
        F3W2 = [F3W[:, b, 1024:2048].rearrange("p (k n) -> p k n", k=4) for b in range(4)]
        F3B1 = [F3W[:, b, 2048:2052] for b in range(4)]
        xg = R1[:, 0:1024].rearrange("p (b n) -> p b n", b=4)
        xgT = R1[:, 1024:1536].rearrange("p (b k n) -> p b k n", b=2, k=KD)
        hx = R1[:, 1536:2560].rearrange("p (b m n) -> p b m n", b=2, m=4)
        yo = R1[:, 2560:3584].rearrange("p (b n) -> p b n", b=4)
        yg = R3[:, 0:2 * T * D].rearrange("p (t c n) -> p t c n", t=T, c=2)
        oh3 = R3[:, 2560:2560 + 2 * T * X3].rearrange("p (c t e) -> p c t e", c=2, t=T)
        rank3 = R3[:, 2720:2800].rearrange("p (t e) -> p t e", t=T)
        place3 = R3[:, 2800:2880].rearrange("p (t e) -> p t e", t=T)
        ohp3 = R3[:, 2880:3040].rearrange("p (c t e) -> p c t e", c=2, t=T)
        more3 = R3[:, 3040:3104].rearrange("p (e j) -> p e j", j=4)
        less3 = R3[:, 3104:3360].rearrange("p (e f) -> p e f", e=X3)
        e3 = R3[:, 3360:3360 + 5 * X3].rearrange("p (i e) -> p i e", i=5)
        below3 = R3[:, 3440:3440 + OV3 * X3].rearrange("p (k e) -> p k e", k=OV3)
        idf3 = R3[:, 3600:3600 + OV3]
        m3b = sb("m3b", [128, T, X3], BF16)
        row3 = sb("row3", [128, 2, T], U32)
        id3 = sb("id3", [128, OV3], U32)
        rows3 = nc.dram_tensor("slot_rows", (J3 * 128, D), F32, kind="Internal").ap()
        outs3 = nc.dram_tensor("slot_outputs", (J3 * 128, D), F32, kind="Internal").ap()

        st = sb("st", [128, T, 6])
        mv = sb("mv", [128, T, 2])
        sd = sb("sd", [128, T])
        rs = sb("rs", [128, T])

        def row(name, n):
            return a[name].rearrange("(a n) -> a n", a=1).broadcast_to([n, a[name].shape[0]])

        def kpn(ap):
            return ap.rearrange("(k p) n -> p k n", p=128)

        def tile(t):
            return slice(t * NP, (t + 1) * NP)

        block = ctx.enter_context(nc.Block())

        @block.sync
        def _(sp):
            def load(dst, src, s):
                sp.dma_start(dst, src).then_inc(sem(s), 16)

            for i, name in enumerate(("src", "dst")):
                load(idi1[0:EP1, i, :], a[name].rearrange("(p t) -> p t", p=EP1), "ld_edges1")
            load(x[0:NP, :, :], a["x"].rearrange("(t p) n -> p t n", p=NP), "ld_x")
            for i in range(2):
                load(idi2[0:EP2, i, :], a["L0_ffn_edge_index"][i, :].rearrange("(p t) -> p t", p=EP2), "ld_edges2")
            load(W01, kpn(a["L0_gnn_W1"]), "ld_g0")
            load(W02, kpn(a["L0_gnn_W2"]), "ld_g0")
            load(b02[0:NP, :], row("L0_gnn_b2", NP), "ld_g0")
            load(bcols[:, :], a["bias_columns"], "ld_g0")
            sp.wait_ge(sem("zeros"), 1)
            for t in range(T):
                sp.dma_start(rows3.rearrange("(p c r) n -> p c (r n)", p=128, c=T)[:, t, :],
                             h2[:, :, :].rearrange("p t n -> p (t n)")).then_inc(sem("zeroed"), 16)
            load(Wg[:, :, :], kpn(a["L0_ffn_W_gat"]), "ld_gat")
            for i, name in enumerate(("L0_ffn_att_src", "L0_ffn_att_dst")):
                load(gatc[0:NP, i, :], a[name].rearrange("h (a e) -> a (h e)", a=1).broadcast_to([NP, 16]), "ld_gat")
            for i, name in enumerate(("L0_ffn_b_gat", "L0_ffn_ln_gamma", "L0_ffn_ln_beta")):
                load(gatc[0:NP, 2 + i, :], row(name, NP), "ld_gat")
            for e in range(X0):
                load(RW[:, e * 2048:(e + 1) * 2048], a["L0_experts"][e], "ld_f0")
            load(f0b2[:, :], a["L0_ffn_b2"], "ld_f0")
            for i in range(3):
                load(Wc[:, i, :, :], kpn(a[f"L1_gnn_W{i + 1}"]), "ld_g1")
            load(bc3[0:NP, :], row("L1_gnn_b3", NP), "ld_g1")
            load(br[0:NP, :], row("L1_ffn_br", NP), "ld_g1")
            load(G2[:, :, :], kpn(a["L2_ffn_gate_w"]), "ld_s2")
            load(g2b[0:NP, :], row("L2_ffn_gate_b", NP), "ld_s2")
            load(G3[:, :, :], kpn(a["L3_ffn_gate_w"]), "ld_s3")
            load(g3b[0:NP, :], row("L3_ffn_gate_b", NP), "ld_s3")
            sp.wait_ge(sem("f0_out_mm"), T * (X0 + 1))
            load(m2b[0:NP, :], row("L1_ffn_b2", NP), "ld_f1")
            load(M1, kpn(a["L1_ffn_w1"]), "ld_f1")
            load(M2, kpn(a["L1_ffn_w2"]), "ld_f1")
            load(Wsn[:, :, 0:D], kpn(a["L2_gnn_W_self"]), "ld_late")
            load(Wsn[:, :, D:2 * D], kpn(a["L2_gnn_W_neigh"]), "ld_late")
            for e in range(X2):
                load(f2b2[0:CAP, e, :], a["L2_ffn_b2"][e:e + 1, :].broadcast_to([CAP, D]), "ld_late")
            load(W3[:, :, 0:D], kpn(a["L3_gnn_weight"]), "ld_late")

            def f2_load(e, b, half):
                c = slice(half * KD * F2, (half + 1) * KD * F2)
                load(F2W[:, b, c], e("L2_experts")[:, c], f"ld_f2w{b}{half}")

            def f3_load(e, b):
                load(F3W[:, b, :], e("L3_experts"), f"ld_f3w{b}")

            def of(e):
                return lambda name: a[name][e]

            def at(e):
                return lambda name: a[name][bass.ds(e, 1)].rearrange("a p n -> (a p) n")

            sp.wait_ge(sem("g1e_mm"), T)
            for i, name in enumerate(("L3_gnn_attn_r", "L3_gnn_attn_l")):
                load(att3[:, i, :], a[name].rearrange("h (a e) -> a (h e)", a=1).broadcast_to([128, D]), "ld_s3")
            load(f3b2[:, :], a["L3_ffn_b2"], "ld_s3")
            load(gam[0:NP, :], row("L3_ffn_gamma", NP), "ld_s3")
            load(bet[0:NP, :], row("L3_ffn_beta", NP), "ld_s3")
            for e in range(2):
                for half in range(2):
                    f2_load(of(e), e, half)
            f3_load(of(2), 2)
            f3_load(of(3), 3)
            with sp.Fori(1, X2 // 2) as i:
                for b in range(2):
                    sp.wait_ge(sem("f2_hid_mm"), 4 * i + 2 * b - 2)
                    f2_load(at(2 * i + b), b, 0)
                    sp.wait_ge(sem("f2_out_mm"), 2 * i + b - 1)
                    f2_load(at(2 * i + b), b, 1)
            sp.wait_ge(sem("f2_out_mm"), X2)
            f3_load(of(0), 0)
            f3_load(of(1), 1)
            sp.wait_ge(sem("scattered"), 16 * 2 * T)

            def slot3(ap, j):
                return ap.rearrange("(j p) n -> j p n", p=128)[bass.ds(j, 1)].rearrange("a p n -> (a p) n")

            def f3_slot(j, b):
                if isinstance(j, int):
                    if j + 4 < J3:
                        sp.wait_ge(sem("xg_mm"), j + 1)
                        sp.dma_start(xg[:, b, :], rows3[(j + 4) * 128:(j + 5) * 128, :]).then_inc(sem(f"ld_xg{b}"), 16)
                    if j + 4 < X3:
                        sp.wait_ge(sem("f3_out_mm"), j + 1)
                        f3_load(of(j + 4), b)
                    sp.wait_ge(sem("f3_out_ev"), T + j + 1)
                    sp.dma_start(outs3[j * 128:(j + 1) * 128, :], yo[:, b, :]).then_inc(sem(f"st_y{b}"), 16)
                    return
                sp.wait_ge(sem("xg_mm"), j + 1)
                sp.dma_start(xg[:, b, :], slot3(rows3, j + 4)).then_inc(sem(f"ld_xg{b}"), 16)
                sp.wait_ge(sem("f3_out_mm"), j + 1)
                f3_load(at(j + 4), b)
                sp.wait_ge(sem("f3_out_ev"), j + T + 1)
                sp.dma_start(slot3(outs3, j), yo[:, b, :]).then_inc(sem(f"st_y{b}"), 16)

            for b in range(4):
                sp.dma_start(xg[:, b, :], rows3[b * 128:(b + 1) * 128, :]).then_inc(sem(f"ld_xg{b}"), 16)
            with sp.Fori(0, X3 // 4 - 1) as i:
                for b in range(4):
                    f3_slot(4 * i + b, b)
            for j in range(X3 - 4, J3):
                f3_slot(j, j % 4)
            for t in range(T):
                sp.wait_ge(sem("x_final"), t + 1)
                sp.dma_start(out[tile(t), :], x[0:NP, t, :]).then_inc(sem("stored"), 16)
            sp.wait_ge(sem("stored"), 16 * T)

        @block.gpsimd
        def _(pool):
            pool.iota(iota[:, :], pattern=[[1, SL]], base=0, channel_multiplier=0,
                      allow_small_or_imprecise_dtypes=True).then_inc(sem("c_iota"), 1)
            pool.iota(node[:, :], pattern=[[NP, T]], base=0, channel_multiplier=1,
                      allow_small_or_imprecise_dtypes=True).then_inc(sem("c_iota"), 1)
            pool.iota(desc[:, :], pattern=[[-1, X3]], base=X3, channel_multiplier=0,
                      allow_small_or_imprecise_dtypes=True).then_inc(sem("c_iota"), 1)
            pool.memset(ones[:, :], 1.0).then_inc(sem("c_set"), 1)
            pool.memset(onesb[:, :], 1.0).then_inc(sem("c_set"), 1)
            pool.memset(zerob[:, :], 0.0).then_inc(sem("c_set"), 1)
            pool.memset(epsc[:, :], EPS).then_inc(sem("c_set"), 1)
            pool.memset(haug[:, :, :, :], 0.0).then_inc(sem("haug0"), 1)
            pool.wait_ge(sem("haug0"), 1)
            pool.memset(haug[:, :, :, :].rearrange("p t h c -> p t (h c)")[:, :, 4:4 * 20:25], 1.0).then_inc(sem("c_set"), 1)
            pool.memset(digc[:, :], -0.5 * (BASE - 1) / BASE).then_inc(sem("c_set"), 1)
            pool.memset(AHB[:, T * N:], 0.0).then_inc(sem("c_set"), 1)
            pool.memset(AT[:, :, :], 0.0).then_inc(sem("c_set"), 1)
            pool.memset(h2[:, :, :], 0.0).then_inc(sem("zeros"), 1)

            pool.wait_ge(sem("c_set"), 8)
            for g, group in enumerate(GROUPS):
                C, sums = (AT, BT)[group[0]], sums2[g % 2]
                pool.wait_ge(sem("high"), 2 * g + 2)
                nc.gpsimd.tensor_tensor(sums[0:NP, :, :], sums[0:NP, :, :], nhigh[0:NP, :, :], ALU.add
                                        ).then_inc(sem("low"), 1)
                nc.gpsimd.tensor_tensor(C[0:NP, :, HALF:N], C[0:NP, :, HALF:N], high[0:NP, :, 0:N - HALF], ALU.add
                                        ).then_inc(sem("counted"), 1)
                pool.wait_ge(sem("low"), g + 1)
                nc.gpsimd.tensor_tensor(C[0:NP, :, 0:HALF], C[0:NP, :, 0:HALF], sums[0:NP, :, :], ALU.add
                                        ).then_inc(sem("counted"), 1)
            pool.wait_ge(sem("f1_out_mm"), T)
            for i, name in enumerate(("dst", "src")):
                pool.dma_start(rci[0:NP, i, :], a[name][0:N].rearrange("(a n) -> a n", a=1).broadcast_to([NP, N])
                               ).then_inc(sem("ld_rc"), 16)
            pool.wait_ge(sem("zeroed"), 16 * T)
            pool.wait_ge(sem("row3"), 1)
            for t in range(T):
                for c in range(2):
                    pool.indirect_dma_start(out=rows3,
                                            out_offset=bass.IndirectOffsetOnAxis(ap=row3[0:NP, c, t:t + 1], axis=0),
                                            in_=xn[0:NP, t, :], in_offset=None).then_inc(sem("scattered"), 16)
            pool.wait_ge(sem("id3"), 1)
            weights = a["L3_experts"].rearrange("e p n -> (e p) n")
            for k in range(OV3):
                j, b = X3 + k, (X3 + k) % 4
                pool.wait_ge(sem("f3_out_mm"), j - 3)
                pool.indirect_dma_start(out=F3W[:, b, :], out_offset=None, in_=weights,
                                        in_offset=bass.IndirectOffsetOnAxis(ap=id3[:, k:k + 1], axis=0)
                                        ).then_inc(sem(f"ld_more{b}"), 16)
            for b in range(4):
                pool.wait_ge(sem(f"st_y{b}"), 16 * len(range(b, J3, 4)))
            for t in range(T):
                for c in range(2):
                    pool.indirect_dma_start(out=yg[0:NP, t, c, :], out_offset=None, in_=outs3,
                                            in_offset=bass.IndirectOffsetOnAxis(ap=row3[0:NP, c, t:t + 1], axis=0)
                                            ).then_inc(sem(f"ld_yg{t}"), 16)

        @block.tensor
        def _(pe):
            def mm(o, l, r, k, last, **kw):
                return nc.tensor.matmul(o, l, r, start=(k == 0), stop=last, **kw)

            def count_edges(g):
                graph, parts, unroll, first, iters, before = GROUPS[g]

                def body(i, fresh):
                    for j in range(unroll):
                        pe.wait_ge(sem("oh_ready"), 2 * (i * unroll + j) + 2 * before + 2)
                        for k, (m, b) in enumerate(BANKS[g % 2]):
                            start = fresh and j == 0
                            if start and g > 1 and k == 0:
                                pe.wait_ge(sem("flushed"), T * (g - 1))
                            if start and g and k == 3:
                                pe.wait_ge(sem("flushed"), T * (g - 1) + 2)
                            last = nc.tensor.matmul(ps[:, b, 0:HALF], oh_s[0:parts, j, m * NP:m * NP + 128],
                                                    oh_d[0:parts, j, 0:HALF], start=start, stop=False,
                                                    skip_group_check=True)
                        last.then_inc(sem("oh_free"), 1)

                body(0, True)
                if iters > 1:
                    with pe.Fori(1, iters) as i:
                        body(i, False)
                for m, b in BANKS[g % 2]:
                    last = nc.tensor.matmul(ps[:, b, 0:2], zerob[0:1, 0:128], zerob[0:1, 0:2], start=False,
                                            stop=True, skip_group_check=True)
                last.then_inc(sem("count_mm"), 1)

            turned = [0]

            def turn():
                n = turned[0]
                turned[0] += 1
                for t in range(T):
                    pe.wait_ge(sem("xn"), T * XN_OF_TURN[n] + t + 1)
                    for k in range(KD):
                        o = ps[:, k, t * NP:(t + 1) * NP] if t < 4 else ps[:, 2, k * NP:(k + 1) * NP]
                        last = nc.tensor.transpose(o, xn[0:NP, t, k * 128:(k + 1) * 128], ident[0:NP, 0:NP])
                    if t >= 3:
                        last.then_inc(sem("turn_mm"), 1)
                pe.wait_ge(sem("turn_a"), 2 * n + 2)
                pe.wait_ge(sem("turn_v"), n + 1)

            def agg_cols(rhs_rows, s, b0=0):
                for m in range(KD):
                    for q, (c, n) in enumerate(PIECES):
                        for t in range(T):
                            last = mm(ps[:, b0 + 2 * m + q, 0:n], rhs_rows[0:NP, t, m * 128:(m + 1) * 128],
                                      Ahat[0:NP, t, c:c + n], t, t == T - 1)
                        last.then_inc(sem(s), 1)

            def agg_rows(A, rhs_rows, s, b0=0):
                for t in range(T):
                    for k in range(T):
                        last = mm(ps[0:NP, b0 + t, 0:D], A[0:NP, k, tile(t)], rhs_rows[0:NP, k, :], k, k == T - 1)
                    last.then_inc(sem(s), 1)

            def lin_cols(W, XT, K, M, s, ring=8, b0=0, wait=None, n0=0):
                for m in range(M):
                    for q, (c, n) in enumerate(PIECES):
                        u = n0 + 2 * m + q
                        if wait and u >= ring:
                            pe.wait_ge(sem(wait), u - ring + 1)
                        for k in range(K):
                            last = mm(ps[:, b0 + u % ring, 0:n], W[:, k, m * 128:(m + 1) * 128], XT[:, k, c:c + n],
                                      k, k == K - 1)
                        last.then_inc(sem(s), 1)

            def lin_rows(XT, W, K, n, s, b0=0, ring=8, wait=None, n0=0):
                for t in range(T):
                    u = n0 + t
                    if wait and u >= ring:
                        pe.wait_ge(sem(wait), u - ring + 1)
                    for k in range(K):
                        last = mm(ps[0:NP, b0 + u % ring, 0:n], XT[:, k, tile(t)], W[:, k, 0:n], k, k == K - 1)
                    last.then_inc(sem(s), 1)

            pe.wait_ge(sem("c_set"), 3)
            pe.wait_ge(sem("c_mat"), 3)
            for g in range(GALL):
                if g == GA + 1:
                    pe.wait_ge(sem("counted"), 2 * GA)
                    pe.wait_ge(sem("flushed"), T * GA)
                    b = BANKS[g % 2][0][1]
                    for q, (c, n) in enumerate(PIECES):
                        for t in range(T):
                            mm(ps[0:NP, b + q, 0:n], ones[0:NP, 0:NP], AT[0:NP, t, c:c + n], t, t == T - 1)
                    for d in range(T):
                        for t in range(T):
                            last = mm(ps[0:NP, b + 2, d:d + 1], AT[0:NP, t, tile(d)], ones[0:NP, 0:1], t, t == T - 1)
                    last.then_inc(sem("deg_mm"), 1)
                    pe.wait_ge(sem("deg_ev"), 4)
                count_edges(g)
            pe.wait_ge(sem("flushed"), T * GALL)

            pe.wait_ge(sem("xn"), T)
            pe.wait_ge(sem("ahat"), T)
            agg_cols(xn, "g0a_mm")
            pe.wait_ge(sem("g0a_ev"), 4)
            pe.wait_ge(sem("ld_g0"), 64)
            lin_cols(W01, aggT, KD, 4, "g0b_mm")
            pe.wait_ge(sem("g0b_ev"), 8)
            lin_rows(h1T, W02, 4, D, "g0c_mm")
            pe.wait_ge(sem("g0c_ev"), T)

            def turn_mask(ds):
                for d in ds:
                    for t in range(T):
                        last = nc.tensor.transpose(psb[0:NP, 5 + d % 3, t * (NP + 1):t * (NP + 1) + NP],
                                                   maskb[0:NP, t, tile(d)], identb[0:NP, 0:NP])
                last.then_inc(sem("mask_mm"), 1)

            pe.wait_ge(sem("maskb"), T)
            turn_mask((0, 1, 2))
            agg_rows(Ahat, h2, "g0d_mm")
            pe.wait_ge(sem("bneg"), 2)
            turn_mask((3, 4))

            def row_of(c4, h, t):
                o = ps[0:NP, 2 * h, tile(t)] if t < 4 else ps[0:NP, 2 * h + 1, 0:NP]
                return nc.tensor.matmul(o, c4[0:NP, t, h:h + 1].broadcast_to([NP, NP]), ident[0:NP, 0:NP],
                                        start=True, stop=True)

            turn()
            pe.wait_ge(sem("ld_gat"), 96)
            for t in range(T):
                for k in range(KD):
                    last = mm(ps[0:NP, 3, t * 16:(t + 1) * 16], xnT[:, k, tile(t)], Wg[:, k, :], k, k == KD - 1)
            last.then_inc(sem("gat_h_mm"), 1)
            pe.wait_ge(sem("asd"), 1)
            for h in range(HEADS):
                for t in range(T):
                    last = row_of(asd[:, 0, :, :], h, t)
                last.then_inc(sem("arow_mm"), 1)
            pe.wait_ge(sem("arow_ev"), HEADS)
            pe.wait_ge(sem("ld_f0"), 80)
            for e in range(2):
                lin_cols(FW1[e], xnT, KD, 4, "f0_hid_mm", ring=4, wait="f0_hid_ev", n0=8 * e)
            pe.wait_ge(sem("f0_hid_ev"), 16)
            pe.wait_ge(sem("pq"), 1)
            for i in range(2):
                for h in range(HEADS):
                    if i:
                        pe.wait_ge(sem("pqrow_ev"), h + 1)
                    for t in range(T):
                        last = row_of(asd[:, 4 + i, :, :], h, t)
                    last.then_inc(sem("pqrow_mm"), 1)
            pe.wait_ge(sem("pqrow_ev"), 8)
            for h in range(HEADS):
                for t in range(T):
                    pe.wait_ge(sem("ee"), T * h + t + 1)
                    for q, (c, n) in enumerate(PIECES):
                        last = nc.tensor.matmul(ps[0:20, 6 + q, 0:n], haug[0:NP, t, h, :], EE[0:NP, h % 2, t, c:c + n],
                                                start=(h == 0 and t == 0), stop=(h == HEADS - 1 and t == T - 1))
                last.then_inc(sem("gat_mm"), 1)
            pe.wait_ge(sem("gatT_ev"), 2)
            pe.wait_ge(sem("gat_mm"), HEADS)
            for d in range(T):
                last = nc.tensor.transpose(ps[0:NP, 5, d * 20:(d + 1) * 20], gatT[:, tile(d)], ident[0:20, 0:20])
            last.then_inc(sem("gat_mm"), 1)
            lin_cols(FW1[2], xnT, KD, 4, "f0_hid_mm", ring=4, wait="f0_hid_ev", n0=16)
            pe.wait_ge(sem("f0_hid_ev"), 24)
            pe.wait_ge(sem("gate"), 1)
            for t in range(T):
                last = nc.tensor.transpose(ps[0:X0, t // 4, (t % 4) * NP:(t % 4 + 1) * NP], gate[0:NP, t, 0:X0],
                                           ident[0:NP, 0:NP])
            last.then_inc(sem("gT_mm"), 1)
            pe.wait_ge(sem("gT_ev"), 2)
            pe.wait_ge(sem("ld_f0"), 80)
            for t in range(T):
                if t == 4:
                    pe.wait_ge(sem("f0_out_ev"), 1)
                nc.tensor.matmul(ps[0:NP, 4 + t % 4, 0:D], gT[0:X0, tile(t)], f0b2[:, :], start=True, stop=True
                                 ).then_inc(sem("f0_out_mm"), 1)
            for e in range(X0 + 1):
                if 3 <= e < X0:
                    lin_cols(FW1[e], xnT, KD, 4, "f0_hid_mm", ring=4, wait="f0_hid_ev", n0=8 * e)
                if e >= 1:
                    pe.wait_ge(sem("f0_hid_ev"), 8 * e)
                    lin_rows(hh[(e - 1) % 3], FW2[e - 1], 4, D, "f0_out_mm", b0=4, ring=4,
                             wait="f0_out_ev", n0=T * e)

            pe.wait_ge(sem("xn"), 3 * T)
            agg_cols(xn, "g1a_mm")
            pe.wait_ge(sem("ld_g1"), 80)
            pe.wait_ge(sem("g1a_ev"), 4)
            lin_cols(Wc[:, 0, :, :], aggT, KD, 2, "g1b_mm", b0=4, ring=4)
            pe.wait_ge(sem("g1b_ev"), 4)
            lin_rows(h1T, Wc[:, 1, :, :], KD, D, "g1c_mm")
            pe.wait_ge(sem("g1c_ev"), T)
            agg_cols(h2, "g1d_mm")
            pe.wait_ge(sem("g1d_ev"), 4)
            lin_rows(aggT, Wc[:, 2, :, :], KD, D, "g1e_mm")
            pe.wait_ge(sem("g1e_ev"), T)
            agg_rows(Ahat, h2, "g1f_mm")

            turn()
            pe.wait_ge(sem("ld_g1"), 80)
            for q, (c, n) in enumerate(PIECES):
                for k in range(KD):
                    last = mm(ps[0:NP, 4 + q, 0:n], wr[:, k:k + 1].broadcast_to([128, NP]), xnT[:, k, c:c + n],
                              k, k == KD - 1)
            last.then_inc(sem("wrow_mm"), 1)
            pe.wait_ge(sem("ld_f1"), 48)
            lin_cols(M1, xnT, KD, 8, "f1_hid_mm", ring=4, wait="f1_hid_ev")
            pe.wait_ge(sem("f1_hid_ev"), 16)
            pe.wait_ge(sem("wrow_ev"), 2)
            lin_rows(hT, M2, 8, D, "f1_out_mm")

            turn()
            pe.wait_ge(sem("ld_late"), 16 * (3 + X2))
            lin_rows(xnT, Wsn, KD, 2 * D, "g2a_mm", b0=3, ring=5)
            pe.wait_ge(sem("hn"), T)
            for s in range(T):
                pe.wait_ge(sem("hs"), s + 1)
                for t in range(T):
                    last = mm(ps[0:NP, t, 0:D], AT[0:NP, s, tile(t)], hn[0:NP, s, :], s, s == T - 1)
                    if s == T - 1:
                        last.then_inc(sem("g2b_mm"), 1)

            turn()
            pe.wait_ge(sem("ld_s2"), 32)
            for t in range(T):
                for k in range(KD):
                    last = mm(ps[0:NP, 3, t * X2:(t + 1) * X2], xnT[:, k, tile(t)], G2[:, k, :], k, k == KD - 1)
            last.then_inc(sem("lg2_mm"), 1)
            pe.wait_ge(sem("ohb"), 1)
            for t in range(T):
                for s in range(t + 1):
                    last = mm(ps[0:NP, 4, t * X2:(t + 1) * X2], (tri if s == t else onesb)[0:NP, 0:NP],
                              ohb[0:NP, s, :], s, s == t)
            last.then_inc(sem("pos_mm"), 1)
            pe.wait_ge(sem("slot"), 1)
            for t in range(T):
                o = ps[0:NP, 5, tile(t)] if t < 4 else ps[0:NP, 6, 0:NP]
                last = nc.tensor.matmul(o, slot[0:NP, t:t + 1].broadcast_to([NP, NP]), ident[0:NP, 0:NP],
                                        start=True, stop=True)
            last.then_inc(sem("srow_mm"), 1)
            pe.wait_ge(sem("sc"), T)
            for m in range(KD):
                for q in range(2):
                    for t in range(T):
                        last = mm(ps[:, 2 * m + q, 0:SL // 2], xn[0:NP, t, m * 128:(m + 1) * 128],
                                  SC[0:NP, t, q * (SL // 2):(q + 1) * (SL // 2)], t, t == T - 1)
                    last.then_inc(sem("disp_mm"), 1)
            pe.wait_ge(sem("disp_ev"), 4)
            pe.wait_ge(sem("srow_ev"), 2)

            def f2_hid(e, b):
                pe.wait_ge(sem(f"ld_f2w{b}0"), 8 * (e - b) + 16)
                for m in range(8):
                    for k in range(KD):
                        last = mm(ps[:, 2 * b + m // 4, (m % 4) * CAP:(m % 4 + 1) * CAP],
                                  F2W1[b][:, k, m * 128:(m + 1) * 128], XbT[:, k, bass.ds(e * CAP, CAP)],
                                  k, k == KD - 1)
                    if m % 4 == 3:
                        last.then_inc(sem("f2_hid_mm"), 1)

            def f2_out(e, b):
                pe.wait_ge(sem(f"ld_f2w{b}1"), 8 * (e - b) + 16)
                pe.wait_ge(sem("f2_hid_ev"), 8 * e + 8)
                for k in range(8):
                    last = mm(ps[0:CAP, 4 + b, 0:D], hTe[:, b, k, :], F2W2[b][:, k, :], k, k == 7)
                last.then_inc(sem("f2_out_mm"), 1)

            f2_hid(0, 0)
            f2_hid(1, 1)
            f2_out(0, 0)
            with pe.Fori(1, X2 // 2) as i:
                f2_hid(2 * i, 0)
                pe.wait_ge(sem("f2_out_ev"), 2 * i - 1)
                f2_out(2 * i - 1, 1)
                f2_hid(2 * i + 1, 1)
                pe.wait_ge(sem("f2_out_ev"), 2 * i)
                f2_out(2 * i, 0)
            f2_out(X2 - 1, 1)
            pe.wait_ge(sem("f2_out_ev"), X2)
            pe.wait_ge(sem("st"), X2)
            for t in range(T):
                for e in range(X2):
                    last = mm(ps[0:NP, t, 0:D], ST[0:CAP, e, tile(t)], ybuf[0:CAP, e, :], e, e == X2 - 1)
                last.then_inc(sem("comb_mm"), 1)

            turn()
            pe.wait_ge(sem("w3"), 2)
            lin_rows(xnT, W3, KD, W3C, "g3a_mm", b0=3, ring=5)
            pe.wait_ge(sem("g3a_ev"), T)
            pe.wait_ge(sem("gcr"), 2 * T)
            for t in range(T):
                for s in range(T):
                    mm(ps[0:NP, t, 0:D + HEADS], Gc[0:NP, s, tile(t)], xt[0:NP, s, 0:D + HEADS], s, s == T - 1,
                       skip_group_check=True)
                for s in range(T):
                    last = nc.tensor.matmul(ps[0:NP, t, D:D + HEADS], Gr[0:NP, s, tile(t)], xt[0:NP, s, D + HEADS:W3C],
                                            start=False, stop=(s == T - 1), skip_group_check=True)
                last.then_inc(sem("g3b_mm"), 1)

            turn()
            pe.wait_ge(sem("ld_s3"), 112)
            for t in range(T):
                for k in range(KD):
                    last = mm(ps[0:NP, 3, t * X3:(t + 1) * X3], xnT[:, k, tile(t)], G3[:, k, :], k, k == KD - 1)
            last.then_inc(sem("lg3_mm"), 1)
            pe.wait_ge(sem("m3b"), 1)
            for t in range(T):
                for s in range(t + 1):
                    mm(ps[:, 4, t * X3:(t + 1) * X3], (tri if s == t else onesb)[0:NP, :], m3b[0:NP, s, :], s, s == t)
            for s in range(T):
                last = mm(ps[:, 4, 128:128 + X3], onesb[0:NP, :], m3b[0:NP, s, :], s, s == T - 1)
            last.then_inc(sem("rank_mm"), 1)
            pe.wait_ge(sem("gate"), 2)
            for t in range(T):
                last = nc.tensor.transpose(ps[0:X3, t // 4, (t % 4) * NP:(t % 4 + 1) * NP], gate[0:NP, t, :],
                                           ident[0:NP, 0:NP])
            last.then_inc(sem("gT_mm"), 1)
            pe.wait_ge(sem("gT_ev"), 4)
            for t in range(T):
                last = nc.tensor.matmul(ps[0:NP, 5 + t // 2, (t % 2) * D:(t % 2 + 1) * D], gT[:, tile(t)],
                                        f3b2[:, :], start=True, stop=True)
            last.then_inc(sem("f3_bias_mm"), 1)

            def f3_rows(j, s, b):
                pe.wait_ge(sem(f"ld_xg{b}"), 4 * (j - b) + 16)
                if not (isinstance(j, int) and j < 2):
                    pe.wait_ge(sem("xgT_ev"), j - 1)
                for k in range(KD):
                    last = nc.tensor.transpose(ps[:, s, k * 128:(k + 1) * 128], xg[:, b, k * 128:(k + 1) * 128],
                                               ident[:, :])
                last.then_inc(sem("xg_mm"), 1)

            def f3_hid(j, s, b, first):
                if first:
                    pe.wait_ge(sem(f"ld_f3w{b}"), 4 * (j - b) + 16)
                else:
                    pe.wait_ge(sem(f"ld_more{b}"), 4 * (j - b) + (16 - 4 * X3))
                pe.wait_ge(sem("xgT_ev"), j + 1)
                if not (isinstance(j, int) and j < 2):
                    pe.wait_ge(sem("f3_hid_ev"), 4 * j - 4)
                for m in range(4):
                    for k in range(KD):
                        last = mm(ps[:, 2 + 4 * s + m // 2, (m % 2) * 128:(m % 2 + 1) * 128],
                                  F3W1[b][:, k, m * 128:(m + 1) * 128],
                                  xgT[:, s, k, :], k, k == KD - 1)
                    if m % 2:
                        last.then_inc(sem("f3_hid_mm"), 1)

            def f3_out(j, s, b):
                pe.wait_ge(sem("f3_out_ev"), j + T - 1)
                for k in range(4):
                    pe.wait_ge(sem("f3_hid_ev"), 4 * j + k + 1)
                    last = mm(ps[:, 4 + s, 0:D], hx[:, s, k, :], F3W2[b][:, k, :], k, k == 3)
                last.then_inc(sem("f3_out_mm"), 1)

            def f3_step(j, b, first):
                if not isinstance(j, int) or j + 1 < J3:
                    f3_rows(j + 1, (b + 1) % 2, (b + 1) % 4)
                f3_hid(j, b % 2, b, first)
                if not isinstance(j, int) or j:
                    f3_out(j - 1, (b + 1) % 2, (b + 3) % 4)

            pe.wait_ge(sem("f3_out_ev"), T)
            f3_rows(0, 0, 0)
            for j in range(4):
                f3_step(j, j, True)
            with pe.Fori(1, X3 // 4) as i:
                for b in range(4):
                    f3_step(4 * i + b, b, True)
            with pe.Fori(X3 // 4, J3 // 4) as i:
                for b in range(4):
                    f3_step(4 * i + b, b, False)
            for j in range(J3 // 4 * 4, J3):
                f3_step(j, j % 4, False)
            f3_out(J3 - 1, (J3 - 1) % 2, (J3 - 1) % 4)

        @block.scalar
        def _(act):
            def std(n):
                for t in range(T):
                    std_tile(n, t)

            def std_tile(n, t):
                act.wait_ge(sem("ln_var"), T * n + t + 1)
                nc.scalar.activation(sd[0:NP, t:t + 1], mv[0:NP, t, 1:2], ACT.Sqrt, bias=epsc[0:NP, :]
                                     ).then_inc(sem("ln_std"), 1)

            turned = [0]

            def turn():
                n = turned[0]
                turned[0] += 1
                act.wait_ge(sem("turn_mm"), 2 * n + 1)
                nc.scalar.copy(xnT[:, 0, 0:4 * NP], ps[:, 0, 0:4 * NP]).then_inc(sem("turn_a"), 1)
                act.wait_ge(sem("turn_mm"), 2 * n + 2)
                nc.scalar.copy(xnT[:, :, 4 * NP:N], ps[:, 2, 0:2 * NP].rearrange("p (k n) -> p k n", k=2)
                               ).then_inc(sem("turn_a"), 1)

            def flush(g):
                sums = sums2[g % 2]
                act.wait_ge(sem("count_mm"), g + 1)
                for i, (m, b) in enumerate(sorted(BANKS[g % 2], key=lambda mb: mb[1])):
                    if i == 2 and g == GA:
                        degrees()
                    nc.scalar.copy(sums[0:NP, m, :], ps[0:NP, b, 0:HALF]).then_inc(sem("flushed"), 1)
                act.wait_ge(sem("flushed"), T * (g + 1))
                nc.scalar.activation(highi[0:NP, :, :], sums[0:NP, :, :], ACT.Identity, scale=1.0 / BASE,
                                     bias=digc[0:NP, :]).then_inc(sem("rounded"), 1)
                act.wait_ge(sem("rounded"), g + 1)
                if g:
                    act.wait_ge(sem("counted"), 2 * g)
                nc.scalar.activation(nhigh[0:NP, :, :], highi[0:NP, :, :], ACT.Copy, scale=-float(BASE)
                                     ).then_inc(sem("high"), 1)
                nc.scalar.copy(high[0:NP, :, :], highi[0:NP, :, :]).then_inc(sem("high"), 1)

            def degrees():
                act.wait_ge(sem("deg_mm"), 1)
                b = BANKS[(GA + 1) % 2][0][1]
                for q, (c, n) in enumerate(PIECES):
                    nc.scalar.activation(dinvr[0:NP, c:c + n], ps[0:NP, b + q, 0:n], ACT.Sqrt, bias=ones[0:NP, 0:1]
                                         ).then_inc(sem("deg_ev"), 1)
                nc.scalar.activation(dinvc[0:NP, :], ps[0:NP, b + 2, 0:T], ACT.Sqrt, bias=ones[0:NP, 0:1]
                                     ).then_inc(sem("deg_ev"), 1)
                nc.scalar.copy(rdeg[0:NP, :], ps[0:NP, b + 2, 0:T]).then_inc(sem("deg_ev"), 1)

            act.wait_ge(sem("c_set"), 8)
            for g in range(GALL):
                flush(g)
                if GA + 2 <= g < GA + 2 + T:
                    std_tile(0, g - GA - 2)

            def drain_cols(mm_sem, ev_sem, dst, func=ACT.Copy, bias=None, M=KD, b0=0):
                for m in range(M):
                    for q, (c, n) in enumerate(PIECES):
                        act.wait_ge(sem(mm_sem), 2 * m + q + 1)
                        kw = {} if bias is None else {"bias": bias[:, m:m + 1]}
                        nc.scalar.activation(dst[:, m, c:c + n], ps[:, b0 + 2 * m + q, 0:n], func, **kw
                                             ).then_inc(sem(ev_sem), 1)

            def drain_rows(mm_sem, ev_sem, dst, w, b0=0):
                for t in range(T):
                    act.wait_ge(sem(mm_sem), t + 1)
                    nc.scalar.copy(dst[0:NP, t, 0:w], ps[0:NP, b0 + t, 0:w]).then_inc(sem(ev_sem), 1)

            drain_cols("g0a_mm", "g0a_ev", aggT)
            act.wait_ge(sem("ld_g0"), 64)
            drain_cols("g0b_mm", "g0b_ev", h1T, ACT.Relu, b01, M=4)
            drain_rows("g0c_mm", "g0c_ev", h2, D)

            std(1)
            turn()
            for h in range(HEADS):
                act.wait_ge(sem("arow_mm"), h + 1)
                nc.scalar.copy(arow[0:NP, h, 0:4 * NP], ps[0:NP, 2 * h, 0:4 * NP])
                nc.scalar.copy(arow[0:NP, h, 4 * NP:N], ps[0:NP, 2 * h + 1, 0:NP]).then_inc(sem("arow_ev"), 1)

            def f0_drain(e, units=range(8)):
                for i in units:
                    m, (c, n) = i // 2, PIECES[i % 2]
                    act.wait_ge(sem("f0_hid_mm"), 8 * e + i + 1)
                    nc.scalar.activation(hh[e % 3][:, m, c:c + n], ps[:, i % 4, 0:n], ACT.Gelu,
                                         bias=f0b1[:, 4 * e + m:4 * e + m + 1]).then_inc(sem("f0_hid_ev"), 1)

            act.wait_ge(sem("ld_f0"), 80)
            f0_drain(0)
            f0_drain(1)
            for i, r in enumerate((prow, qrow)):
                for h in range(HEADS):
                    act.wait_ge(sem("pqrow_mm"), 4 * i + h + 1)
                    nc.scalar.copy(r[0:NP, h, 0:4 * NP], ps[0:NP, 2 * h, 0:4 * NP])
                    nc.scalar.copy(r[0:NP, h, 4 * NP:N], ps[0:NP, 2 * h + 1, 0:NP]).then_inc(sem("pqrow_ev"), 1)
            act.wait_ge(sem("pqrow_ev"), 8)
            for i in range(HEADS * T):
                h, t = i // T, i % T
                if i >= 2:
                    act.wait_ge(sem("ee"), i - 1)
                nc.scalar.activation(up[0:NP, i % 2, :], prow[0:NP, h, :], ACT.Exp, bias=asd[0:NP, 0, t, h:h + 1]
                                     ).then_inc(sem("ev"), 1)
                nc.scalar.activation(uq[0:NP, i % 2, :], qrow[0:NP, h, :], ACT.Exp, bias=asd[0:NP, 6, t, h:h + 1]
                                     ).then_inc(sem("ev"), 1)
            act.wait_ge(sem("gat_mm"), HEADS)
            for q, (c, n) in enumerate(PIECES):
                nc.scalar.copy(gatT[:, c:c + n], ps[0:20, 6 + q, 0:n]).then_inc(sem("gatT_ev"), 1)
            f0_drain(2, range(0, 2))
            act.wait_ge(sem("var16"), 1)
            nc.scalar.activation(sca[0:NP, 2, :], sca[0:NP, 1, :], ACT.Sqrt, scale=1.0 / 16, bias=epsc[0:NP, :]
                                 ).then_inc(sem("std16"), 1)
            f0_drain(2, range(2, 5))
            act.wait_ge(sem("to_exp"), 1)
            nc.scalar.activation(sca[0:NP, 8, :], sca[0:NP, 7, :], ACT.Exp).then_inc(sem("exped"), 1)
            f0_drain(2, range(5, 8))
            act.wait_ge(sem("gT_mm"), 1)
            nc.scalar.copy(gT[0:X0, 0:4 * NP], ps[0:X0, 0, 0:4 * NP]).then_inc(sem("gT_ev"), 1)
            nc.scalar.copy(gT[0:X0, 4 * NP:N], ps[0:X0, 1, 0:NP]).then_inc(sem("gT_ev"), 1)
            for e in range(3, X0):
                act.wait_ge(sem("f0_out_mm"), T * (e - 1))
                f0_drain(e)

            std(2)
            drain_cols("g1a_mm", "g1a_ev", aggT)
            act.wait_ge(sem("ld_g1"), 80)
            drain_cols("g1b_mm", "g1b_ev", h1T, ACT.Gelu_apprx_tanh, bc12[0], b0=4)
            drain_rows("g1c_mm", "g1c_ev", h2, D)
            drain_cols("g1d_mm", "g1d_ev", aggT, ACT.Gelu_apprx_tanh, bc12[1])
            drain_rows("g1e_mm", "g1e_ev", h2, D)
            std(3)
            turn()
            act.wait_ge(sem("wrow_mm"), 1)
            act.wait_ge(sem("ld_g1"), 80)
            for q, (c, n) in enumerate(PIECES):
                nc.scalar.activation(wrow[0:NP, c:c + n], ps[0:NP, 4 + q, 0:n], ACT.Identity, bias=br[0:NP, :]
                                     ).then_inc(sem("wrow_ev"), 1)
            for m in range(8):
                for q, (c, n) in enumerate(PIECES):
                    u = 2 * m + q
                    act.wait_ge(sem("f1_hid_mm"), u + 1)
                    nc.scalar.activation(hT[:, m, c:c + n], ps[:, u % 4, 0:n], ACT.Gelu_apprx_tanh,
                                         bias=m1b[:, m:m + 1]).then_inc(sem("f1_hid_ev"), 1)
            std(4)
            turn()
            for t in range(T):
                act.wait_ge(sem("g2a_v"), t + 1)
                nc.scalar.copy(hn[0:NP, t, :], ps[0:NP, 3 + t, D:2 * D]).then_inc(sem("hn"), 1)
            std(5)
            turn()
            act.wait_ge(sem("to_exp"), 2)
            nc.scalar.activation(scr[0:NP, 1, :, 0:X2], scr[0:NP, 0, :, 0:X2], ACT.Exp).then_inc(sem("exped"), 1)
            act.wait_ge(sem("srow_mm"), 1)
            nc.scalar.copy(srow[0:NP, 0:4 * NP], ps[0:NP, 5, 0:4 * NP]).then_inc(sem("srow_ev"), 1)
            nc.scalar.copy(srow[0:NP, 4 * NP:N], ps[0:NP, 6, 0:NP]).then_inc(sem("srow_ev"), 1)
            for u in range(4):
                act.wait_ge(sem("disp_mm"), u + 1)
                nc.scalar.copy(XbT[:, u // 2, (u % 2) * (SL // 2):(u % 2 + 1) * (SL // 2)], ps[:, u, 0:SL // 2]
                               ).then_inc(sem("disp_ev"), 1)
            act.wait_ge(sem("ld_s2"), 32)

            def f2_drain(e, b, first):
                nc.scalar.copy(bnow[:, b, :], f2b1[:, bass.ds(8 * e, 8)]).then_inc(sem("f2_bias"), 1)
                act.wait_ge(sem("f2_bias"), e + 1)
                if not first:
                    act.wait_ge(sem("f2_out_mm"), e - 1)
                for m in range(8):
                    if m % 4 == 0:
                        act.wait_ge(sem("f2_hid_mm"), 2 * e + m // 4 + 1)
                    nc.scalar.activation(hTe[:, b, m, :], ps[:, 2 * b + m // 4, (m % 4) * CAP:(m % 4 + 1) * CAP],
                                         ACT.Relu, bias=bnow[:, b, m:m + 1]).then_inc(sem("f2_hid_ev"), 1)

            for b in range(2):
                f2_drain(b, b, True)
            with act.Fori(1, X2 // 2) as i:
                for b in range(2):
                    f2_drain(2 * i + b, b, False)
            std(6)
            turn()
            drain_rows("g3a_mm", "g3a_ev", xt, W3C, b0=3)
            act.wait_ge(sem("to_exp"), 3)
            nc.scalar.activation(z3[0:NP, 1, :, :], z3[0:NP, 0, :, :], ACT.Exp).then_inc(sem("exped"), 1)
            std(7)
            turn()
            act.wait_ge(sem("to_exp"), 4)
            nc.scalar.activation(sca[0:NP, 8, :], sca[0:NP, 7, :], ACT.Exp).then_inc(sem("exped"), 1)
            act.wait_ge(sem("gT_mm"), 2)
            nc.scalar.copy(gT[0:X3, 0:4 * NP], ps[0:X3, 0, 0:4 * NP]).then_inc(sem("gT_ev"), 1)
            nc.scalar.copy(gT[0:X3, 4 * NP:N], ps[0:X3, 1, 0:NP]).then_inc(sem("gT_ev"), 1)

            def f3_drain(j, b):
                if not (isinstance(j, int) and j < 2):
                    act.wait_ge(sem("f3_out_mm"), j - 1)
                for m in range(4):
                    if m % 2 == 0:
                        act.wait_ge(sem("f3_hid_mm"), 2 * j + m // 2 + 1)
                    nc.scalar.activation(hx[:, b % 2, m, :],
                                         ps[:, 2 + 4 * (b % 2) + m // 2, (m % 2) * 128:(m % 2 + 1) * 128], ACT.Relu,
                                         bias=F3B1[b][:, m:m + 1]).then_inc(sem("f3_hid_ev"), 1)

            for j in range(4):
                f3_drain(j, j)
            with act.Fori(1, J3 // 4) as i:
                for b in range(4):
                    f3_drain(4 * i + b, b)
            for j in range(J3 // 4 * 4, J3):
                f3_drain(j, j % 4)
            for t in range(T):
                act.wait_ge(sem("y_var"), t + 1)
                nc.scalar.activation(sd[0:NP, t:t + 1], mv[0:NP, t, 1:2], ACT.Sqrt, bias=epsc[0:NP, :]
                                     ).then_inc(sem("y_std"), 1)

        @block.vector
        def _(dve):
            V = nc.vector
            chain = [0]

            def link(ins):
                chain[0] += 1
                ins.then_inc(sem("dve_chain"), 1)
                dve.wait_ge(sem("dve_chain"), chain[0])

            def link_all(instructions):
                for ins in instructions:
                    chain[0] += 1
                    ins.then_inc(sem("dve_chain"), 1)
                dve.wait_ge(sem("dve_chain"), chain[0])

            norms = [1]

            def norm(src, add=None):
                n = norms[0]
                norms[0] += 1
                for t in range(T + 1):
                    norm_tile(n, src, t, add)
                dve.wait_ge(sem("xn"), T * (n + 1))

            def norm_tile(n, src, t, add=None):
                if t < T:
                    if add is not None:
                        add(t)
                    link(V.bn_stats(st[0:NP, t, :], src[0:NP, t, :]))
                    V.bn_aggr(mv[0:NP, t, :], st[0:NP, t, :]).then_inc(sem("ln_var"), 1)
                if t >= 1:
                    u = t - 1
                    dve.wait_ge(sem("ln_var"), T * n + t)
                    dve.wait_ge(sem("ln_std"), T * n + t)
                    link(V.reciprocal(rs[0:NP, u:t], sd[0:NP, u:t]))
                    V.tensor_scalar(xn[0:NP, u, :], src[0:NP, u, :], mv[0:NP, u, 0:1], rs[0:NP, u:t],
                                    ALU.subtract, ALU.mult).then_inc(sem("xn"), 1)

            turned = [0]

            def turn():
                n = turned[0]
                turned[0] += 1
                dve.wait_ge(sem("turn_mm"), 2 * n + 1)
                V.tensor_copy(xnT[:, 1, 0:4 * NP], ps[:, 1, 0:4 * NP]).then_inc(sem("turn_v"), 1)

            def digits(parts, idf, idi):
                d, w = idf[0:parts, 1, :], idf[0:parts, 2, :]
                link(V.tensor_copy(d, idi[0:parts, 1, :]))
                link(V.tensor_scalar(w, d, float(HALF), float(BASE - 1), ALU.is_ge, ALU.mult))
                link(V.tensor_scalar(w, w, 1.0, None, ALU.add))
                link(V.scalar_tensor_tensor(out=w, in0=d, scalar=float(N), in1=w, op0=ALU.is_lt, op1=ALU.mult))
                h = digs[0:parts, 0:idf.shape[2]]
                link(V.tensor_scalar(h, d, float(HALF), float(-HALF), ALU.is_ge, ALU.mult))
                link(V.tensor_tensor(d, d, h, ALU.add))

            def one_hots(g, between):
                graph, parts, unroll, first, iters, before = GROUPS[g]
                idf = (idf1, idf2)[graph]

                def body(i, fresh):
                    for j in range(unroll):
                        if fresh and g and j == 0:
                            dve.wait_ge(sem("oh_free"), before)
                        elif not fresh:
                            dve.wait_ge(sem("oh_free"), i * unroll + (before + j + 1 - unroll))
                        V.tensor_scalar(oh_s[0:parts, j, 0:N + 3], iota[0:parts, 0:N + 3],
                                        idf[0:parts, 0, bass.ds(i * unroll + (first + j), 1)], None,
                                        ALU.is_equal).then_inc(sem("oh_ready"), 1)
                        V.tensor_scalar(oh_d[0:parts, j, 0:HALF], iota[0:parts, 0:HALF],
                                        idf[0:parts, 1, bass.ds(i * unroll + (first + j), 1)],
                                        idf[0:parts, 2, bass.ds(i * unroll + (first + j), 1)],
                                        ALU.is_equal, ALU.mult).then_inc(sem("oh_ready"), 1)

                body(0, g in (0, GA))
                cut = min(16 // unroll, iters)
                if cut > 1:
                    with dve.Fori(1, cut) as i:
                        body(i, False)
                between(g)
                if cut < iters:
                    with dve.Fori(cut, iters) as i:
                        body(i, False)

            def first_max(vals, E, oh, top, tmp):
                link(V.tensor_reduce(top, vals, AX.X, ALU.max))
                link(V.tensor_tensor(tmp, vals, top.unsqueeze(2).broadcast_to([NP, T, E]), ALU.is_equal))
                link(V.tensor_tensor(tmp, tmp, desc[0:NP, 0:E].unsqueeze(1).broadcast_to([NP, T, E]), ALU.mult))
                link(V.tensor_reduce(sca[0:NP, 15, :], tmp, AX.X, ALU.max))
                link(V.tensor_tensor(oh, tmp, sca[0:NP, 15, :].unsqueeze(2).broadcast_to([NP, T, E]), ALU.is_equal))

            def top2_gate(vals, E, n, chosen=None):
                oh1, oh2, tmp = (scr[0:NP, i, :, 0:E] for i in (3, 4, 5))
                first_max(vals, E, oh1, sca[0:NP, 5, :], tmp)
                link(V.scalar_tensor_tensor(out=scr[0:NP, 6, :, 0:E], in0=oh1, scalar=-3e38, in1=vals,
                                            op0=ALU.mult, op1=ALU.add))
                first_max(scr[0:NP, 6, :, 0:E], E, oh2, sca[0:NP, 6, :], tmp)
                if chosen is not None:
                    V.tensor_tensor(m3b[0:NP, :, :], oh1, oh2, ALU.add).then_inc(sem("m3b"), 1)
                    V.tensor_copy(chosen[:, 0, :, :], oh1)
                    V.tensor_copy(chosen[:, 1, :, :], oh2)
                V.tensor_tensor(sca[0:NP, 7, :], sca[0:NP, 6, :], sca[0:NP, 5, :], ALU.subtract).then_inc(sem("to_exp"), 1)
                dve.wait_ge(sem("exped"), n)
                link(V.tensor_scalar(sca[0:NP, 9, :], sca[0:NP, 8, :], 1.0, None, ALU.add))
                link(V.reciprocal(sca[0:NP, 10, :], sca[0:NP, 9, :]))
                link(V.tensor_tensor(sca[0:NP, 11, :], sca[0:NP, 8, :], sca[0:NP, 10, :], ALU.mult))
                V.tensor_tensor(oh1, oh1, sca[0:NP, 10, :].unsqueeze(2).broadcast_to([NP, T, E]), ALU.mult)
                link(V.tensor_tensor(oh2, oh2, sca[0:NP, 11, :].unsqueeze(2).broadcast_to([NP, T, E]), ALU.mult))
                V.tensor_tensor(gate[0:NP, :, 0:E], oh1, oh2, ALU.add).then_inc(sem("gate"), 1)

            dve.wait_ge(sem("c_iota"), 3)
            V.tensor_scalar(ident[:, :], iota[:, 0:128], node[:, 0:1], None, ALU.is_equal).then_inc(sem("c_mat"), 1)
            V.tensor_scalar(identb[:, :], iota[:, 0:128], node[:, 0:1], None, ALU.is_equal).then_inc(sem("c_mat"), 1)
            V.tensor_scalar(tri[:, :], iota[:, 0:128], node[:, 0:1], None, ALU.is_ge).then_inc(sem("c_mat"), 1)
            dve.wait_ge(sem("ld_edges1"), 32)
            link(V.tensor_copy(idf1[0:EP1, 0, :], idi1[0:EP1, 0, :]))
            digits(EP1, idf1, idi1)

            def between(g):
                if g == 1:
                    dve.wait_ge(sem("c_set"), 8)
                    dve.wait_ge(sem("ld_edges2"), 32)
                    digits(EP2, idf2, idi2)
                    link(V.tensor_scalar(idf2[0:EP2, 0, :], idi2[0:EP2, 0, :], float(N - 1), None, ALU.min))
                if g == GA + 1:
                    dve.wait_ge(sem("deg_ev"), 4)
                    V.tensor_scalar(dinvc[0:NP, :], dinvc[0:NP, :], 1.0, None, ALU.max)
                    V.tensor_scalar(rdeg[0:NP, :], rdeg[0:NP, :], 1.0, None, ALU.max)
                    link(V.tensor_scalar(dinvr[0:NP, :], dinvr[0:NP, :], 1.0, None, ALU.max))
                    V.reciprocal(dinvc[0:NP, :], dinvc[0:NP, :])
                    V.reciprocal(rdeg[0:NP, :], rdeg[0:NP, :])
                    link(V.reciprocal(dinvr[0:NP, :], dinvr[0:NP, :]))
                if g == GA + 2:
                    dve.wait_ge(sem("ld_x"), 16)
                if GA + 2 <= g <= GA + 2 + T:
                    norm_tile(0, x, g - GA - 2)
                if GA + 2 <= g < GA + 2 + T:
                    t = g - GA - 2
                    if t == 0:
                        dve.wait_ge(sem("zeroed"), 16 * T)
                    V.scalar_tensor_tensor(out=Ahat[0:NP, t, :], in0=AT[0:NP, t, :], scalar=dinvc[0:NP, t:t + 1],
                                           in1=dinvr[0:NP, :], op0=ALU.mult, op1=ALU.mult)
                    link(V.scalar_tensor_tensor(out=dtmp[0:NP, t, :], in0=ident[0:NP, 0:NP], scalar=dinvc[0:NP, t:t + 1],
                                                in1=dinvr[0:NP, tile(t)], op0=ALU.mult, op1=ALU.mult))
                    V.tensor_tensor(Ahat[0:NP, t, tile(t)], Ahat[0:NP, t, tile(t)], dtmp[0:NP, t, :], ALU.add
                                    ).then_inc(sem("ahat"), 1)

            for g in range(GALL):
                one_hots(g, between)
            dve.wait_ge(sem("counted"), 2 * GALL)
            for t in range(T):
                i = V.tensor_tensor(BT[0:NP, t, tile(t)], BT[0:NP, t, tile(t)], ident[0:NP, 0:NP], ALU.add)
            link(i)
            for t in range(T):
                V.tensor_scalar(maskb[0:NP, t, :], BT[0:NP, t, :], 1.0, None, ALU.min).then_inc(sem("maskb"), 1)

            def mask(ts):
                for t in ts:
                    V.tensor_scalar(Bneg[0:NP, t, :].rearrange("p (s c) -> p s c", c=NP),
                                    psb[0:NP, 5 + t % 3, 0:T * (NP + 1)].rearrange("p (s c) -> p s c", c=NP + 1)[:, :, 0:NP],
                                    1.0, BIG, ALU.subtract, ALU.mult).then_inc(sem("bneg"), 1)

            dve.wait_ge(sem("mask_mm"), 1)
            mask((0, 1, 2))

            def rows_added(mm_sem):
                def add(t):
                    dve.wait_ge(sem(mm_sem), t + 1)
                    link(V.tensor_tensor(x[0:NP, t, :], ps[0:NP, t, 0:D], x[0:NP, t, :], ALU.add))
                return add

            def add_bias(b):
                link(V.tensor_tensor(x[0:NP, :, :], x[0:NP, :, :], b[0:NP, :].unsqueeze(1).broadcast_to([NP, T, D]),
                                     ALU.add))

            dve.wait_ge(sem("ld_g0"), 64)
            add_bias(b02)

            norm(x, rows_added("g0d_mm"))
            turn()
            dve.wait_ge(sem("mask_mm"), 2)
            mask((3, 4))
            dve.wait_ge(sem("gat_h_mm"), 1)
            dve.wait_ge(sem("ld_gat"), 96)
            for h in range(HEADS):
                V.tensor_copy(haug[0:NP, :, h, 5 * h:5 * h + 4],
                              ps[0:NP, 3, 0:80].rearrange("p (t g) -> p t g", t=T)[:, :, 4 * h:4 * h + 4])
            link(V.tensor_copy(hg[0:NP, :, :].rearrange("p t c -> p (t c)"), ps[0:NP, 3, 0:80]))
            for i in range(2):
                link(V.tensor_tensor(prod[0:NP, :, :], hg[0:NP, :, :],
                                     gatc[0:NP, i, :].unsqueeze(1).broadcast_to([NP, T, 16]), ALU.mult))
                link(V.tensor_reduce(asd[0:NP, i, :, :].rearrange("p t h -> p (t h)"),
                                     prod[0:NP, :, :].rearrange("p t (h c) -> p (t h) c", c=4), AX.X, ALU.add))
            V.tensor_scalar(asd[0:NP, 6, :, :], asd[0:NP, 0, :, :], 0.2, None, ALU.mult).then_inc(sem("asd"), 1)
            dve.wait_ge(sem("bneg"), T)
            n = 0
            for h in range(HEADS):
                dve.wait_ge(sem("arow_ev"), h + 1)
                for t in range(T):
                    link(V.tensor_tensor_reduce(out=junk[0:NP, n % 2, :], in0=Bneg[0:NP, t, :], in1=arow[0:NP, h, :],
                                                scale=1.0, scalar=-3e38, op0=ALU.add, op1=ALU.max,
                                                accum_out=asd[0:NP, 2, t, h:h + 1]))
                    n += 1
            link(V.tensor_tensor(asd[0:NP, 2, :, :], asd[0:NP, 2, :, :], asd[0:NP, 1, :, :], ALU.add))
            link(V.scalar_tensor_tensor(out=asd[0:NP, 3, :, :], in0=asd[0:NP, 2, :, :], scalar=0.2,
                                        in1=asd[0:NP, 2, :, :], op0=ALU.mult, op1=ALU.max))
            V.tensor_tensor(asd[0:NP, 4, :, :], asd[0:NP, 1, :, :], asd[0:NP, 3, :, :], ALU.subtract)
            V.scalar_tensor_tensor(out=asd[0:NP, 5, :, :], in0=asd[0:NP, 1, :, :], scalar=0.2,
                                   in1=asd[0:NP, 3, :, :], op0=ALU.mult, op1=ALU.subtract).then_inc(sem("pq"), 1)
            for i in range(HEADS * T):
                h, t = i // T, i % T
                dve.wait_ge(sem("ev"), 2 * i + 2)
                link(V.tensor_tensor(ev[0:NP, i % 2, :], up[0:NP, i % 2, :], uq[0:NP, i % 2, :], ALU.max))
                if t == 0 and h >= 2:
                    dve.wait_ge(sem("gat_mm"), h - 1)
                V.scalar_tensor_tensor(out=EE[0:NP, h % 2, t, :], in0=ev[0:NP, i % 2, :], scalar=1.0,
                                       in1=BT[0:NP, t, :], op0=ALU.min, op1=ALU.mult).then_inc(sem("ee"), 1)
            dve.wait_ge(sem("gat_mm"), HEADS + 1)
            g5 = ps[0:NP, 5, 0:100].rearrange("p (g c) -> p g c", c=5)
            link(V.tensor_scalar(scr[0:NP, 0, :, 0:4].rearrange("p t h -> p t h"),
                                 ps[0:NP, 5, 0:100].rearrange("p (t h c) -> p t h c", t=T, c=5)[:, :, :, 4],
                                 1e-16, None, ALU.add))
            link(V.reciprocal(asd[0:NP, 3, :, :], scr[0:NP, 0, :, 0:4]))
            agg = scr[0:NP, 1, :, :]
            link(V.tensor_tensor(agg.rearrange("p t c -> p (t c)").rearrange("p (g c) -> p g c", c=4),
                                 g5[:, :, 0:4],
                                 asd[0:NP, 3, :, :].rearrange("p t h -> p (t h)").unsqueeze(2).broadcast_to([NP, 20, 4]),
                                 ALU.mult))

            def wide(i):
                return gatc[0:NP, i, :].unsqueeze(1).broadcast_to([NP, T, 16])

            def tall(c):
                return sca[0:NP, c, :].unsqueeze(2).broadcast_to([NP, T, 16])

            link(V.tensor_tensor(agg, agg, wide(2), ALU.add))
            link(V.tensor_reduce(sca[0:NP, 0, :], agg, AX.X, ALU.add))
            link(V.tensor_scalar(sca[0:NP, 0, :], sca[0:NP, 0, :], 1.0 / 16, None, ALU.mult))
            link(V.tensor_tensor(agg, agg, tall(0), ALU.subtract))
            link(V.tensor_tensor(scr[0:NP, 2, :, :], agg, agg, ALU.mult))
            V.tensor_reduce(sca[0:NP, 1, :], scr[0:NP, 2, :, :], AX.X, ALU.add).then_inc(sem("var16"), 1)
            dve.wait_ge(sem("std16"), 1)
            link(V.reciprocal(sca[0:NP, 3, :], sca[0:NP, 2, :]))
            link(V.tensor_tensor(agg, agg, tall(3), ALU.mult))
            link(V.tensor_tensor(agg, agg, wide(3), ALU.mult))
            link(V.tensor_tensor(agg, agg, wide(4), ALU.add))
            link(V.tensor_reduce(scr[0:NP, 0, :, 0:4], agg.rearrange("p t (h c) -> p t c h", c=4), AX.X, ALU.add))
            link(V.tensor_scalar(scr[0:NP, 2, :, 0:4], scr[0:NP, 0, :, 0:4], 0.25, None, ALU.mult))
            top2_gate(scr[0:NP, 2, :, 0:4], X0, 1)
            for t in range(T):
                dve.wait_ge(sem("f0_out_mm"), t + 1)
                i = V.tensor_tensor(x[0:NP, t, :], ps[0:NP, 4 + t % 4, 0:D], x[0:NP, t, :], ALU.add)
                i.then_inc(sem("f0_out_ev"), 1)

            def f0_sum(e, t):
                n = T * (e + 1) + t
                dve.wait_ge(sem("f0_out_mm"), n + 1)
                dve.wait_ge(sem("f0_out_ev"), n - T + 1)
                i = V.scalar_tensor_tensor(out=x[0:NP, t, :], in0=ps[0:NP, 4 + n % 4, 0:D],
                                           scalar=gate[0:NP, t, e:e + 1], in1=x[0:NP, t, :],
                                           op0=ALU.mult, op1=ALU.add)
                i.then_inc(sem("f0_out_ev"), 1)
                if e == X0 - 1:
                    dve.wait_ge(sem("f0_out_ev"), n + 1)

            for e in range(X0 - 1):
                for t in range(T):
                    f0_sum(e, t)

            norm(x, lambda t: f0_sum(X0 - 1, t))
            dve.wait_ge(sem("ld_g1"), 80)
            add_bias(bc3)
            norm(x, rows_added("g1f_mm"))
            link(V.tensor_tensor(x[0:NP, :, :], x[0:NP, :, :], xn[0:NP, :, :], ALU.add))
            for t in range(T):
                i = V.tensor_scalar(ltmask[0:NP, t, :], iota[0:NP, 0:N], node[0:NP, t:t + 1], None, ALU.is_lt)
            turn()
            dve.wait_ge(sem("wrow_ev"), 2)
            for t in range(T):
                i = V.tensor_tensor_reduce(out=dtmp[0:NP, t, :], in0=wrow[0:NP, tile(t)], in1=ident[0:NP, 0:NP],
                                           scale=1.0, scalar=0.0, op0=ALU.mult, op1=ALU.add,
                                           accum_out=wcol[0:NP, t:t + 1])
            link(i)
            for t in range(T):
                i2 = V.tensor_scalar(wj[0:NP, 0, :], wrow[0:NP, :], wcol[0:NP, t:t + 1], 0.0, ALU.is_gt, ALU.add,
                                    accum_out=rk[0:NP, 0, t:t + 1])
                i = V.scalar_tensor_tensor(out=wj[0:NP, 1, :], in0=wrow[0:NP, :], scalar=wcol[0:NP, t:t + 1],
                                           in1=ltmask[0:NP, t, :], op0=ALU.is_equal, op1=ALU.mult,
                                           accum_out=rk[0:NP, 1, t:t + 1])
                link_all([i2, i])
            link(V.tensor_tensor(rk[0:NP, 2, :], rk[0:NP, 0, :], rk[0:NP, 1, :], ALU.add))
            link(V.scalar_tensor_tensor(out=rk[0:NP, 3, :], in0=rk[0:NP, 2, :], scalar=float(KEEP1),
                                        in1=wcol[0:NP, :], op0=ALU.is_lt, op1=ALU.mult))
            dve.wait_ge(sem("ld_f1"), 48)

            def added(t):
                dve.wait_ge(sem("f1_out_mm"), t + 1)
                link(V.tensor_tensor(h2[0:NP, t, :], ps[0:NP, t, 0:D], m2b[0:NP, :], ALU.add))
                link(V.scalar_tensor_tensor(out=x[0:NP, t, :], in0=h2[0:NP, t, :], scalar=rk[0:NP, 3, t:t + 1],
                                            in1=x[0:NP, t, :], op0=ALU.mult, op1=ALU.add))

            norm(x, added)
            turn()
            for t in range(T):
                dve.wait_ge(sem("g2a_mm"), t + 1)
                V.tensor_tensor(x[0:NP, t, :], ps[0:NP, 3 + t, 0:D], x[0:NP, t, :], ALU.add
                                ).then_inc(sem("g2a_v"), 1)
            for tiles in ((0, 1), (2, 3), (4,)):
                dve.wait_ge(sem("hn"), tiles[-1] + 1)
                at = {t: hn[0:NP, t, :] for t in tiles}
                for r in range(MAXK // 8):
                    link_all([V.max(top8[0:NP, t, r, :], at[t]) for t in tiles])
                    link_all([V.match_replace(wk[0:NP, r % 2, t, :], top8[0:NP, t, r, :], at[t], -3e38) for t in tiles])
                    at = {t: wk[0:NP, r % 2, t, :] for t in tiles}
                for t in tiles:
                    V.scalar_tensor_tensor(out=hn[0:NP, t, :], in0=at[t], scalar=-3e38, in1=hn[0:NP, t, :],
                                           op0=ALU.is_equal, op1=ALU.mult).then_inc(sem("hs"), 1)

            def added(t):
                dve.wait_ge(sem("g2b_mm"), t + 1)
                link(V.scalar_tensor_tensor(out=x[0:NP, t, :], in0=ps[0:NP, t, 0:D], scalar=rdeg[0:NP, t:t + 1],
                                            in1=x[0:NP, t, :], op0=ALU.mult, op1=ALU.add))
            norm(x, added)
            turn()
            dve.wait_ge(sem("lg2_mm"), 1)
            dve.wait_ge(sem("ld_s2"), 32)
            lg, ex, oh = scr[0:NP, 0, :, 0:X2], scr[0:NP, 1, :, 0:X2], scr[0:NP, 2, :, 0:X2]

            def each(c):
                return sca[0:NP, c, :].unsqueeze(2).broadcast_to([NP, T, X2])

            link(V.tensor_tensor(lg, ps[0:NP, 3, 0:T * X2].rearrange("p (t e) -> p t e", t=T),
                                 g2b[0:NP, :].unsqueeze(1).broadcast_to([NP, T, X2]), ALU.add))
            link(V.tensor_reduce(sca[0:NP, 0, :], lg, AX.X, ALU.max))
            V.tensor_tensor(lg, lg, each(0), ALU.subtract).then_inc(sem("to_exp"), 1)
            dve.wait_ge(sem("exped"), 2)
            link(V.tensor_reduce(sca[0:NP, 1, :], ex, AX.X, ALU.add))
            link(V.reciprocal(sca[0:NP, 2, :], sca[0:NP, 1, :]))
            link(V.tensor_tensor(ex, ex, each(2), ALU.mult))
            first_max(ex, X2, oh, sca[0:NP, 3, :], scr[0:NP, 5, :, 0:X2])
            V.tensor_copy(ohb[0:NP, :, :], oh).then_inc(sem("ohb"), 1)
            link(V.tensor_tensor(scr[0:NP, 3, :, 0:X2], oh,
                                 iota[0:NP, 0:SL:CAP].unsqueeze(1).broadcast_to([NP, T, X2]), ALU.mult))
            link(V.tensor_reduce(sca[0:NP, 4, :], scr[0:NP, 3, :, 0:X2], AX.X, ALU.add))
            dve.wait_ge(sem("pos_mm"), 1)
            link(V.tensor_tensor(scr[0:NP, 4, :, 0:X2], ps[0:NP, 4, 0:T * X2].rearrange("p (t e) -> p t e", t=T),
                                 oh, ALU.mult))
            link(V.tensor_reduce(sca[0:NP, 5, :], scr[0:NP, 4, :, 0:X2], AX.X, ALU.add))
            link(V.tensor_scalar(sca[0:NP, 6, :], sca[0:NP, 5, :], float(CAP), None, ALU.is_le))
            V.tensor_tensor(prk[0:NP, :], sca[0:NP, 3, :], sca[0:NP, 6, :], ALU.mult)
            link(V.tensor_tensor(sca[0:NP, 7, :], sca[0:NP, 4, :], sca[0:NP, 5, :], ALU.add))
            link(V.tensor_tensor(sca[0:NP, 8, :], sca[0:NP, 7, :], sca[0:NP, 6, :], ALU.mult))
            V.tensor_scalar(slot[0:NP, :], sca[0:NP, 8, :], 1.0, None, ALU.subtract).then_inc(sem("slot"), 1)
            dve.wait_ge(sem("slot"), 1)
            for t in range(T):
                V.tensor_scalar(SC[0:NP, t, :], iota[0:NP, 0:SL], slot[0:NP, t:t + 1], None, ALU.is_equal
                                ).then_inc(sem("sc"), 1)
            dve.wait_ge(sem("srow_ev"), 2)
            for e in range(X2):
                V.tensor_scalar(ST[0:CAP, e, :], srow[0:CAP, :], float(e * CAP), node[0:CAP, 0:1],
                                ALU.subtract, ALU.is_equal).then_inc(sem("st"), 1)
            dve.wait_ge(sem("ld_late"), 16 * (3 + X2))
            dve.wait_ge(sem("ld_s3"), 112)
            for i in range(2):
                link(V.tensor_tensor(pr3, W3[:, :, 0:D], att3[:, i, :].unsqueeze(1).broadcast_to([128, KD, D]), ALU.mult))
                for k in range(KD):
                    j = V.tensor_reduce(W3[:, k, D + HEADS * i:D + HEADS * (i + 1)],
                                        pr3[:, k, :].rearrange("p (h c) -> p h c", h=HEADS), AX.X, ALU.add)
                j.then_inc(sem("w3"), 1)
                dve.wait_ge(sem("w3"), i + 1)
            dve.wait_ge(sem("disp_mm"), 4)
            dve.wait_ge(sem("ld_rc"), 32)
            link(V.tensor_copy(rcf[0:NP, :, :], rci[0:NP, :, :]))
            for i, g in enumerate((Gc, Gr)):
                for t in range(T):
                    V.tensor_scalar(g[0:NP, t, :], rcf[0:NP, i, :], node[0:NP, t:t + 1], None, ALU.is_equal
                                    ).then_inc(sem("gcr"), 1)

            with dve.Fori(0, X2 // 2) as i:
                for b in range(2):
                    dve.wait_ge(sem("f2_out_mm"), 2 * i + b + 1)
                    V.tensor_tensor(ybuf[0:CAP, bass.ds(2 * i + b, 1), :].rearrange("p a n -> p (a n)"),
                                    ps[0:CAP, 4 + b, 0:D],
                                    f2b2[0:CAP, bass.ds(2 * i + b, 1), :].rearrange("p a n -> p (a n)"), ALU.add
                                    ).then_inc(sem("f2_out_ev"), 1)
            V.memset(cst4[:, 0:1], 1e4)
            V.memset(cst4[:, 1:2], -1e4)
            V.memset(h2[0:NP, :, :], 0.0)
            mi = RW[:, 4 * N:4 * N + T * D].bitcast(I32).rearrange("p (t n) -> p t n", t=T)

            def added(t):
                dve.wait_ge(sem("comb_mm"), t + 1)
                y, m = xn[0:NP, t, :], mi[0:NP, t, :]
                link(V.tensor_scalar(y, ps[0:NP, t, 0:D], prk[0:NP, t:t + 1], None, ALU.mult))
                link(V.tensor_tensor(m, y, y, ALU.is_equal))
                link(V.copy_predicated(h2[0:NP, t, :], m, y))
                for c, (op, lim) in enumerate(((ALU.is_gt, 3.4028234e38), (ALU.is_lt, -3.4028234e38))):
                    link(V.tensor_scalar(m, y, lim, None, op))
                    link(V.copy_predicated(h2[0:NP, t, :], m, cst4[0:NP, c:c + 1].broadcast_to([NP, D])))
                link(V.tensor_tensor(x[0:NP, t, :], x[0:NP, t, :], h2[0:NP, t, :], ALU.add))

            norm(x, added)
            turn()
            for t in range(T):
                dve.wait_ge(sem("g3b_mm"), t + 1)
                i = V.tensor_copy(z3[0:NP, 0, t, :], ps[0:NP, t, D:D + HEADS])
            link(i)
            z = z3[0:NP, 0, :, :]

            def each4(c):
                return sca[0:NP, c, :].unsqueeze(2).broadcast_to([NP, T, HEADS])

            link(V.scalar_tensor_tensor(out=z3[0:NP, 2, :, :], in0=z, scalar=0.01, in1=z, op0=ALU.mult, op1=ALU.max))
            link(V.tensor_reduce(sca[0:NP, 0, :], z3[0:NP, 2, :, :], AX.X, ALU.max))
            V.tensor_tensor(z, z3[0:NP, 2, :, :], each4(0), ALU.subtract).then_inc(sem("to_exp"), 1)
            dve.wait_ge(sem("exped"), 3)
            link(V.tensor_reduce(sca[0:NP, 1, :], z3[0:NP, 1, :, :], AX.X, ALU.add))
            link(V.reciprocal(sca[0:NP, 2, :], sca[0:NP, 1, :]))
            link(V.tensor_tensor(z3[0:NP, 2, :, :], z3[0:NP, 1, :, :], each4(2), ALU.mult))
            for h in range(HEADS):
                for t in range(T):
                    xs = ps[0:NP, t, h * HD3:(h + 1) * HD3]
                    al = z3[0:NP, 2, t, h:h + 1]
                    if h == 0:
                        i = V.tensor_scalar(tmp3[0:NP, 0, t, :], xs, al, None, ALU.mult)
                    else:
                        i = V.scalar_tensor_tensor(out=tmp3[0:NP, h % 2, t, :], in0=xs, scalar=al,
                                                   in1=tmp3[0:NP, (h + 1) % 2, t, :], op0=ALU.mult, op1=ALU.add)
                link(i)

            def added(t):
                xv = x[0:NP, t, :].rearrange("p (h c) -> p h c", h=HEADS)
                link(V.tensor_tensor(xv, xv, tmp3[0:NP, 1, t, :].unsqueeze(1).broadcast_to([NP, HEADS, HD3]), ALU.add))

            norm(x, added)
            turn()
            dve.wait_ge(sem("lg3_mm"), 1)
            lg = scr[0:NP, 2, :, :]
            link(V.tensor_tensor(lg, ps[0:NP, 3, 0:T * X3].rearrange("p (t e) -> p t e", t=T),
                                 g3b[0:NP, :].unsqueeze(1).broadcast_to([NP, T, X3]), ALU.add))
            top2_gate(lg, X3, 4, oh3[0:NP])
            dve.wait_ge(sem("rank_mm"), 1)
            V.tensor_scalar(rank3[0:NP, :, :], ps[0:NP, 4, 0:T * X3].rearrange("p (t e) -> p t e", t=T), 1.0, None,
                            ALU.subtract)
            more, before, upto, numb, shift = (e3[:, i, :] for i in range(5))
            link(V.tensor_copy(numb, ps[:, 4, 128:128 + X3]))
            V.tensor_tensor(more3[:, :, :], numb.unsqueeze(2).broadcast_to([128, X3, 4]),
                            iota[:, 128:640:128].unsqueeze(1).broadcast_to([128, X3, 4]), ALU.is_gt)
            link(V.tensor_tensor(less3[:, :, :], iota[:, 0:X3].unsqueeze(1).broadcast_to([128, X3, X3]),
                                 iota[:, 0:X3].unsqueeze(2).broadcast_to([128, X3, X3]), ALU.is_lt))
            link(V.tensor_reduce(more, more3[:, :, :], AX.X, ALU.add))
            link(V.tensor_tensor(less3[:, :, :], less3[:, :, :], more.unsqueeze(1).broadcast_to([128, X3, X3]),
                                 ALU.mult))
            link(V.tensor_reduce(before, less3[:, :, :], AX.X, ALU.add))
            link(V.tensor_tensor(shift, before, iota[:, 0:X3], ALU.subtract))
            link(V.tensor_scalar(shift, shift, float(X3 - 1), 128.0, ALU.add, ALU.mult))
            link(V.scalar_tensor_tensor(out=place3[0:NP, :, :], in0=rank3[0:NP, :, :], scalar=128.0,
                                        in1=shift[0:NP, :].unsqueeze(1).broadcast_to([NP, T, X3]),
                                        op0=ALU.is_ge, op1=ALU.mult))
            link(V.tensor_tensor(place3[0:NP, :, :], place3[0:NP, :, :], rank3[0:NP, :, :], ALU.add))
            link(V.scalar_tensor_tensor(out=place3[0:NP, :, :], in0=iota[0:NP, 0:X3].unsqueeze(1).broadcast_to([NP, T, X3]),
                                        scalar=128.0, in1=place3[0:NP, :, :], op0=ALU.mult, op1=ALU.add))
            for c in range(2):
                i = V.tensor_tensor(ohp3[0:NP, c, :, :], oh3[0:NP, c, :, :], place3[0:NP, :, :], ALU.mult)
            link(i)
            for c in range(2):
                i = V.tensor_reduce(scr[0:NP, 0, c:c + 1, 0:T], ohp3[0:NP, c:c + 1, :, :], AX.X, ALU.add)
            link(i)
            V.tensor_copy(row3[0:NP, :, :], scr[0:NP, 0, 0:2, 0:T]).then_inc(sem("row3"), 1)
            link(V.tensor_tensor(upto, before, more, ALU.add))
            link(V.tensor_tensor(below3[:, :, :], upto.unsqueeze(1).broadcast_to([128, OV3, X3]),
                                 iota[:, 0:OV3].unsqueeze(2).broadcast_to([128, OV3, X3]), ALU.is_le))
            link(V.tensor_reduce(idf3, below3[:, :, :], AX.X, ALU.add))
            link(V.tensor_scalar(idf3, idf3, float(X3 - 1), 128.0, ALU.min, ALU.mult))
            link(V.tensor_scalar(idf3, idf3, node[:, 0:1], None, ALU.add))
            V.tensor_copy(id3[:, :], idf3).then_inc(sem("id3"), 1)
            dve.wait_ge(sem("f3_bias_mm"), 1)
            for t in range(T):
                V.tensor_tensor(h2[0:NP, t, :], ps[0:NP, 5 + t // 2, (t % 2) * D:(t % 2 + 1) * D], xn[0:NP, t, :],
                                ALU.add).then_inc(sem("f3_out_ev"), 1)

            def f3_turn(j, s):
                dve.wait_ge(sem("xg_mm"), j + 1)
                if not (isinstance(j, int) and j < 2):
                    dve.wait_ge(sem("f3_hid_mm"), 2 * j - 2)
                V.tensor_copy(xgT[:, s, :, :], ps[:, s, 0:D].rearrange("p (k n) -> p k n", k=KD)
                              ).then_inc(sem("xgT_ev"), 1)

            def f3_step(j, b):
                if not isinstance(j, int) or j + 2 < J3:
                    f3_turn(j + 2, b % 2)
                dve.wait_ge(sem("f3_out_mm"), j + 1)
                if not (isinstance(j, int) and j < 4):
                    dve.wait_ge(sem(f"st_y{b}"), 4 * (j - b))
                V.tensor_copy(yo[:, b, :], ps[:, 4 + b % 2, 0:D]).then_inc(sem("f3_out_ev"), 1)

            V.tensor_tensor(x[0:NP, :, :], x[0:NP, :, :], bet[0:NP, :].unsqueeze(1).broadcast_to([NP, T, D]), ALU.add
                            ).then_inc(sem("x_beta"), 1)
            f3_turn(0, 0)
            f3_turn(1, 1)
            for j in range(4):
                f3_step(j, j)
            with dve.Fori(1, (J3 - 2) // 4) as i:
                for b in range(4):
                    f3_step(4 * i + b, b)
            for j in range((J3 - 2) // 4 * 4, J3):
                f3_step(j, j % 4)
            for t in range(T + 1):
                if t < T:
                    dve.wait_ge(sem(f"ld_yg{t}"), 32)
                    for c in range(2):
                        link(V.scalar_tensor_tensor(out=h2[0:NP, t, :], in0=yg[0:NP, t, c, :],
                                                    scalar=sca[0:NP, 10 + c, t:t + 1], in1=h2[0:NP, t, :],
                                                    op0=ALU.mult, op1=ALU.add))
                    link(V.bn_stats(st[0:NP, t, :], h2[0:NP, t, :]))
                    V.bn_aggr(mv[0:NP, t, :], st[0:NP, t, :]).then_inc(sem("y_var"), 1)
                if t >= 1:
                    u = t - 1
                    dve.wait_ge(sem("y_var"), t)
                    dve.wait_ge(sem("y_std"), t)
                    link(V.reciprocal(rs[0:NP, u:t], sd[0:NP, u:t]))
                    link(V.tensor_scalar(xn[0:NP, u, :], h2[0:NP, u, :], mv[0:NP, u, 0:1], rs[0:NP, u:t],
                                         ALU.subtract, ALU.mult))
                    link(V.tensor_tensor(xn[0:NP, u, :], xn[0:NP, u, :], gam[0:NP, :], ALU.mult))
                    dve.wait_ge(sem("x_beta"), 1)
                    V.tensor_tensor(x[0:NP, u, :], x[0:NP, u, :], xn[0:NP, u, :], ALU.add).then_inc(sem("x_final"), 1)


BANKS = [[(2, 2), (3, 3), (4, 4), (0, 0), (1, 1)], [(0, 5), (1, 6), (2, 7), (3, 0), (4, 1)]]
XN_OF_TURN = [1, 3, 4, 5, 6, 7]


_INS = ["x", "src", "dst", "L0_gnn_W1", "L0_gnn_W2", "L0_gnn_b2", "L0_ffn_W_gat", "L0_ffn_att_src", "L0_ffn_att_dst",
        "L0_ffn_b_gat", "L0_ffn_ln_gamma", "L0_ffn_ln_beta", "L0_ffn_b2", "L0_ffn_edge_index", "L1_gnn_W1",
        "L1_gnn_W2", "L1_gnn_W3", "L1_gnn_b3", "L1_ffn_br", "L1_ffn_w1", "L1_ffn_w2", "L1_ffn_b2",
        "L2_gnn_W_self", "L2_gnn_W_neigh", "L2_ffn_gate_w", "L2_ffn_gate_b", "L2_ffn_b2", "L3_gnn_weight",
        "L3_gnn_attn_l", "L3_gnn_attn_r", "L3_ffn_gate_w", "L3_ffn_gate_b", "L3_ffn_b2", "L3_ffn_gamma",
        "L3_ffn_beta"]
_EXPERTS = {"L0_experts": ("L0_ffn_W1", "L0_ffn_W2"), "L2_experts": ("L2_ffn_w1", "L2_ffn_w2"),
            "L3_experts": ("L3_ffn_w1", "L3_ffn_w2", "L3_ffn_b1")}


def laid_out(np, inputs):
    arrays = {name: np.ascontiguousarray(inputs[name]) for name in _INS}

    def by_partition(w):
        if w.ndim == 2:
            w = w[:, :, None]
        e, k, n = w.shape
        return w.reshape(e, k // 128, 128, n).transpose(0, 2, 1, 3).reshape(e, 128, -1)

    for name, pair in _EXPERTS.items():
        arrays[name] = np.concatenate([by_partition(np.asarray(inputs[w])) for w in pair], axis=2)
    arrays["bias_columns"] = np.ascontiguousarray(
        np.concatenate([np.asarray(inputs[name]).reshape(-1, 128).T for name, _ in BIAS_COLUMNS], axis=1))
    return arrays


def kernel(**inputs):
    import numpy as _np
    import concourse.bacc as _bacc
    from concourse import mybir as _mybir
    from concourse.bass_utils import run_bass_kernel_spmd as _run

    nc = _bacc.Bacc("TRN2", target_bir_lowering=False, num_devices=1)
    arrays, args = {}, {}
    for name, v in laid_out(_np, inputs).items():
        arrays[f"in_{name}"] = v
        args[name] = nc.dram_tensor(f"in_{name}", v.shape, _mybir.dt.from_np(v.dtype), kind="ExternalInput").ap()
    out = nc.dram_tensor("out_x", (N, D), F32, kind="ExternalOutput").ap()
    graph_mlp_stack(nc, args, out)
    r = _run(nc, [arrays], core_ids=[0])
    return r.results[0]["out_x"]
```
